# Optimizing a Trainium2 kernel written in Bass

```python
import numpy as np
import jax
import jax.numpy as jnp

def _softmax(x, axis=-1):
    return jax.nn.softmax(x, axis=axis)

def _gelu(x):
    return jax.nn.gelu(x, approximate=True)

def _silu(x):
    return jax.nn.silu(x)

def _sigmoid(x):
    return jax.nn.sigmoid(x)

def _layernorm(x, axis=-1, eps=1e-05):
    m = jnp.mean(x, axis=axis, keepdims=True)
    v = jnp.var(x, axis=axis, keepdims=True)
    return (x - m) / jnp.sqrt(v + eps)

def _scatter_add(tgt, idx, src, axis=0):
    return tgt.at[idx].add(src)

def _segment_sum(src, seg, n):
    return jax.ops.segment_sum(src, seg, n)
kernel_name = 'mk_gnn_ffn_d4_gnn_r32_2840a9'

def setup_inputs(seed: int=0):
    np.random.seed(seed)
    _w = jnp.asarray

    def _rec_inputs():
        import jax
        import jax.numpy as jnp
        _gk = jax.random.key(seed)
        x = -8.776e-05 + 1 * jax.random.normal(jax.random.fold_in(_gk, 1), (625, 256), jnp.float32)
        src = jax.random.randint(jax.random.fold_in(_gk, 2), (10000,), 0, 625, jnp.int32)
        dst = jax.random.randint(jax.random.fold_in(_gk, 3), (10000,), 0, 625, jnp.int32)
        _o = jnp.argsort(dst, stable=True)
        src = src[_o]
        dst = dst[_o]
        edge_attr_64 = 0.000279952 + 1.00013 * jax.random.normal(jax.random.fold_in(_gk, 11), (10000, 64), jnp.float32)
        return (x, src, dst, edge_attr_64)
    x, src, dst, edge_attr_64 = _rec_inputs()

    def _L0_gnn_setup():
        import jax, jax.numpy as jnp
        import numpy as np
        NUM_NODES = 625
        NUM_EDGES = 10000
        NODE_DIM = 256
        EDGE_DIM = 64
        HIDDEN = 512

        def _glorot(key, shape):
            fan_in = shape[0]
            bound = 1.0 / np.sqrt(fan_in)
            return jax.random.uniform(key, shape, jnp.float32, -bound, bound)
        key = jax.random.key(seed)
        ks = jax.random.split(key, 12)
        node_features = jax.random.normal(ks[0], (NUM_NODES, NODE_DIM), jnp.float32)
        edge_index = jax.random.randint(ks[1], (2, NUM_EDGES), 0, NUM_NODES, jnp.int64 if jax.config.jax_enable_x64 else jnp.int32)
        edge_features = jax.random.normal(ks[2], (NUM_EDGES, EDGE_DIM), jnp.float32)
        edge_in = 2 * NODE_DIM + EDGE_DIM
        node_in = NODE_DIM + HIDDEN
        params = {'W1': _glorot(ks[3], (edge_in, HIDDEN)), 'b1': _glorot(ks[4], (HIDDEN,)), 'W2': _glorot(ks[5], (HIDDEN, HIDDEN)), 'b2': _glorot(ks[6], (HIDDEN,)), 'W3': _glorot(ks[7], (node_in, HIDDEN)), 'b3': _glorot(ks[8], (HIDDEN,)), 'W4': _glorot(ks[9], (HIDDEN, NODE_DIM)), 'b4': _glorot(ks[10], (NODE_DIM,))}
        return {'node_features': node_features, 'edge_index': edge_index, 'edge_features': edge_features, **params}
    _L0_gnn_all = _L0_gnn_setup()
    _L0_gnn_in = {k: v for k, v in _L0_gnn_all.items() if k in ('W1', 'b1', 'W2', 'b2', 'W3', 'b3', 'W4', 'b4')}
    del _L0_gnn_all

    def _L0_ffn_setup():
        import jax, jax.numpy as jnp
        import numpy as np
        D_MODEL = 256
        EXPERT_DIM = 512
        NUM_EXPERTS = 8
        TOP_K = 2
        SEQ_LEN = 64
        BATCH = 2
        key = jax.random.key(seed)
        ks = jax.random.split(key, 8)
        s = 0.02
        x = jax.random.normal(ks[0], (SEQ_LEN, BATCH, D_MODEL), dtype=jnp.float32)
        Wg = jax.random.normal(ks[1], (D_MODEL, NUM_EXPERTS), dtype=jnp.float32) * s
        bg = jax.random.normal(ks[2], (NUM_EXPERTS,), dtype=jnp.float32) * s
        bias = jnp.zeros((NUM_EXPERTS,), dtype=jnp.float32)
        W1 = jax.random.normal(ks[3], (NUM_EXPERTS, D_MODEL, EXPERT_DIM), dtype=jnp.float32) * s
        b1 = jax.random.normal(ks[4], (NUM_EXPERTS, EXPERT_DIM), dtype=jnp.float32) * s
        W2 = jax.random.normal(ks[5], (NUM_EXPERTS, EXPERT_DIM, D_MODEL), dtype=jnp.float32) * s
        b2 = jax.random.normal(ks[6], (NUM_EXPERTS, D_MODEL), dtype=jnp.float32) * s
        return {'x': x, 'Wg': Wg, 'bg': bg, 'bias': bias, 'W1': W1, 'b1': b1, 'W2': W2, 'b2': b2}
    _L0_ffn_all = _L0_ffn_setup()
    _L0_ffn_in = {k: v for k, v in _L0_ffn_all.items() if k in ('Wg', 'bg', 'bias', 'W1', 'b1', 'W2', 'b2')}
    del _L0_ffn_all

    def _L1_gnn_setup():
        import jax, jax.numpy as jnp
        import numpy as np
        N_NODES = 50000

        def gcn_conv(x, W, b, src, dst, n_nodes):
            h = x @ W
            ones = jnp.ones(src.shape[0], dtype=h.dtype)
            deg = jax.ops.segment_sum(ones, dst, num_segments=n_nodes) + 1.0
            dinv = jax.lax.rsqrt(deg)
            norm = dinv[src] * dinv[dst]
            msg = h[src] * norm[:, None]
            agg = jax.ops.segment_sum(msg, dst, num_segments=n_nodes)
            agg = agg + h * (dinv * dinv)[:, None]
            return agg + b
        key = jax.random.key(seed)
        k1, k2, k3, k4 = jax.random.split(key, 4)
        embedding = jax.random.normal(k1, (N_NODES, 256), dtype=jnp.float32)
        edge_index = jax.random.randint(k2, (2, 25000), 0, N_NODES, dtype=jnp.int64)
        W1 = jax.random.normal(k3, (256, 64), dtype=jnp.float32) / np.sqrt(256.0)
        b1 = jnp.zeros((64,), dtype=jnp.float32)
        W2 = jax.random.normal(k4, (64, 256), dtype=jnp.float32) / np.sqrt(64.0)
        b2 = jnp.zeros((256,), dtype=jnp.float32)
        return {'embedding': embedding, 'edge_index': edge_index, 'W1': W1, 'b1': b1, 'W2': W2, 'b2': b2}
    _L1_gnn_all = _L1_gnn_setup()
    _L1_gnn_in = {k: v for k, v in _L1_gnn_all.items() if k in ('W1', 'b1', 'W2', 'b2')}
    del _L1_gnn_all

    def _L1_ffn_setup():
        import jax, jax.numpy as jnp
        import numpy as np
        B, S, D, E, H, K = (4, 128, 256, 8, 512, 2)
        key = jax.random.key(seed)
        ks = jax.random.split(key, 6)
        x = jax.random.normal(ks[0], (B, S, D), jnp.float32)
        Wg = jax.random.normal(ks[1], (D, E), jnp.float32) * 0.02
        bg = jnp.zeros((E,), jnp.float32)
        W1 = jax.random.normal(ks[2], (E, D, H), jnp.float32) * 0.02
        b1 = jnp.zeros((E, H), jnp.float32)
        W2 = jax.random.normal(ks[3], (E, H, D), jnp.float32) * 0.02
        b2 = jnp.zeros((E, D), jnp.float32)
        return {'x': x, 'Wg': Wg, 'bg': bg, 'W1': W1, 'b1': b1, 'W2': W2, 'b2': b2}
    _L1_ffn_all = _L1_ffn_setup()
    _L1_ffn_in = {k: v for k, v in _L1_ffn_all.items() if k in ('Wg', 'bg', 'W1', 'b1', 'W2', 'b2')}
    del _L1_ffn_all

    def _L2_gnn_setup():
        import jax, jax.numpy as jnp
        import numpy as np
        N = 625
        IN = 256
        HID = 256
        H = 4
        C = HID // H
        E = 10000
        NEG_SLOPE = 0.2

        def _gatv2_layer(x, src, dst, Wl, Wr, att, bias):
            xl = (x @ Wl).reshape(N, H, C)
            xr = (x @ Wr).reshape(N, H, C)
            e = jax.nn.leaky_relu(xl[src] + xr[dst], NEG_SLOPE)
            score = jnp.einsum('ehc,hc->eh', e, att)
            m = jax.ops.segment_max(score, dst, num_segments=N)
            m = jnp.where(jnp.isfinite(m), m, 0.0)
            p = jnp.exp(score - jax.lax.stop_gradient(m)[dst])
            denom = jax.ops.segment_sum(p, dst, num_segments=N)
            alpha = p / (denom[dst] + 1e-16)
            out = jax.ops.segment_sum(alpha[:, :, None] * xl[src], dst, num_segments=N)
            return out.reshape(N, H * C) + bias
        key = jax.random.key(seed)
        ks = jax.random.split(key, 12)
        s = 1.0 / np.sqrt(IN)
        s2 = 1.0 / np.sqrt(HID)
        inp = {'x': jax.random.normal(ks[0], (N, IN), dtype=jnp.float32), 'edge_index': jax.random.randint(ks[1], (2, E), 0, N, dtype=jnp.int64), 'Wl0': jax.random.normal(ks[2], (IN, H * C), dtype=jnp.float32) * s, 'Wr0': jax.random.normal(ks[3], (IN, H * C), dtype=jnp.float32) * s, 'att0': jax.random.normal(ks[4], (H, C), dtype=jnp.float32) * (1.0 / np.sqrt(C)), 'b0': jnp.zeros((H * C,), dtype=jnp.float32), 'Wl1': jax.random.normal(ks[5], (HID, H * C), dtype=jnp.float32) * s2, 'Wr1': jax.random.normal(ks[6], (HID, H * C), dtype=jnp.float32) * s2, 'att1': jax.random.normal(ks[7], (H, C), dtype=jnp.float32) * (1.0 / np.sqrt(C)), 'b1': jnp.zeros((H * C,), dtype=jnp.float32)}
        return inp
    _L2_gnn_all = _L2_gnn_setup()
    _L2_gnn_in = {k: v for k, v in _L2_gnn_all.items() if k in ('Wl0', 'Wr0', 'att0', 'b0', 'Wl1', 'Wr1', 'att1', 'b1')}
    del _L2_gnn_all

    def _L2_ffn_setup():
        import jax, jax.numpy as jnp
        import numpy as np
        C = 256
        HID = 1024
        E = 8
        TEMP = 1.0
        key = jax.random.key(seed)
        ks = jax.random.split(key, 7)
        x = jax.random.normal(ks[0], (8, 512, C), dtype=jnp.float32)
        W1 = jax.random.normal(ks[1], (C, HID), dtype=jnp.float32) * 0.02
        b1 = jnp.zeros((HID,), dtype=jnp.float32)
        Wg = jax.random.normal(ks[2], (HID, E), dtype=jnp.float32) * 0.02
        bg = jnp.zeros((E,), dtype=jnp.float32)
        Wd = jax.random.normal(ks[3], (E, HID, C), dtype=jnp.float32) * 0.02
        bd = jnp.zeros((E, C), dtype=jnp.float32)
        return {'x': x, 'W1': W1, 'b1': b1, 'Wg': Wg, 'bg': bg, 'Wd': Wd, 'bd': bd}
    _L2_ffn_all = _L2_ffn_setup()
    _L2_ffn_in = {k: v for k, v in _L2_ffn_all.items() if k in ('W1', 'b1', 'Wg', 'bg', 'Wd', 'bd')}
    del _L2_ffn_all

    def _L3_gnn_setup():
        import jax, jax.numpy as jnp
        import numpy as np
        N = 50000
        E = 25000
        D = 256

        def gcn_conv(x, W, src, dst, n):
            h = x @ W
            ones = jnp.ones(src.shape[0], dtype=h.dtype)
            deg = jax.ops.segment_sum(ones, dst, num_segments=n)
            dinv = jnp.where(deg > 0, jax.lax.rsqrt(deg), 0.0)
            norm = dinv[src] * dinv[dst]
            msgs = h[src] * norm[:, None]
            return jax.ops.segment_sum(msgs, dst, num_segments=n)
        key = jax.random.key(seed)
        k1, k2, k3, k4 = jax.random.split(key, 4)
        x = jax.random.normal(k1, (N, D), dtype=jnp.float32)
        edge_index = jax.random.randint(k2, (2, E), 0, N, dtype=jnp.int64)
        scale = 1.0 / np.sqrt(D)
        W1 = jax.random.normal(k3, (D, D), dtype=jnp.float32) * scale
        W2 = jax.random.normal(k4, (D, D), dtype=jnp.float32) * scale
        return {'x': x, 'edge_index': edge_index, 'W1': W1, 'W2': W2}
    _L3_gnn_all = _L3_gnn_setup()
    _L3_gnn_in = {k: v for k, v in _L3_gnn_all.items() if k in ('W1', 'W2')}
    del _L3_gnn_all

    def _L3_ffn_setup():
        import jax, jax.numpy as jnp
        import numpy as np
        E, D, H, TOP_K = (6, 256, 256, 2)
        ROUTER_H = D // 2
        key = jax.random.key(seed)
        ks = jax.random.split(key, 12)
        s = 1.0 / np.sqrt(D)
        sh = 1.0 / np.sqrt(H)
        sr = 1.0 / np.sqrt(ROUTER_H)
        return {'features': jax.random.normal(ks[0], (8, 128, D), dtype=jnp.float32), 'router_w1': jax.random.uniform(ks[1], (D, ROUTER_H), jnp.float32, -s, s), 'router_b1': jnp.zeros((ROUTER_H,), jnp.float32), 'router_w2': jax.random.uniform(ks[2], (ROUTER_H, E), jnp.float32, -sr, sr), 'router_b2': jnp.zeros((E,), jnp.float32), 'expert_w1': jax.random.uniform(ks[3], (E, D, H), jnp.float32, -s, s), 'expert_b1': jnp.zeros((E, H), jnp.float32), 'expert_w2': jax.random.uniform(ks[4], (E, H, H), jnp.float32, -sh, sh), 'expert_b2': jnp.zeros((E, H), jnp.float32), 'expert_w3': jax.random.uniform(ks[5], (E, H, D), jnp.float32, -sh, sh), 'expert_b3': jnp.zeros((E, D), jnp.float32)}
    _L3_ffn_all = _L3_ffn_setup()
    _L3_ffn_in = {k: v for k, v in _L3_ffn_all.items() if k in ('router_w1', 'router_b1', 'router_w2', 'router_b2', 'expert_w1', 'expert_b1', 'expert_w2', 'expert_b2', 'expert_w3', 'expert_b3')}
    del _L3_ffn_all
    return {'x': x, 'src': src, 'dst': dst, 'edge_attr_64': edge_attr_64, 'L0_gnn_W1': _L0_gnn_in['W1'], 'L0_gnn_b1': _L0_gnn_in['b1'], 'L0_gnn_W2': _L0_gnn_in['W2'], 'L0_gnn_b2': _L0_gnn_in['b2'], 'L0_gnn_W3': _L0_gnn_in['W3'], 'L0_gnn_b3': _L0_gnn_in['b3'], 'L0_gnn_W4': _L0_gnn_in['W4'], 'L0_gnn_b4': _L0_gnn_in['b4'], 'L0_ffn_Wg': _L0_ffn_in['Wg'], 'L0_ffn_bg': _L0_ffn_in['bg'], 'L0_ffn_bias': _L0_ffn_in['bias'], 'L0_ffn_W1': _L0_ffn_in['W1'], 'L0_ffn_b1': _L0_ffn_in['b1'], 'L0_ffn_W2': _L0_ffn_in['W2'], 'L0_ffn_b2': _L0_ffn_in['b2'], 'L1_gnn_W1': _L1_gnn_in['W1'], 'L1_gnn_b1': _L1_gnn_in['b1'], 'L1_gnn_W2': _L1_gnn_in['W2'], 'L1_gnn_b2': _L1_gnn_in['b2'], 'L1_ffn_Wg': _L1_ffn_in['Wg'], 'L1_ffn_bg': _L1_ffn_in['bg'], 'L1_ffn_W1': _L1_ffn_in['W1'], 'L1_ffn_b1': _L1_ffn_in['b1'], 'L1_ffn_W2': _L1_ffn_in['W2'], 'L1_ffn_b2': _L1_ffn_in['b2'], 'L2_gnn_Wl0': _L2_gnn_in['Wl0'], 'L2_gnn_Wr0': _L2_gnn_in['Wr0'], 'L2_gnn_att0': _L2_gnn_in['att0'], 'L2_gnn_b0': _L2_gnn_in['b0'], 'L2_gnn_Wl1': _L2_gnn_in['Wl1'], 'L2_gnn_Wr1': _L2_gnn_in['Wr1'], 'L2_gnn_att1': _L2_gnn_in['att1'], 'L2_gnn_b1': _L2_gnn_in['b1'], 'L2_ffn_W1': _L2_ffn_in['W1'], 'L2_ffn_b1': _L2_ffn_in['b1'], 'L2_ffn_Wg': _L2_ffn_in['Wg'], 'L2_ffn_bg': _L2_ffn_in['bg'], 'L2_ffn_Wd': _L2_ffn_in['Wd'], 'L2_ffn_bd': _L2_ffn_in['bd'], 'L3_gnn_W1': _L3_gnn_in['W1'], 'L3_gnn_W2': _L3_gnn_in['W2'], 'L3_ffn_router_w1': _L3_ffn_in['router_w1'], 'L3_ffn_router_b1': _L3_ffn_in['router_b1'], 'L3_ffn_router_w2': _L3_ffn_in['router_w2'], 'L3_ffn_router_b2': _L3_ffn_in['router_b2'], 'L3_ffn_expert_w1': _L3_ffn_in['expert_w1'], 'L3_ffn_expert_b1': _L3_ffn_in['expert_b1'], 'L3_ffn_expert_w2': _L3_ffn_in['expert_w2'], 'L3_ffn_expert_b2': _L3_ffn_in['expert_b2'], 'L3_ffn_expert_w3': _L3_ffn_in['expert_w3'], 'L3_ffn_expert_b3': _L3_ffn_in['expert_b3']}

def reference(x, src, dst, edge_attr_64, L0_gnn_W1, L0_gnn_b1, L0_gnn_W2, L0_gnn_b2, L0_gnn_W3, L0_gnn_b3, L0_gnn_W4, L0_gnn_b4, L0_ffn_Wg, L0_ffn_bg, L0_ffn_bias, L0_ffn_W1, L0_ffn_b1, L0_ffn_W2, L0_ffn_b2, L1_gnn_W1, L1_gnn_b1, L1_gnn_W2, L1_gnn_b2, L1_ffn_Wg, L1_ffn_bg, L1_ffn_W1, L1_ffn_b1, L1_ffn_W2, L1_ffn_b2, L2_gnn_Wl0, L2_gnn_Wr0, L2_gnn_att0, L2_gnn_b0, L2_gnn_Wl1, L2_gnn_Wr1, L2_gnn_att1, L2_gnn_b1, L2_ffn_W1, L2_ffn_b1, L2_ffn_Wg, L2_ffn_bg, L2_ffn_Wd, L2_ffn_bd, L3_gnn_W1, L3_gnn_W2, L3_ffn_router_w1, L3_ffn_router_b1, L3_ffn_router_w2, L3_ffn_router_b2, L3_ffn_expert_w1, L3_ffn_expert_b1, L3_ffn_expert_w2, L3_ffn_expert_b2, L3_ffn_expert_w3, L3_ffn_expert_b3):
    import jax
    import jax.numpy as jnp

    def _L0_gnn_ref(node_features, edge_index, edge_features, W1, b1, W2, b2, W3, b3, W4, b4):
        import jax, jax.numpy as jnp
        import numpy as np
        NUM_NODES = 625
        NUM_EDGES = 10000
        NODE_DIM = 256
        EDGE_DIM = 64
        HIDDEN = 512

        def _glorot(key, shape):
            fan_in = shape[0]
            bound = 1.0 / np.sqrt(fan_in)
            return jax.random.uniform(key, shape, jnp.float32, -bound, bound)
        src_idx = edge_index[0]
        tgt_idx = edge_index[1]
        edge_input = jnp.concatenate([node_features[src_idx], node_features[tgt_idx], edge_features], axis=-1)
        h = jax.nn.relu(edge_input @ W1 + b1)
        messages = h @ W2 + b2
        aggregated = jax.ops.segment_sum(messages, tgt_idx, num_segments=NUM_NODES)
        node_input = jnp.concatenate([node_features, aggregated], axis=-1)
        g = jax.nn.relu(node_input @ W3 + b3)
        node_update = g @ W4 + b4
        return node_features + node_update

    def _L0_ffn_ref(x, Wg, bg, bias, W1, b1, W2, b2):
        import jax, jax.numpy as jnp
        import numpy as np
        D_MODEL = 256
        EXPERT_DIM = 512
        NUM_EXPERTS = 8
        TOP_K = 2
        SEQ_LEN = 64
        BATCH = 2
        x_flat = x.reshape(-1, D_MODEL)
        gate_logits = x_flat @ Wg + bg + bias
        topk_vals, topk_idx = jax.lax.top_k(gate_logits, TOP_K)
        topk_w = jax.nn.softmax(topk_vals, axis=-1)
        combine = (jax.nn.one_hot(topk_idx, NUM_EXPERTS, dtype=x.dtype) * topk_w[..., None]).sum(axis=1)
        h = jax.nn.relu(jnp.einsum('td,edh->teh', x_flat, W1) + b1)
        y = jnp.einsum('teh,ehd->ted', h, W2) + b2
        out = jnp.einsum('ted,te->td', y, combine)
        return out.reshape(x.shape)

    def _L1_gnn_ref(embedding, edge_index, W1, b1, W2, b2):
        import jax, jax.numpy as jnp
        import numpy as np
        N_NODES = 50000

        def gcn_conv(x, W, b, src, dst, n_nodes):
            h = x @ W
            ones = jnp.ones(src.shape[0], dtype=h.dtype)
            deg = jax.ops.segment_sum(ones, dst, num_segments=n_nodes) + 1.0
            dinv = jax.lax.rsqrt(deg)
            norm = dinv[src] * dinv[dst]
            msg = h[src] * norm[:, None]
            agg = jax.ops.segment_sum(msg, dst, num_segments=n_nodes)
            agg = agg + h * (dinv * dinv)[:, None]
            return agg + b
        src, dst = (edge_index[0], edge_index[1])
        n = embedding.shape[0]
        h1 = jax.nn.relu(gcn_conv(embedding, W1, b1, src, dst, n))
        h2 = jax.nn.relu(gcn_conv(h1, W2, b2, src, dst, n))
        return h2

    def _L1_ffn_ref(x, Wg, bg, W1, b1, W2, b2):
        import jax, jax.numpy as jnp
        import numpy as np
        B, S, D, E, H, K = (4, 128, 256, 8, 512, 2)
        Bv, Sv, Dv = x.shape
        gate_scores = x @ Wg + bg
        _, idx = jax.lax.top_k(gate_scores, K)
        mask = jax.nn.one_hot(idx, E, dtype=x.dtype).sum(axis=-2)
        xf = x.reshape(-1, Dv)
        mf = mask.reshape(-1, E)
        h = jax.nn.gelu(jnp.einsum('td,edh->teh', xf, W1) + b1[None], approximate=False)
        y = jnp.einsum('teh,ehd->ted', h, W2) + b2[None]
        out = jnp.einsum('ted,te->td', y, mf)
        return out.reshape(Bv, Sv, Dv)

    def _L2_gnn_ref(x, edge_index, Wl0, Wr0, att0, b0, Wl1, Wr1, att1, b1):
        import jax, jax.numpy as jnp
        import numpy as np
        N = 625
        IN = 256
        HID = 256
        H = 4
        C = HID // H
        E = 10000
        NEG_SLOPE = 0.2

        def _gatv2_layer(x, src, dst, Wl, Wr, att, bias):
            xl = (x @ Wl).reshape(N, H, C)
            xr = (x @ Wr).reshape(N, H, C)
            e = jax.nn.leaky_relu(xl[src] + xr[dst], NEG_SLOPE)
            score = jnp.einsum('ehc,hc->eh', e, att)
            m = jax.ops.segment_max(score, dst, num_segments=N)
            m = jnp.where(jnp.isfinite(m), m, 0.0)
            p = jnp.exp(score - jax.lax.stop_gradient(m)[dst])
            denom = jax.ops.segment_sum(p, dst, num_segments=N)
            alpha = p / (denom[dst] + 1e-16)
            out = jax.ops.segment_sum(alpha[:, :, None] * xl[src], dst, num_segments=N)
            return out.reshape(N, H * C) + bias
        loops = jnp.arange(N, dtype=edge_index.dtype)
        ei = jnp.concatenate([edge_index, jnp.stack([loops, loops])], axis=1)
        src, dst = (ei[0], ei[1])
        h = jax.nn.elu(_gatv2_layer(x, src, dst, Wl0, Wr0, att0, b0))
        h = jax.nn.elu(_gatv2_layer(h, src, dst, Wl1, Wr1, att1, b1))
        return h

    def _L2_ffn_ref(x, W1, b1, Wg, bg, Wd, bd):
        import jax, jax.numpy as jnp
        import numpy as np
        C = 256
        HID = 1024
        E = 8
        TEMP = 1.0
        orig_shape = x.shape
        xf = x.reshape(-1, orig_shape[-1])
        H = jax.nn.gelu(xf @ W1 + b1, approximate=False)
        probs = jax.nn.softmax((H @ Wg + bg) / TEMP, axis=-1)
        assign = jnp.argmax(probs, axis=-1)
        out = jnp.zeros_like(xf)
        for e in range(Wd.shape[0]):
            y = H @ Wd[e] + bd[e]
            sel = (assign == e)[:, None]
            out = out + jnp.where(sel, probs[:, e:e + 1] * y, 0.0)
        return out.reshape(orig_shape)

    def _L3_gnn_ref(x, edge_index, W1, W2):
        import jax, jax.numpy as jnp
        import numpy as np
        N = 50000
        E = 25000
        D = 256

        def gcn_conv(x, W, src, dst, n):
            h = x @ W
            ones = jnp.ones(src.shape[0], dtype=h.dtype)
            deg = jax.ops.segment_sum(ones, dst, num_segments=n)
            dinv = jnp.where(deg > 0, jax.lax.rsqrt(deg), 0.0)
            norm = dinv[src] * dinv[dst]
            msgs = h[src] * norm[:, None]
            return jax.ops.segment_sum(msgs, dst, num_segments=n)
        n = x.shape[0]
        loops = jnp.arange(n, dtype=edge_index.dtype)
        src = jnp.concatenate([edge_index[0], loops])
        dst = jnp.concatenate([edge_index[1], loops])
        h = gcn_conv(x, W1, src, dst, n)
        h = jax.nn.relu(h)
        return gcn_conv(h, W2, src, dst, n)

    def _L3_ffn_ref(features, router_w1, router_b1, router_w2, router_b2, expert_w1, expert_b1, expert_w2, expert_b2, expert_w3, expert_b3):
        import jax, jax.numpy as jnp
        import numpy as np
        E, D, H, TOP_K = (6, 256, 256, 2)
        ROUTER_H = D // 2
        rh = jax.nn.relu(features @ router_w1 + router_b1)
        expert_logits = jax.nn.softmax(rh @ router_w2 + router_b2, axis=-1)
        top_w, top_i = jax.lax.top_k(expert_logits, TOP_K)
        routing_weights = jax.nn.softmax(top_w, axis=-1)
        h1 = jax.nn.relu(jnp.einsum('bsd,edh->bseh', features, expert_w1) + expert_b1)
        h2 = jax.nn.relu(jnp.einsum('bseh,ehf->bsef', h1, expert_w2) + expert_b2)
        expert_out = jnp.einsum('bsef,efo->bseo', h2, expert_w3) + expert_b3
        sel = jnp.take_along_axis(expert_out, top_i[:, :, :, None], axis=2)
        combined = jnp.sum(sel * routing_weights[..., None], axis=2)
        return combined
    edge_index = jnp.stack([src, dst])
    x = x + _L0_gnn_ref(_layernorm(x, axis=-1), edge_index, edge_attr_64, L0_gnn_W1, L0_gnn_b1, L0_gnn_W2, L0_gnn_b2, L0_gnn_W3, L0_gnn_b3, L0_gnn_W4, L0_gnn_b4)
    x = x + _L0_ffn_ref(_layernorm(x, axis=-1)[None], L0_ffn_Wg, L0_ffn_bg, L0_ffn_bias, L0_ffn_W1, L0_ffn_b1, L0_ffn_W2, L0_ffn_b2)[0]
    x = x + _L1_gnn_ref(_layernorm(x, axis=-1), edge_index, L1_gnn_W1, L1_gnn_b1, L1_gnn_W2, L1_gnn_b2)
    x = x + _L1_ffn_ref(_layernorm(x, axis=-1)[None], L1_ffn_Wg, L1_ffn_bg, L1_ffn_W1, L1_ffn_b1, L1_ffn_W2, L1_ffn_b2)[0]
    x = x + _L2_gnn_ref(_layernorm(x, axis=-1), edge_index, L2_gnn_Wl0, L2_gnn_Wr0, L2_gnn_att0, L2_gnn_b0, L2_gnn_Wl1, L2_gnn_Wr1, L2_gnn_att1, L2_gnn_b1)
    x = x + _L2_ffn_ref(_layernorm(x, axis=-1)[None], L2_ffn_W1, L2_ffn_b1, L2_ffn_Wg, L2_ffn_bg, L2_ffn_Wd, L2_ffn_bd)[0]
    x = x + _L3_gnn_ref(_layernorm(x, axis=-1), edge_index, L3_gnn_W1, L3_gnn_W2)
    x = x + _L3_ffn_ref(_layernorm(x, axis=-1)[None], L3_ffn_router_w1, L3_ffn_router_b1, L3_ffn_router_w2, L3_ffn_router_b2, L3_ffn_expert_w1, L3_ffn_expert_b1, L3_ffn_expert_w2, L3_ffn_expert_b2, L3_ffn_expert_w3, L3_ffn_expert_b3)[0]
    return x

_drawn_inputs = setup_inputs


def setup_inputs(seed=0):
    import zlib

    import numpy as np

    out = dict(_drawn_inputs(seed))
    spreads = {'L0_ffn_bias': (0.0, 0.276),
     'L1_gnn_b1': (0.0, 0.397),
     'L1_gnn_b2': (0.0, 0.1),
     'L1_ffn_bg': (0.0, 0.1),
     'L1_ffn_b1': (0.0, 0.423),
     'L1_ffn_b2': (0.0, 0.1),
     'L2_gnn_b0': (0.0, 0.1),
     'L2_gnn_b1': (0.0, 0.1),
     'L2_ffn_b1': (0.0, 0.8),
     'L2_ffn_bg': (0.0, 0.628),
     'L2_ffn_bd': (0.0, 0.8),
     'L3_ffn_router_b1': (0.0, 0.421),
     'L3_ffn_router_b2': (0.0, 0.332),
     'L3_ffn_expert_b1': (0.0, 2.0),
     'L3_ffn_expert_b2': (0.0, 0.599),
     'L3_ffn_expert_b3': (0.0, 0.474)}
    factors = {'L0_gnn_b1': 3.043,
     'L0_gnn_b3': 6.593,
     'L0_ffn_bg': 7.374,
     'L0_ffn_b1': 8.0,
     'L0_ffn_b2': 5.637,
     'L2_gnn_Wr0': 6.35,
     'L2_gnn_Wr1': 8.0,
     'L2_gnn_att1': 7.63,
     'L2_ffn_W1': 4.847,
     'L2_ffn_Wg': 5.601,
     'L2_ffn_Wd': 5.406,
     'L3_ffn_expert_w1': 3.829}
    for name, (base, spread) in spreads.items():
        noise = np.random.default_rng([zlib.crc32(name.encode()), seed]).standard_normal(out[name].shape)
        drawn = base * np.exp(spread * noise) if base else spread * noise
        out[name] = jnp.asarray(drawn.astype(out[name].dtype))
    for name, factor in factors.items():
        out[name] = (out[name] * factor).astype(out[name].dtype)
    return out
```

```python
from contextlib import ExitStack

import numpy as np

import concourse.bass as bass
from concourse import mybir

F32 = mybir.dt.float32
F32R = mybir.dt.float32r
BF16 = mybir.dt.bfloat16
I32 = mybir.dt.int32
U32 = mybir.dt.uint32
ALU = mybir.AluOpType
ACT = mybir.ActivationFunctionType
AX = mybir.AxisListType

N, E, D, ED, H0 = 625, 10000, 256, 64, 512
P = 125
NT, ET = N // P, E // P
NP = N + 1
NH = NP // 2
DC, HC = D // 128, H0 // 128
HEADS, HD = 4, 64
GH = 64
U = 4
EI = ET // U
LN_EPS = 1e-5
NEG = -1.0e30

FFNS = {
    "f0": dict(experts=8, hidden=4, act=ACT.Relu, layer=1),
    "f1": dict(experts=8, hidden=4, act=ACT.Gelu, layer=3),
    "f2": dict(experts=8, hidden=8, act=ACT.Gelu, layer=5),
    "f3": dict(experts=6, hidden=2, act=ACT.Relu, layer=7),
}


class Signal:

    def __init__(self, sem, base):
        self.sem, self.base = sem, base

    def __call__(self, n):
        return self.sem, self.base + n


def build(nc, a, out):
    with ExitStack() as ctx:
        def sb(name, shape, dt=F32):
            return ctx.enter_context(nc.sbuf_tensor(name, shape, dt))

        def sem(name):
            return ctx.enter_context(nc.semaphore(name))

        def dram(name, shape):
            return nc.dram_tensor(name, shape, F32).ap()

        P_tab = dram("P_tab", [N, H0])
        Q_tab = dram("Q_tab", [N, H0])
        XL_tab = [dram(f"XL_tab{l}", [N, D]) for l in range(2)]
        XR_tab = [dram(f"XR_tab{l}", [N, D]) for l in range(2)]
        S_tab = [dram(f"S_tab{l}", [N * (N + 1), HEADS]) for l in range(2)]

        x = sb("x", [P, NT, D])
        xn = sb("xn", [P, NT, D])
        xnT = sb("xnT", [128, DC, NP])
        AT = sb("AT", [P, NT, NP])
        ident = sb("ident", [128, 128])
        iota = sb("iota", [128, NP])
        iota8 = iota[0:P, 0:8]
        ones = sb("ones", [128, 8])
        zrow = sb("zrow", [1, 512], BF16)
        neghalf = sb("neghalf", [P, 8])
        negfill = sb("negfill", [P, N])
        src_i = sb("src_i", [P, ET], I32)
        dst_i = sb("dst_i", [P, ET], I32)
        pair_i = sb("pair_i", [P, ET], I32)
        srcf = sb("srcf", [P, ET])
        dstf = sb("dstf", [P, ET])
        deg = sb("deg", [P, 8])
        dinv = sb("dinv", [P, 8])
        dinv2 = sb("dinv2", [P, 8])
        indeg_row = sb("indeg_row", [1, NP])
        nw = sb("nw", [P, 4, 8])
        stats = sb("stats", [P, NT, 6])
        mv = sb("mv", [P, NT, 2])
        rstd = sb("rstd", [P, 8])
        bias_rows = sb("bias_rows", [P, 4, D])
        b1row = sb("b1row", [P, H0])
        gcnb = sb("gcnb", [P, GH])
        att = sb("att", [P, 2, D])
        b3T = sb("b3T", [128, HC])
        ffb = {"f0": sb("f0_b", [128, 8 * 4]), "f1": sb("f1_b", [128, 8 * 4]), "f2": sb("f2_b", [128, 8]),
               "f3": sb("f3_b", [128, 6 * 4]), "rt": sb("rt_b", [128, 1])}
        ffb2 = {k: sb(k + "_b2", [8, D]) for k in FFNS}
        wg = {"f0": sb("f0_wg", [128, DC, 8]), "f1": sb("f1_wg", [128, DC, 8]), "f2": sb("f2_wg", [128, 8, 8]),
              "f3": sb("f3_wg", [128, 6])}
        rw1 = sb("rw1", [128, DC, 128])
        rhT = sb("rhT", [128, NP])
        bg = sb("bg", [P, 5, 8])
        lg = sb("lg", [P, NT, 8])
        top = sb("top", [P, NT, 8])
        topi = sb("topi", [P, NT, 8], U32)
        topf = sb("topf", [P, NT, 8])
        gt = sb("gt", [P, 4, NT, 8])
        gate = sb("gate", [P, NT, 8])
        gateT = sb("gateT", [8, NP])
        OH = sb("OH", [P, 2, NP], F32R)
        hi = sb("hi", [P, 2, H0], F32R)
        lo = sb("lo", [P, 2, H0], F32R)
        eaT = sb("eaT", [ED, 2, 2 * P])
        gidx = sb("gidx", [P, 2, 4], I32)
        sidx = sb("sidx", [P, 2, 2], I32)
        s4 = sb("s4", [P, 2, 2, HEADS])
        s4self = sb("s4self", [P, NT, HEADS])
        nmax = sb("nmax", [P, NT, HEADS])
        rden = sb("rden", [P, NT, HEADS])
        xl1 = sb("xl1", [P, NT, HEADS, HD + 1])
        w1s = sb("w1s", [128, 2, 2048])
        w2s = sb("w2s", [128, 2, 2048])
        WA = sb("WA", [128, 9216])
        W1a = WA[:, 0:1024].rearrange("p (c m) -> p c m", c=DC)
        W1b = WA[:, 1024:2048].rearrange("p (c m) -> p c m", c=DC)
        W1c = WA[0:ED, 2048:2560]
        W2 = WA[:, 2560:4608].rearrange("p (c m) -> p c m", c=HC)
        W3 = WA[:, 4608:7680].rearrange("p (c m) -> p c m", c=DC + HC)
        W4 = WA[:, 7680:8704].rearrange("p (c m) -> p c m", c=HC)
        b2row = WA[0:1, 8704:9216]
        C1W1 = WA[:, 0:128].rearrange("p (c m) -> p c m", c=DC)
        C1W2 = WA[0:GH, 128:384]
        GW = [[WA[:, 512 * (1 + 2 * l + r):512 * (2 + 2 * l + r)].rearrange("p (c m) -> p c m", c=DC)
               for r in range(2)] for l in range(2)]
        C3W = [WA[:, 2560 + 512 * l:3072 + 512 * l].rearrange("p (c m) -> p c m", c=DC) for l in range(2)]
        Z = sb("Z", [128, 13312])

        def z(at, dims, parts=128):
            n = int(np.prod(dims))
            v = Z[0:parts, at:at + n]
            names = "abcd"[:len(dims)]
            if len(dims) == 1:
                return v
            return v.rearrange(f"p ({' '.join(names)}) -> p {' '.join(names)}", **dict(zip(names, dims)))

        PQ = z(0, [2, NT, H0], P)
        gP = z(5120, [2, H0], P)
        gQ = z(6144, [2, H0], P)
        tsum = z(7168, [2, H0], P)
        aggT = z(0, [HC, NP])
        msgT = z(2504, [HC, NP])
        gT = z(8192, [HC, NP])
        ohS = Z[0:P, 11264:11264 + 2 * NP].bitcast(BF16).rearrange("p (s n) -> p s n", s=4)
        hT = z(0, [2, HC, NP])
        HT8 = z(0, [2 * HC, NP])
        h2T = z(5008, [2, DC, NP])
        hs = z(0, [NT, D], P)
        cT = z(1280, [DC, NP])
        h1c = z(2600, [NT, D], P)
        ctmp = z(3900, [NT, D], P)
        XLR = z(0, [2, NT, D], P)
        ag = z(2560, [2, 2, D], P)
        bgth = z(3584, [2, 2, D], P)
        sf = z(4608, [NT, D], P)
        sf2 = z(5888, [NT, D], P)
        Sd = z(0, [2, N, HEADS], P)
        ex = z(5000, [HEADS, N], P)
        PT = z(7500, [NT, HEADS, P], P)
        v = z(10000, [NT, D], P)
        v2 = z(11280, [NT, D], P)

        PS = ctx.enter_context(nc.psum_tensor("PS", [128, 8, 512], F32))

        ld_first = [sem(f"ld_first{i}") for i in range(6)]
        ld_small = sem("ld_small")
        ld_w0 = sem("ld_w0")
        ld_wg = sem("ld_wg")
        c_iota, c_ident, c_ones, c_zero, c_half, c_neg = (sem(s) for s in ("c_iota", "c_ident", "c_ones", "c_zero", "c_half", "c_neg"))
        c_xnT = sem("c_xnT")
        s_init = sem("s_init")
        idx_f = sem("idx_f")
        pairs_ready = sem("pairs_ready")
        ln_var = sem("ln_var")
        ln_pow = sem("ln_pow")
        ln_xn = sem("ln_xn")
        ln_tr = sem("ln_tr")
        ln_xnT = sem("ln_xnT")
        x_new = [sem(f"x_new{i}") for i in range(9)]
        dch = sem("dch")
        ach = sem("ach")
        pq_mm, p_ev, q_ev, pq_st = sem("pq_mm"), sem("p_ev"), sem("q_ev"), sem("pq_st")
        a_oh, a_mm, a_done, at_ready = sem("a_oh"), sem("a_mm"), sem("a_done"), sem("at_ready")
        deg_mm, deg_v, deg_pow, dinv_ready = sem("deg_mm"), sem("deg_v"), sem("deg_pow"), sem("dinv_ready")
        ea_ld = [sem(f"ea_ld{i}") for i in range(2)]
        g_idx = sem("g_idx")
        pool_go = sem("pool_go")
        gp_ld = [sem(f"gp_ld{i}") for i in range(2)]
        l0_free = sem("l0_free")
        l0_oh = sem("l0_oh")
        l0_e = sem("l0_e")
        l0_sum = sem("l0_sum")
        l0_pre = sem("l0_pre")
        l0_hi = sem("l0_hi")
        l0_lo = sem("l0_lo")
        l0_seg = sem("l0_seg")
        l0_acc = sem("l0_acc")
        l0_aggT, l0_m, l0_msgT, l0_g, l0_gT, l0_o = (sem(s) for s in ("l0_aggT", "l0_m", "l0_msgT", "l0_g", "l0_gT", "l0_o"))
        l0_base = sem("l0_base")
        ff, raised = {k: {} for k in FFNS}, {}
        for k, f in FFNS.items():
            n_e, hc = f["experts"], f["hidden"]
            totals = dict(w1a=8 * n_e, w1b=8 * n_e, w2a=8 * n_e, w2b=8 * n_e, lgmm=1, lgv=1, gexp=1, gate=1, gT=NT, gTs=NT, b2mm=NT,
                          hmm=hc * n_e, h=hc * n_e + 2, ymm=NT * n_e)
            if k == "f2":
                totals.update(w1a=16, w1b=0, hmm=hc, h=hc)
            if k == "f3":
                totals.update(w1a=16 * n_e, w1b=16 * n_e, lgv=2, gexp=2, h=hc * n_e, h2mm=hc * n_e, h2=hc * n_e + 2, rmm=1, rh=1)
            if k == "f1":
                totals.update(lgv=0, gexp=0)
            for n, total in totals.items():
                if n not in raised:
                    raised[n] = [sem(f"ff_{n}"), 0]
                ff[k][n] = Signal(*raised[n])
                raised[n][1] += total
        gc = {k: {s: sem(f"{k}_{s}") for s in ("hmm", "hs", "amm", "aT", "ymm", "h1", "a2mm", "a2T", "omm")}
              for k in ("c1", "c3")}
        totals = dict(xmm=2 * NT, xev=2 * NT, st=32, self=1, diag=16 * NT, gi=ET, gl0=16 * ET, gl1=16 * ET, lr=3 * ET // 2,
                      s4=ET // 2, si=ET // 2, scat0=8 * ET, scat1=8 * ET, sd0=16 * 3, sd1=16 * 2, max=NT, exp=NT * HEADS, tr=NT * NT,
                      pt=NT * NT, omm=NT, min=1, emin=1, h=NT, htr=NT, hT=NT)
        ga_sems = {n: sem(f"ga_{n}") for n in totals}
        ga = [{n: Signal(ga_sems[n], l * total) for n, total in totals.items()} for l in range(2)]
        out_done = sem("out_done")

        block = ctx.enter_context(nc.Block())
        bg_of = {"f0": 0, "f1": 2, "f2": 3, "f3": 4}

        @block.sync
        def _(sp):
            sp.dma_start(x[:, :, :], a["x"].rearrange("(t p) d -> p t d", p=P)).then_inc(ld_first[2], 16)
            sp.dma_start(src_i[:, :], a["src"]).then_inc(ld_first[0], 16)
            sp.dma_start(dst_i[:, :], a["dst"]).then_inc(ld_first[1], 16)
            sp.dma_start(W1a, a["L0_gnn_W1"][0:D, :].rearrange("(c p) m -> p c m", p=128)).then_inc(ld_w0, 16)
            sp.dma_start(W1b, a["L0_gnn_W1"][D:2 * D, :].rearrange("(c p) m -> p c m", p=128)).then_inc(ld_w0, 16)
            sp.dma_start(W1c, a["L0_gnn_W1"][2 * D:2 * D + ED, :]).then_inc(ld_w0, 16)
            sp.dma_start(W2, a["L0_gnn_W2"].rearrange("(c p) m -> p c m", p=128)).then_inc(ld_w0, 16)
            sp.dma_start(W3, a["L0_gnn_W3"].rearrange("(c p) m -> p c m", p=128)).then_inc(ld_w0, 16)
            sp.dma_start(W4, a["L0_gnn_W4"].rearrange("(c p) m -> p c m", p=128)).then_inc(ld_w0, 16)
            sp.dma_start(b2row, a["L0_gnn_b2"]).then_inc(ld_w0, 16)
            sp.dma_start(b1row[:, :], a["L0_gnn_b1"].to_broadcast([P, H0])).then_inc(ld_w0, 16)
            n = 0
            for dst_ap, src_ap in (
                    [(bias_rows[:, j, :], a[k].to_broadcast([P, D])) for j, k in
                     enumerate(("L0_gnn_b4", "L1_gnn_b2", "L2_gnn_b0", "L2_gnn_b1"))]
                    + [(gcnb[:, :], a["L1_gnn_b1"].to_broadcast([P, GH])), (b3T[:, :], a["L0_gnn_b3"])]
                    + [(att[:, l, :], a[f"L2_gnn_att{l}"].to_broadcast([P, D])) for l in range(2)]
                    + [(ffb[k][:, :], a[s]) for k, s in
                       (("f0", "L0_ffn_b1"), ("f1", "L1_ffn_b1"), ("f2", "L2_ffn_b1"), ("f3", "L3_b12"), ("rt", "L3_ffn_router_b1"))]
                    + [(ffb2[k][0:FFNS[k]["experts"], :], a[s]) for k, s in
                       (("f0", "L0_ffn_b2"), ("f1", "L1_ffn_b2"), ("f2", "L2_ffn_bd"), ("f3", "L3_ffn_expert_b3"))]
                    + [(wg[k][:, :, :], a[s].rearrange("(c p) e -> p c e", p=128)) for k, s in
                       (("f0", "L0_ffn_Wg"), ("f1", "L1_ffn_Wg"), ("f2", "L2_ffn_Wg"))]
                    + [(wg["f3"][:, :], a["L3_ffn_router_w2"]),
                       (rw1[:, :, :], a["L3_ffn_router_w1"].rearrange("(c p) m -> p c m", p=128))]
                    + [(bg[:, j, 0:m], a[k].to_broadcast([P, m])) for j, (k, m) in
                       enumerate((("L0_ffn_bg", 8), ("L0_ffn_bias", 8), ("L1_ffn_bg", 8), ("L2_ffn_bg", 8), ("L3_ffn_router_b2", 6)))]):
                sp.dma_start(dst_ap, src_ap).then_inc(ld_small, 16)
                n += 1
            assert n == N_SMALL
            sp.wait_ge(c_neg, 1)
            for l in range(2):
                rows = S_tab[l][0:N * N, :].rearrange("(t p s) h -> t p (s h)", t=NT, p=P)
                for t in range(NT):
                    for q in range(HEADS):
                        sp.dma_start(rows[t, :, q * N:(q + 1) * N], negfill[:, :]).then_inc(s_init, 16)
            for j, tab in enumerate((P_tab, Q_tab)):
                sp.wait_ge((p_ev, q_ev)[j], NT)
                sp.dma_start(tab.rearrange("(t p) m -> p t m", p=P), PQ[:, j, :, :]).then_inc(pq_st, 16)
            for h in range(2):
                sp.dma_start(eaT[:, h, :], a["edge_attr_64"][h]).then_inc(ea_ld[h], 16)
            with sp.Fori(0, EI - 1) as i:
                for h in range(2):
                    sp.wait_ge(l0_e, U * i + 2 * h + 2)
                    sp.dma_start(eaT[:, h, :], a["edge_attr_64"][bass.ds((i + 1) * 2 + h, 1)].rearrange("a p m -> (a p) m"))\
                        .then_inc(ea_ld[h], 16)

            def experts(k, w1, w2, before):
                f, n_e = ff[k], FFNS[k]["experts"]
                before()
                for u, (s1, s2) in enumerate(((f["w1a"].sem, f["w2a"].sem), (f["w1b"].sem, f["w2b"].sem))):
                    w1(0, u, s1)
                    w2(0, u, s2)
                with sp.Fori(1, n_e // 2) as i:
                    for u, (s1, s2) in enumerate(((f["w1a"].sem, f["w2a"].sem), (f["w1b"].sem, f["w2b"].sem))):
                        if w1 is not nothing:
                            sp.wait_ge(*f["hmm" if k != "f3" else "h2mm"](FFNS[k]["hidden"] * (2 * i - 2 + u + 1)))
                            w1(i, u, s1)
                        sp.wait_ge(*f["ymm"](NT * (2 * i - 2 + u + 1)))
                        w2(i, u, s2)

            def nothing(i, u, s):
                pass

            def wload(slots, cols, name):
                def load(i, u, s):
                    dst_ap = slots[:, u, 0:cols]
                    src_ap = a[name][bass.ds(2 * i + u, 1)].rearrange("e p m -> (e p) m") if not isinstance(i, int) \
                        else a[name][2 * i + u]
                    sp.dma_start(dst_ap, src_ap).then_inc(s, 16)
                return load

            experts("f0", wload(w1s, 1024, "L0_ffn_W1"), wload(w2s, 1024, "L0_ffn_W2"), lambda: None)
            sp.wait_ge(l0_o, NT)
            sp.dma_start(C1W1, a["L1_gnn_W1"].rearrange("(c p) m -> p c m", p=128)).then_inc(ld_wg, 16)
            sp.dma_start(C1W2, a["L1_gnn_W2"]).then_inc(ld_wg, 16)
            for l in range(2):
                for r, k in enumerate(("l", "r")):
                    sp.dma_start(GW[l][r], a[f"L2_gnn_W{k}{l}"].rearrange("(c p) m -> p c m", p=128)).then_inc(ld_wg, 16)
                sp.dma_start(C3W[l], a[f"L3_gnn_W{l + 1}"].rearrange("(c p) m -> p c m", p=128)).then_inc(ld_wg, 16)
            experts("f1", wload(w1s, 1024, "L1_ffn_W1"), wload(w2s, 1024, "L1_ffn_W2"),
                    lambda: sp.wait_ge(*ff["f0"]["ymm"](8 * NT)))

            def gat_tables(l):
                g = ga[l]
                for r, tab in enumerate((XL_tab[l], XR_tab[l])):
                    sp.wait_ge(*g["xev"](NT * (r + 1)))
                    sp.dma_start(tab.rearrange("(t p) m -> p t m", p=P), XLR[:, r, :, :]).then_inc(g["st"].sem, 16)
                sp.wait_ge(*g["self"](1))
                sp.wait_ge(s_init, 16 * 2 * NT * HEADS)
                for t in range(NT):
                    diag = S_tab[l].rearrange("(t p r) h -> t p r h", t=NT, p=P)[t, :, 0, :]
                    sp.dma_start(diag, s4self[:, t, :]).then_inc(g["diag"].sem, 16)
                for h in range(2):
                    sp.wait_ge(*g[f"scat{h}"](8 * ET))
                rows = S_tab[l][0:N * N, :].rearrange("(t p s) h -> t p s h", t=NT, p=P)
                for t in range(NT):
                    if t >= 2:
                        sp.wait_ge(*g["exp"](HEADS * (t - 1)))
                    sp.dma_start(Sd[:, t % 2, :, :], rows[t]).then_inc(g[f"sd{t % 2}"].sem, 16)

            gat_tables(0)
            gat_tables(1)

            def before_f2():
                sp.wait_ge(*ff["f1"]["ymm"](8 * NT))
                sp.dma_start(w1s[:, 0, :], a["L2_ffn_W1"]).then_inc(ff["f2"]["w1a"].sem, 16)

            experts("f2", nothing, wload(w2s, 2048, "L2_ffn_Wd"), before_f2)

            def before_f3():
                sp.wait_ge(*ff["f2"]["ymm"](8 * NT))

            def w12(i, u, s):
                for j in range(2):
                    name = f"L3_ffn_expert_w{j + 1}"
                    src_ap = a[name][2 * i + u] if isinstance(i, int) else \
                        a[name][bass.ds(2 * i + u, 1)].rearrange("e p m -> (e p) m")
                    sp.dma_start(w1s[:, u, 512 * j:512 * j + 512], src_ap).then_inc(s, 16)

            experts("f3", w12, wload(w2s, 512, "L3_ffn_expert_w3"), before_f3)
            sp.wait_ge(x_new[8], NT * 7)
            sp.dma_start(out.rearrange("(t p) d -> p t d", p=P), x[:, :, :]).then_inc(out_done, 16)
            sp.wait_ge(out_done, 16)
            sp.wait_ge(pq_st, 32)
            for l in range(2):
                sp.wait_ge(*ga[l]["st"](32))
                sp.wait_ge(*ga[l]["diag"](16 * NT))
                for h in range(2):
                    sp.wait_ge(*ga[l][f"scat{h}"](8 * ET))

        @block.gpsimd
        def _(pool):
            g = nc.gpsimd
            g.iota(iota[:, :], [[1, NP]], base=0, channel_multiplier=0, allow_small_or_imprecise_dtypes=True).then_inc(c_iota, 1)
            g.memset(ident[:, :], 0.0).then_inc(c_ident, 1)
            g.memset(ones[:, :], 1.0).then_inc(c_ones, 1)
            g.memset(xnT[:, :, N:NP], 0.0).then_inc(c_xnT, 1)
            g.memset(zrow[:, :], 0.0).then_inc(c_zero, 1)
            g.memset(neghalf[:, :], -0.5).then_inc(c_half, 1)
            g.memset(negfill[:, :], NEG).then_inc(c_neg, 1)
            g.memset(xl1[:, :, :, HD:HD + 1], 1.0).then_inc(c_ones, 1)
            pool.wait_ge(c_ident, 1)
            g.affine_select(out=ident[:, :], in_=ident[:, :], compare_op=ALU.not_equal, fill=1.0, base=0,
                            pattern=[[-1, 128]], channel_multiplier=1).then_inc(c_ident, 1)

            def layernorm_pow(i):
                pool.wait_ge(ln_var, i + 1)
                g.tensor_tensor(nw[:, 1, 0:NT], nw[:, 0, 0:NT], neghalf[:, 0:NT], ALU.pow).then_inc(ln_pow, 1)

            pool.wait_ge(c_half, 1)
            layernorm_pow(0)
            pool.wait_ge(deg_v, 1)
            g.tensor_tensor(nw[:, 1, 0:NT], deg[:, 0:NT], neghalf[:, 0:NT], ALU.pow).then_inc(deg_pow, 1)

            pool.wait_ge(ld_first[0], 16)
            pool.wait_ge(ld_first[1], 16)
            pool.wait_ge(pq_st, 32)

            def gather_step(i):
                for h in range(2):
                    if h or not isinstance(i, int):
                        for u in range(2):
                            pool.wait_ge(gp_ld[u], 64 * i + 32 * h)
                    g.tensor_copy(gidx[:, h, 0:2], src_i[:, bass.ds(U * i + 2 * h, 2)]).then_inc(g_idx, 1)
                    g.tensor_copy(gidx[:, h, 2:4], dst_i[:, bass.ds(U * i + 2 * h, 2)]).then_inc(g_idx, 1)
                    pool.wait_ge(g_idx, 4 * i + 2 * h + 2)
                    for u in range(2):
                        pool.wait_ge(l0_free, U * i + 2 * h + u + 1)
                        pool.sem_inc(pool_go)
                        g.indirect_dma_start(gP[:, u, :], None, P_tab, bass.IndirectOffsetOnAxis(ap=gidx[:, h, u:u + 1], axis=0))\
                            .then_inc(gp_ld[u], 16)
                        g.indirect_dma_start(gQ[:, u, :], None, Q_tab, bass.IndirectOffsetOnAxis(ap=gidx[:, h, 2 + u:3 + u], axis=0))\
                            .then_inc(gp_ld[u], 16)

            gather_step(0)
            with pool.Fori(1, EI) as i:
                gather_step(i)
            for i in range(1, 5):
                layernorm_pow(i)

            def gat(l):
                q = ga[l]
                pool.wait_ge(*q["st"](32))
                q_gl = (q["gl0"], q["gl1"])

                def indices(p, par, k):
                    if not isinstance(k, int) or k:
                        pool.wait_ge(*q_gl[par](64 * k))
                        pool.wait_ge(*q["s4"](p - 1))
                    g.tensor_copy(gidx[:, par, 0:2], src_i[:, bass.ds(2 * p, 2)]).then_inc(q["gi"].sem, 1)
                    g.tensor_copy(gidx[:, par, 2:4], dst_i[:, bass.ds(2 * p, 2)]).then_inc(q["gi"].sem, 1)
                    pool.wait_ge(*q["gi"](2 * p + 2))
                    pool.sem_inc(pool_go)

                def gathers(par, j):
                    g.indirect_dma_start(ag[:, par, j, :], None, XL_tab[l], bass.IndirectOffsetOnAxis(ap=gidx[:, par, j:j + 1], axis=0))\
                        .then_inc(q_gl[par].sem, 16)
                    g.indirect_dma_start(bgth[:, par, j, :], None, XR_tab[l], bass.IndirectOffsetOnAxis(ap=gidx[:, par, 2 + j:3 + j], axis=0))\
                        .then_inc(q_gl[par].sem, 16)

                def scatter(p, par, k, j):
                    if j == 0:
                        g.tensor_copy(sidx[:, par, :], pair_i[:, bass.ds(2 * p, 2)]).then_inc(q["si"].sem, 1)
                        pool.wait_ge(*q["si"](p + 1))
                        pool.wait_ge(*q["s4"](p + 1))
                        if not isinstance(p, int) or p:
                            pool.wait_ge(*q[f"scat{1 - par}"](32 * (k + par)))
                    else:
                        pool.wait_ge(*q[f"scat{par}"](32 * k + 16))
                    pool.sem_inc(pool_go)
                    g.indirect_dma_start(S_tab[l], bass.IndirectOffsetOnAxis(ap=sidx[:, par, j:j + 1], axis=0), s4[:, par, j, :], None)\
                        .then_inc(q[f"scat{par}"].sem, 16)

                def step(p, par, k):
                    indices(p, par, k)
                    scatter(p - 1, 1 - par, k - 1 + par, 0)
                    gathers(par, 0)
                    gathers(par, 1)
                    scatter(p - 1, 1 - par, k - 1 + par, 1)

                indices(0, 0, 0)
                gathers(0, 0)
                gathers(0, 1)
                pool.wait_ge(pairs_ready, 1)
                pool.wait_ge(*q["diag"](16 * NT))
                step(1, 1, 0)
                step(2, 0, 1)
                with pool.Fori(1, ET // 4 - 1) as i:
                    step(2 * i + 1, 1, i)
                    step(2 * i + 2, 0, i + 1)
                step(ET // 2 - 1, 1, ET // 4 - 1)
                scatter(ET // 2 - 1, 1, ET // 4 - 1, 0)
                scatter(ET // 2 - 1, 1, ET // 4 - 1, 1)

            gat(0)
            gat(1)
            for i in range(5, 8):
                layernorm_pow(i)

        @block.scalar
        def _(act):
            s = nc.scalar

            def layernorm_evac(i):
                for t in range(NT):
                    act.wait_ge(ln_tr, NT * i + t + 1)
                    s.activation(xnT[:, :, t * P:(t + 1) * P], PS[:, 6 + t % 2, 0:DC * P].rearrange("p (c n) -> p c n", c=DC),
                                 ACT.Copy).then_inc(ln_xnT, 1)

            act.wait_ge(c_xnT, 1)
            layernorm_evac(0)
            for t in range(NT):
                act.wait_ge(pq_mm, t + 1)
                s.activation(PQ[:, 0, t, :], PS[0:P, t % 4, :], ACT.Copy).then_inc(p_ev, 1)
            with act.Fori(0, EI) as i:
                for u in range(U):
                    act.wait_ge(l0_pre, U * i + u + 3)
                    act.wait_ge(l0_seg, U * i + u + 1)
                    s.activation(hi[:, u % 2, :], tsum[:, u % 2, :], ACT.Relu).then_inc(l0_hi, 1)
            act.wait_ge(l0_acc, 1)
            for c in range(HC):
                s.activation(aggT[:, c, 0:500], PS[:, c, 0:500], ACT.Copy).then_inc(l0_aggT, 1)
            s.activation(aggT[:, :, 500:NP], PS[:, 4, 0:504].rearrange("p (c n) -> p c n", c=HC), ACT.Copy).then_inc(l0_aggT, 1)
            for dst_t, mm, ev, bias in ((msgT, l0_m, l0_msgT, None), (gT, l0_g, l0_gT, b3T)):
                if bias is not None:
                    act.wait_ge(ld_small, 16 * N_SMALL)
                for m in range(HC):
                    act.wait_ge(mm, m + 1)
                    src_ap = PS[:, 2 * (m % 2):2 * (m % 2) + 2, 0:NH]
                    dst_ap = dst_t[:, m, :].rearrange("p (b n) -> p b n", b=2)
                    if bias is None:
                        s.activation(dst_ap, src_ap, ACT.Copy).then_inc(ev, 1)
                    else:
                        s.activation(dst_ap, src_ap, ACT.Relu, bias=bias[:, m:m + 1]).then_inc(ev, 1)

            def hidden(k, dst_of, mm, ev, per, col, stride, func):
                f, n_e = ff[k], FFNS[k]["experts"]
                with act.Fori(0, n_e // 2) as i:
                    for u in range(2):
                        for m in range(per):
                            act.wait_ge(*f[mm](per * (2 * i + u) + m + 1))
                            s.activation(dst_of(u)[:, m, :].rearrange("p (b n) -> p b n", b=2),
                                         PS[:, 2 * (m % 2):2 * (m % 2) + 2, 0:NH], func,
                                         bias=ffb[k][:, bass.ds(stride * (2 * i + u) + col + m, 1)]).then_inc(f[ev].sem, 1)

            def gate_exp(k, out_ap, in_ap):
                act.wait_ge(*ff[k]["lgv"](1))
                s.activation(out_ap, in_ap, ACT.Exp).then_inc(ff[k]["gexp"].sem, 1)

            layernorm_evac(1)
            gate_exp("f0", gt[:, 0, :, 0], gt[:, 1, :, 0])
            hidden("f0", lambda u: hT[:, u], "hmm", "h", HC, 0, HC, ACT.Relu)
            layernorm_evac(2)
            c = gc["c1"]
            for t in range(NT):
                act.wait_ge(c["hmm"], t + 1)
                s.activation(hs[:, t, 0:GH], PS[0:P, t % 2, 0:GH], ACT.Copy, scale=dinv[:, t:t + 1]).then_inc(c["hs"], 1)
            act.wait_ge(c["a2mm"], 1)
            s.activation(cT[0:GH, 0, :].rearrange("p (b n) -> p b n", b=2), PS[0:GH, 4:6, 0:NH], ACT.Copy).then_inc(c["a2T"], 1)
            layernorm_evac(3)
            hidden("f1", lambda u: hT[:, u], "hmm", "h", HC, 0, HC, ACT.Gelu)

            layernorm_evac(4)

            def gat(l):
                q = ga[l]
                for t in range(NT):
                    act.wait_ge(*q["xmm"](t + 1))
                    s.activation(XLR[:, 0, t, :], PS[0:P, t % 2, 0:D], ACT.Copy).then_inc(q["xev"].sem, 1)
                for t in range(NT):
                    act.wait_ge(*q["xmm"](NT + t + 1))
                    s.activation(XLR[:, 1, t, :], PS[0:P, (NT + t) % 2, 0:D], ACT.Copy).then_inc(q["xev"].sem, 1)
                for t in range(NT):
                    act.wait_ge(*q["max"](t + 1))
                    if t:
                        act.wait_ge(*q["tr"](NT * t))
                    for h in range(HEADS):
                        s.activation(ex[:, h, :], Sd[:, t % 2, :, h], ACT.Exp, bias=nmax[:, t, h:h + 1]).then_inc(q["exp"].sem, 1)
                act.wait_ge(*q["min"](1))
                s.activation(v2[:, :, :], v2[:, :, :], ACT.Exp).then_inc(q["emin"].sem, 1)
                if l == 0:
                    for t in range(NT):
                        act.wait_ge(*q["htr"](t + 1))
                        s.activation(xnT[:, :, t * P:(t + 1) * P], PS[:, 6 + t % 2, 0:DC * P].rearrange("p (c n) -> p c n", c=DC),
                                     ACT.Copy).then_inc(q["hT"].sem, 1)

            gat(0)
            gat(1)
            layernorm_evac(5)
            f = ff["f2"]
            for m in range(8):
                act.wait_ge(*f["hmm"](m + 1))
                s.activation(HT8[:, m, :].rearrange("p (b n) -> p b n", b=2), PS[:, 2 * (m % 2):2 * (m % 2) + 2, 0:NH], ACT.Gelu,
                             bias=ffb["f2"][:, m:m + 1]).then_inc(f["h"].sem, 1)
            gate_exp("f2", gt[:, 1, :, :], gt[:, 0, :, :])
            layernorm_evac(6)
            c = gc["c3"]
            for mm, ev in (("amm", "aT"), ("a2mm", "a2T")):
                for m in range(DC):
                    act.wait_ge(c[mm], m + 1)
                    s.activation(cT[:, m, :].rearrange("p (b n) -> p b n", b=2), PS[:, 2 * m:2 * m + 2, 0:NH], ACT.Copy).then_inc(c[ev], 1)
                if mm == "amm":
                    for t in range(NT):
                        act.wait_ge(c["ymm"], t + 1)
                        s.activation(h1c[:, t, :], PS[0:P, 4 + t % 2, 0:D], ACT.Relu, scale=dinv2[:, t:t + 1]).then_inc(c["h1"], 1)
            layernorm_evac(7)
            f = ff["f3"]
            act.wait_ge(*f["rmm"](1))
            s.activation(rhT[:, :].rearrange("p (b n) -> p b n", b=2), PS[:, 4:6, 0:NH], ACT.Relu, bias=ffb["rt"][:, 0:1]).then_inc(f["rh"].sem, 1)
            gate_exp("f3", gt[:, 1, :, :], gt[:, 0, :, :])
            act.wait_ge(*f["lgv"](2))
            s.activation(gt[:, 0, :, 0], gt[:, 2, :, 0], ACT.Exp).then_inc(f["gexp"].sem, 1)
            with act.Fori(0, 3) as i:
                for u in range(2):
                    for step, (mm, ev, dst_t, bank) in enumerate((("hmm", "h", hT, 0), ("h2mm", "h2", h2T, 2))):
                        for m in range(DC):
                            act.wait_ge(*f[mm](DC * (2 * i + u) + m + 1))
                            s.activation(dst_t[:, u, m, :].rearrange("p (b n) -> p b n", b=2),
                                         PS[:, 2 * (m % 2):2 * (m % 2) + 2, 0:NH], ACT.Relu,
                                         bias=ffb["f3"][:, bass.ds(4 * (2 * i + u) + 2 * step + m, 1)]).then_inc(f[ev].sem, 1)

        @block.vector
        def _(dve):
            w = nc.vector
            chain = [0]

            def link(ins):
                chain[0] += 1
                ins.then_inc(dch, 1)
                dve.wait_ge(dch, chain[0])

            def newton(ve, r0, dst):
                link(w.scalar_tensor_tensor(nw[:, 2, 0:NT], r0, -0.5, r0, ALU.mult, ALU.mult))
                link(w.tensor_tensor(nw[:, 3, 0:NT], nw[:, 2, 0:NT], ve, ALU.mult))
                return w.scalar_tensor_tensor(dst, nw[:, 3, 0:NT], 1.5, r0, ALU.add, ALU.mult)

            def layernorm(i, before):
                for t in range(NT):
                    before(t)
                    ins = w.bn_stats(stats[:, t, :], x[:, t, :])
                link(ins)
                for t in range(NT):
                    ins = w.bn_aggr(mv[:, t, :], stats[:, t, :])
                link(ins)
                w.tensor_scalar(nw[:, 0, 0:NT], mv[:, :, 1], LN_EPS, None, ALU.add).then_inc(ln_var, 1)
                dve.wait_ge(ln_pow, i + 1)
                link(newton(nw[:, 0, 0:NT], nw[:, 1, 0:NT], rstd[:, 0:NT]))
                for t in range(NT):
                    w.tensor_scalar(xn[:, t, :], x[:, t, :], mv[:, t, 0:1], rstd[:, t:t + 1], ALU.subtract, ALU.mult)\
                        .then_inc(ln_xn, 1)

            dve.wait_ge(ld_first[0], 16)
            w.tensor_copy(srcf[:, :], src_i[:, :]).then_inc(idx_f, 1)
            dve.wait_ge(ld_first[1], 16)
            w.tensor_copy(dstf[:, :], dst_i[:, :]).then_inc(idx_f, 1)
            dve.wait_ge(idx_f, 2)
            w.scalar_tensor_tensor(pair_i[:, :], dstf[:, :], float(N), srcf[:, :], ALU.mult, ALU.add).then_inc(pairs_ready, 1)
            dve.wait_ge(ld_first[2], 16)
            layernorm(0, lambda t: None)
            dve.wait_ge(ld_w0, 16 * 8)
            for t in range(NT):
                dve.wait_ge(pq_mm, NT + t + 1)
                w.tensor_tensor(PQ[:, 1, t, :], PS[0:P, (NT + t) % 4, :], b1row[:, :], ALU.add).then_inc(q_ev, 1)
            dve.wait_ge(c_iota, 1)
            dve.sem_inc(a_mm, 2)
            with dve.Fori(0, ET // 2) as i:
                for u in range(2):
                    dve.wait_ge(a_mm, 2 * i + u + 1)
                    w.tensor_scalar(ohS[:, 2 * u, :], iota[0:P, :], srcf[:, bass.ds(2 * i + u, 1)], None, ALU.is_equal)
                    w.tensor_scalar(ohS[:, 2 * u + 1, :], iota[0:P, :], dstf[:, bass.ds(2 * i + u, 1)], None, ALU.is_equal).then_inc(a_oh, 1)
            dve.wait_ge(a_done, 1)
            for k in range(NT):
                w.tensor_copy(AT[:, k, 0:500], PS[0:P, k, 0:500])
                ins = w.tensor_copy(AT[:, k, 500:NP], PS[0:P, 5 + k // 4, 126 * (k % 4):126 * (k % 4) + 126])
            link(ins)
            dve.wait_ge(c_ident, 2)
            for k in range(NT):
                w.tensor_tensor(AT[:, k, k * P:(k + 1) * P], AT[:, k, k * P:(k + 1) * P], ident[0:P, 0:P], ALU.add).then_inc(at_ready, 1)
            dve.wait_ge(deg_mm, 1)
            w.tensor_scalar(indeg_row[:, :].rearrange("p (b n) -> p b n", b=2), PS[0:1, 6:8, 0:NH], 1.0, None, ALU.subtract)
            w.tensor_copy(deg[:, 0:NT], PS[0:P, 5, 0:NT]).then_inc(deg_v, 1)
            dve.wait_ge(deg_pow, 1)
            link(newton(deg[:, 0:NT], nw[:, 1, 0:NT], dinv[:, 0:NT]))
            w.tensor_tensor(dinv2[:, 0:NT], dinv[:, 0:NT], dinv[:, 0:NT], ALU.mult).then_inc(dinv_ready, 1)
            dve.wait_ge(ld_small, 16 * N_SMALL)

            dve.sem_inc(l0_free, 2)
            dve.sem_inc(l0_pre, 2)
            dve.sem_inc(l0_seg, 2)
            with dve.Fori(0, EI) as i:
                def pre(u):
                    n = U * i + u
                    dve.wait_ge(l0_seg, n + 1)
                    w.tensor_scalar(OH[:, u % 2, :], iota[0:P, :], dstf[:, bass.ds(n, 1)], None, ALU.is_equal)
                    dve.wait_ge(gp_ld[u % 2], 64 * i + 32 * (u // 2) + 32)
                    w.tensor_tensor(tsum[:, u % 2, :], gP[:, u % 2, :], gQ[:, u % 2, :], ALU.add).then_inc(l0_free, 1)
                    dve.wait_ge(l0_e, n + 1)
                    dve.wait_ge(l0_free, n + 3)
                    w.tensor_tensor(tsum[:, u % 2, :], tsum[:, u % 2, :], PS[0:P, 5 + u % 2, :], ALU.add).then_inc(l0_pre, 1)

                def low(u):
                    n = U * i + u
                    dve.wait_ge(l0_hi, n + 1)
                    w.scalar_tensor_tensor(lo[:, u % 2, :], tsum[:, u % 2, :], 0.0, hi[:, u % 2, :].bitcast(F32), ALU.max, ALU.subtract)\
                        .then_inc(l0_lo, 1)

                pre(0)
                pre(1)
                low(0)
                pre(2)
                low(1)
                pre(3)
                low(2)
                low(3)
            for t in range(NT):
                ins = w.tensor_tensor(x[:, t, :], x[:, t, :], xn[:, t, :], ALU.add)
            link(ins)
            for t in range(NT):
                ins = w.tensor_tensor(x[:, t, :], x[:, t, :], bias_rows[:, 0, :], ALU.add)
            link(ins)
            for t in range(NT):
                dve.wait_ge(l0_o, t + 1)
                w.tensor_tensor(x[:, t, :], x[:, t, :], PS[0:P, 4 + t % 2, 0:D], ALU.add).then_inc(x_new[1], 1)

            def top2(k):
                for t in range(NT):
                    ins = w.max(top[:, t, :], lg[:, t, :])
                link(ins)
                for t in range(NT):
                    ins = w.max_index(topi[:, t, :], top[:, t, :], lg[:, t, :])
                link(ins)
                link(w.tensor_copy(topf[:, :, :], topi[:, :, :]))

            def onehot(j, dst_ap):
                for t in range(NT):
                    ins = w.tensor_scalar(dst_ap[:, t, :], iota8, topf[:, t, j:j + 1], None, ALU.is_equal)
                link(ins)

            def logits(k, biases):
                dve.wait_ge(*ff[k]["lgmm"](1))
                n_e = FFNS[k]["experts"]
                src_ap = PS[0:P, 6, 0:NT * 8].rearrange("p (t e) -> p t e", t=NT)[:, :, 0:n_e]
                for j in biases:
                    b = bg[:, j, 0:n_e].unsqueeze(1).to_broadcast([P, NT, n_e])
                    link(w.tensor_tensor(lg[:, :, 0:n_e], src_ap, b, ALU.add))
                    src_ap = lg[:, :, 0:n_e]

            def bc8(ap, n=8):
                return ap.unsqueeze(2).to_broadcast([P, NT, n])

            def residual(k):
                f = ff[k]
                for t in range(NT):
                    dve.wait_ge(*f["gT"](t + 1))
                    w.tensor_copy(gateT[0:8, t * P:(t + 1) * P], PS[0:8, 6 + t % 2, 0:P]).then_inc(f["gTs"].sem, 1)
                for t in range(NT):
                    dve.wait_ge(*f["b2mm"](t + 1))
                    w.tensor_tensor(x[:, t, :], x[:, t, :], PS[0:P, 6 + t % 2, 0:D], ALU.add)\
                        .then_inc(x_new[FFNS[k]["layer"] + 1], 1)

            def combine(k):
                f, n_e, xs = ff[k], FFNS[k]["experts"], x_new[FFNS[k]["layer"] + 1]
                with dve.Fori(0, n_e // 2) as i:
                    for u in range(2):
                        for t in range(NT):
                            n = NT * (2 * i + u) + t
                            dve.wait_ge(*f["ymm"](n + 1))
                            dve.wait_ge(xs, n + 1)
                            w.scalar_tensor_tensor(x[:, t, :], PS[0:P, 4 + (5 * u + t) % 2, 0:D], gate[:, t, bass.ds(2 * i + u, 1)],
                                                   x[:, t, :], ALU.mult, ALU.add).then_inc(xs, 1)

            def ffn_x(layer):
                n_e = {2: 8, 4: 8, 6: 8, 8: 6}[layer]
                return lambda t: dve.wait_ge(x_new[layer], NT * n_e + t + 1)

            layernorm(1, lambda t: dve.wait_ge(x_new[1], t + 1))
            logits("f0", (0, 1))
            top2("f0")
            w.tensor_tensor(gt[:, 1, :, 0], top[:, :, 1], top[:, :, 0], ALU.subtract).then_inc(ff["f0"]["lgv"].sem, 1)
            onehot(0, gt[:, 2])
            onehot(1, gt[:, 3])
            dve.wait_ge(*ff["f0"]["gexp"](1))
            link(w.tensor_scalar(gt[:, 0, :, 1], gt[:, 0, :, 0], 1.0, None, ALU.add))
            link(w.reciprocal(gt[:, 0, :, 2], gt[:, 0, :, 1]))
            link(w.tensor_tensor(gt[:, 0, :, 3], gt[:, 0, :, 0], gt[:, 0, :, 2], ALU.mult))
            link(w.tensor_tensor(gt[:, 1, :, :], gt[:, 2, :, :], bc8(gt[:, 0, :, 2]), ALU.mult))
            link(w.tensor_tensor(gt[:, 2, :, :], gt[:, 3, :, :], bc8(gt[:, 0, :, 3]), ALU.mult))
            w.tensor_tensor(gate[:, :, :], gt[:, 1, :, :], gt[:, 2, :, :], ALU.add).then_inc(ff["f0"]["gate"].sem, 1)
            residual("f0")
            combine("f0")

            layernorm(2, ffn_x(2))
            c = gc["c1"]
            for t in range(NT):
                dve.wait_ge(c["ymm"], t + 1)
                link(w.scalar_tensor_tensor(ctmp[:, t, 0:GH], PS[0:P, 2 + t % 2, 0:GH], dinv[:, t:t + 1], gcnb[:, :], ALU.mult, ALU.add))
                w.tensor_scalar(h1c[:, t, 0:GH], ctmp[:, t, 0:GH], 0.0, dinv[:, t:t + 1], ALU.max, ALU.mult).then_inc(c["h1"], 1)
            for t in range(NT):
                dve.wait_ge(c["omm"], t + 1)
                link(w.scalar_tensor_tensor(ctmp[:, t, :], PS[0:P, t % 2, 0:D], dinv[:, t:t + 1], bias_rows[:, 1, :], ALU.mult, ALU.add))
                w.scalar_tensor_tensor(x[:, t, :], ctmp[:, t, :], 0.0, x[:, t, :], ALU.max, ALU.add).then_inc(x_new[3], 1)

            layernorm(3, lambda t: dve.wait_ge(x_new[3], t + 1))
            logits("f1", (2,))
            top2("f1")
            onehot(0, gt[:, 2])
            onehot(1, gt[:, 3])
            w.tensor_tensor(gate[:, :, :], gt[:, 2, :, :], gt[:, 3, :, :], ALU.add).then_inc(ff["f1"]["gate"].sem, 1)
            residual("f1")
            combine("f1")

            layernorm(4, ffn_x(4))

            def gat(l):
                q = ga[l]
                for t in range(NT):
                    dve.wait_ge(*q["xev"](t + 1))
                    w.tensor_copy(xl1[:, t, :, 0:HD], XLR[:, 0, t, :].rearrange("p (h c) -> p h c", h=HEADS))
                dve.wait_ge(*q["xev"](2 * NT))
                link(w.tensor_tensor(sf[:, :, :], XLR[:, 0, :, :], XLR[:, 1, :, :], ALU.add))
                link(w.scalar_tensor_tensor(sf2[:, :, :], sf[:, :, :], 0.2, sf[:, :, :], ALU.mult, ALU.max))
                link(w.tensor_tensor(sf[:, :, :], sf2[:, :, :], att[:, l, :].unsqueeze(1).to_broadcast([P, NT, D]), ALU.mult))
                w.tensor_reduce(s4self[:, :, :], sf[:, :, :].rearrange("p t (h c) -> p t h c", h=HEADS), AX.X, ALU.add).then_inc(q["self"].sem, 1)
                att_b = att[:, l, :].unsqueeze(1).to_broadcast([P, 2, D])
                def scores(i):
                    for par in range(2):
                        n = 2 * i + par
                        a_, b_ = ag[:, par, :, :], bgth[:, par, :, :]
                        dve.wait_ge(*q[f"gl{par}"](64 * i + 64))
                        w.tensor_tensor(a_, a_, b_, ALU.add).then_inc(q["lr"].sem, 1)
                        dve.wait_ge(*q["lr"](3 * n + 1))
                        w.scalar_tensor_tensor(b_, a_, 0.2, a_, ALU.mult, ALU.max).then_inc(q["lr"].sem, 1)
                        dve.wait_ge(*q["lr"](3 * n + 2))
                        w.tensor_tensor(a_, b_, att_b, ALU.mult).then_inc(q["lr"].sem, 1)
                        dve.wait_ge(*q["lr"](3 * n + 3))
                        if not isinstance(i, int):
                            dve.wait_ge(*q[f"scat{par}"](32 * i))
                        w.tensor_reduce(s4[:, par, :, :], a_.rearrange("p j (h c) -> p j h c", h=HEADS), AX.X, ALU.add)\
                            .then_inc(q["s4"].sem, 1)

                scores(0)
                with dve.Fori(1, ET // 4) as i:
                    scores(i)
                def tmax(t):
                    dve.wait_ge(*q[f"sd{t % 2}"](16 * (t // 2 + 1)))
                    w.tensor_reduce(nmax[:, t, :], Sd[:, t % 2, :, :].rearrange("p s h -> p h s"), AX.X, ALU.max, negate=True)\
                        .then_inc(q["max"].sem, 1)

                def finish(t):
                    dve.wait_ge(*q["omm"](t + 1))
                    po = PS[0:P, 2 + t % 2, 0:HEADS * (HD + 1)].rearrange("p (h c) -> p h c", h=HEADS)
                    link(w.tensor_scalar(rden[:, t, :], po[:, :, HD], 1e-16, None, ALU.add))
                    link(w.reciprocal(rden[:, t, :], rden[:, t, :]))
                    link(w.tensor_tensor(v[:, t, :].rearrange("p (h c) -> p h c", h=HEADS), po[:, :, 0:HD],
                                         rden[:, t, :].unsqueeze(2).to_broadcast([P, HEADS, HD]), ALU.mult))

                tmax(0)
                for t in range(NT):
                    if t + 1 < NT:
                        tmax(t + 1)
                    for k in range(NT):
                        dve.wait_ge(*q["tr"](NT * t + k + 1))
                        if k == 0 and t:
                            dve.wait_ge(*q["omm"](t))
                        w.tensor_tensor(PT[:, k, :, :], PS[0:P, k % 2, 0:HEADS * P].rearrange("p (h n) -> p h n", h=HEADS),
                                        AT[:, k, t * P:(t + 1) * P].unsqueeze(1).to_broadcast([P, HEADS, P]), ALU.mult)\
                            .then_inc(q["pt"].sem, 1)
                    finish(t)
                link(w.tensor_tensor(v[:, :, :], v[:, :, :], bias_rows[:, 2 + l, :].unsqueeze(1).to_broadcast([P, NT, D]), ALU.add))
                w.tensor_scalar(v2[:, :, :], v[:, :, :], 0.0, None, ALU.min).then_inc(q["min"].sem, 1)
                dve.wait_ge(*q["emin"](1))
                link(w.scalar_tensor_tensor(v[:, :, :], v[:, :, :], 0.0, v2[:, :, :], ALU.max, ALU.add))
                for t in range(NT):
                    if l == 0:
                        w.tensor_scalar(xn[:, t, :], v[:, t, :], -1.0, None, ALU.add).then_inc(q["h"].sem, 1)
                    else:
                        w.scalar_tensor_tensor(x[:, t, :], v[:, t, :], -1.0, x[:, t, :], ALU.add, ALU.add).then_inc(x_new[5], 1)

            gat(0)
            gat(1)

            def softmax8(k, n_e):
                for t in range(NT):
                    ins = w.tensor_reduce(gt[:, 2, t, 0:1], lg[:, t, 0:n_e], AX.X, ALU.max)
                link(ins)
                w.tensor_tensor(gt[:, 0, :, 0:n_e], lg[:, :, 0:n_e], bc8(gt[:, 2, :, 0], n_e), ALU.subtract).then_inc(ff[k]["lgv"].sem, 1)
                dve.wait_ge(*ff[k]["gexp"](1))
                link(w.tensor_reduce(gt[:, 2, :, 1], gt[:, 1, :, 0:n_e], AX.X, ALU.add))
                link(w.reciprocal(gt[:, 2, :, 2], gt[:, 2, :, 1]))
                link(w.tensor_tensor(lg[:, :, 0:n_e], gt[:, 1, :, 0:n_e], bc8(gt[:, 2, :, 2], n_e), ALU.mult))

            layernorm(5, lambda t: dve.wait_ge(x_new[5], t + 1))
            logits("f2", (3,))
            softmax8("f2", 8)
            top2("f2")
            onehot(0, gt[:, 2])
            w.tensor_tensor(gate[:, :, :], gt[:, 2, :, :], bc8(top[:, :, 0]), ALU.mult).then_inc(ff["f2"]["gate"].sem, 1)
            residual("f2")
            combine("f2")

            layernorm(6, ffn_x(6))
            c = gc["c3"]
            for t in range(NT):
                dve.wait_ge(ln_xn, NT * 6 + t + 1)
                w.tensor_scalar(hs[:, t, :], xn[:, t, :], dinv[:, t:t + 1], None, ALU.mult).then_inc(c["hs"], 1)
            for t in range(NT):
                dve.wait_ge(c["omm"], t + 1)
                w.scalar_tensor_tensor(x[:, t, :], PS[0:P, 4 + t % 2, 0:D], dinv[:, t:t + 1], x[:, t, :], ALU.mult, ALU.add)\
                    .then_inc(x_new[7], 1)

            layernorm(7, lambda t: dve.wait_ge(x_new[7], t + 1))
            link(w.memset(lg[:, :, 6:8], -1.0))
            logits("f3", (4,))
            softmax8("f3", 6)
            top2("f3")
            w.tensor_tensor(gt[:, 2, :, 0], top[:, :, 1], top[:, :, 0], ALU.subtract).then_inc(ff["f3"]["lgv"].sem, 1)
            dve.wait_ge(*ff["f3"]["gexp"](2))
            link(w.tensor_scalar(gt[:, 0, :, 1], gt[:, 0, :, 0], 1.0, None, ALU.add))
            link(w.reciprocal(gt[:, 0, :, 2], gt[:, 0, :, 1]))
            link(w.tensor_tensor(gt[:, 0, :, 3], gt[:, 0, :, 0], gt[:, 0, :, 2], ALU.mult))
            onehot(0, gt[:, 2])
            onehot(1, gt[:, 3])
            link(w.tensor_tensor(gt[:, 1, :, :], gt[:, 2, :, :], bc8(gt[:, 0, :, 2]), ALU.mult))
            link(w.tensor_tensor(gt[:, 2, :, :], gt[:, 3, :, :], bc8(gt[:, 0, :, 3]), ALU.mult))
            w.tensor_tensor(gate[:, :, :], gt[:, 1, :, :], gt[:, 2, :, :], ALU.add).then_inc(ff["f3"]["gate"].sem, 1)
            residual("f3")
            combine("f3")

        @block.tensor
        def _(pe):
            m_ = nc.tensor

            def mm(*args, **kw):
                return m_.matmul(*args, skip_group_check=True, **kw)

            def layernorm_transposes(i):
                for t in range(NT):
                    pe.wait_ge(ln_xn, NT * i + t + 1)
                    if t >= 2:
                        pe.wait_ge(ln_xnT, NT * i + t - 1)
                    for c in range(DC):
                        ins = m_.transpose(PS[:, 6 + t % 2, c * P:(c + 1) * P], xn[:, t, c * 128:(c + 1) * 128], ident[0:P, 0:P])
                    ins.then_inc(ln_tr, 1)

            pe.wait_ge(c_ident, 2)
            layernorm_transposes(0)
            pe.wait_ge(ld_w0, 16 * 8)
            pe.wait_ge(ln_xnT, NT)
            for j, wt in enumerate((W1a, W1b)):
                for t in range(NT):
                    n = NT * j + t
                    if n >= 4:
                        pe.wait_ge(p_ev if n - 3 <= NT else q_ev, n - 3 if n - 3 <= NT else n - 3 - NT)
                    for c in range(DC):
                        ins = mm(PS[0:P, n % 4, :], xnT[:, c, t * P:(t + 1) * P], wt[:, c, :], start=(c == 0), stop=(c == DC - 1))
                    ins.then_inc(pq_mm, 1)
            pe.wait_ge(c_zero, 1)
            pe.wait_ge(q_ev, NT)
            for b in range(7):
                mm(PS[0:P, b, :], zrow[:, 0:P], zrow[:, :], start=True, stop=False)
            with pe.Fori(0, ET // 2) as i:
                for u in range(2):
                    pe.wait_ge(a_oh, 2 * i + u + 1)
                    for k in range(NT):
                        wt = ohS[:, 2 * u, k * P:(k + 1) * P]
                        mm(PS[0:P, k, 0:500], wt, ohS[:, 2 * u + 1, 0:500], start=False, stop=False)
                        ins = mm(PS[0:P, 5 + k // 4, 126 * (k % 4):126 * (k % 4) + 126], wt, ohS[:, 2 * u + 1, 500:NP],
                                 start=False, stop=False)
                    ins.then_inc(a_mm, 1)
            for b in range(7):
                ins = mm(PS[0:P, b, :], zrow[:, 0:P], zrow[:, :], start=False, stop=True)
            ins.then_inc(a_done, 1)
            pe.wait_ge(at_ready, NT)
            for t in range(NT):
                for k in range(NT):
                    mm(PS[0:P, 5, t:t + 1], AT[:, k, t * P:(t + 1) * P], ones[0:P, 0:1], start=(k == 0), stop=(k == NT - 1))
            for b in range(2):
                for k in range(NT):
                    ins = mm(PS[0:1, 6 + b, 0:NH], ones[0:P, 0:1], AT[:, k, b * NH:(b + 1) * NH], start=(k == 0), stop=(k == NT - 1))
            ins.then_inc(deg_mm, 1)

            for b in range(5):
                mm(PS[:, b, :], zrow[:, 0:128], zrow[:, :], start=True, stop=False)
            with pe.Fori(0, EI) as i:
                def edge(u):
                    n = U * i + u
                    if u % 2 == 0:
                        pe.wait_ge(ea_ld[u // 2], 16 * i + 16)
                    pe.wait_ge(l0_pre, n + 1)
                    mm(PS[0:P, 5 + u % 2, :], eaT[:, u // 2, (u % 2) * P:(u % 2 + 1) * P], W1c, start=True, stop=True).then_inc(l0_e, 1)

                def segments(u):
                    pe.wait_ge(l0_lo, U * i + u + 1)
                    for c in range(HC):
                        for part in (hi, lo):
                            wt = part[:, u % 2, c * 128:(c + 1) * 128]
                            mm(PS[:, c, 0:500], wt, OH[:, u % 2, 0:500], start=False, stop=False)
                            ins = mm(PS[:, 4, 126 * c:126 * c + 126], wt, OH[:, u % 2, 500:NP], start=False, stop=False)
                    ins.then_inc(l0_seg, 1)

                edge(0)
                edge(1)
                segments(0)
                edge(2)
                segments(1)
                edge(3)
                segments(2)
                segments(3)
            for b in range(5):
                ins = mm(PS[:, b, :], zrow[:, 0:128], zrow[:, :], start=False, stop=True)
            ins.then_inc(l0_acc, 1)
            pe.wait_ge(l0_aggT, HC + 1)
            for m in range(HC):
                if m >= 2:
                    pe.wait_ge(l0_msgT, m - 1)
                for b in range(2):
                    for c in range(HC):
                        mm(PS[:, 2 * (m % 2) + b, 0:NH], W2[:, c, m * 128:(m + 1) * 128], aggT[:, c, b * NH:(b + 1) * NH],
                           start=(c == 0), stop=False)
                    ins = mm(PS[:, 2 * (m % 2) + b, 0:NH], b2row[:, m * 128:(m + 1) * 128], indeg_row[:, b * NH:(b + 1) * NH],
                             start=False, stop=True)
                ins.then_inc(l0_m, 1)
            for m in range(HC):
                pe.wait_ge(l0_msgT, HC)
                if m >= 2:
                    pe.wait_ge(l0_gT, m - 1)
                for b in range(2):
                    for c in range(DC + HC):
                        rhs = xnT[:, c, b * NH:(b + 1) * NH] if c < DC else msgT[:, c - DC, b * NH:(b + 1) * NH]
                        ins = mm(PS[:, 2 * (m % 2) + b, 0:NH], W3[:, c, m * 128:(m + 1) * 128], rhs, start=(c == 0), stop=(c == DC + HC - 1))
                ins.then_inc(l0_g, 1)
            pe.wait_ge(l0_gT, HC)
            for t in range(NT):
                if t >= 2:
                    pe.wait_ge(x_new[1], t - 1)
                for c in range(HC):
                    ins = mm(PS[0:P, 4 + t % 2, 0:D], gT[:, c, t * P:(t + 1) * P], W4[:, c, :], start=(c == 0), stop=(c == HC - 1))
                ins.then_inc(l0_o, 1)

            def gate_logits(k, chunks, act_of, w_of):
                n_e = FFNS[k]["experts"]
                for t in range(NT):
                    for c in range(chunks):
                        ins = mm(PS[0:P, 6, 8 * t:8 * t + n_e], act_of(c)[:, t * P:(t + 1) * P], w_of(c), start=(c == 0), stop=(c == chunks - 1))
                ins.then_inc(ff[k]["lgmm"].sem, 1)

            def gate_biases(k):
                f, n_e = ff[k], FFNS[k]["experts"]
                pe.wait_ge(*f["gate"](1))
                for t in range(NT):
                    if t >= 2:
                        pe.wait_ge(*f["gTs"](t - 1))
                    m_.transpose(PS[0:8, 6 + t % 2, 0:P], gate[:, t, :], ident[0:P, 0:P]).then_inc(f["gT"].sem, 1)
                for t in range(NT):
                    pe.wait_ge(*f["gTs"](NT))
                    if t >= 2:
                        pe.wait_ge(x_new[FFNS[k]["layer"] + 1], t - 1)
                    mm(PS[0:P, 6 + t % 2, 0:D], gateT[0:n_e, t * P:(t + 1) * P], ffb2[k][0:n_e, :], start=True, stop=True)\
                        .then_inc(f["b2mm"].sem, 1)

            def outputs(k, n, u, act_of, chunks, w_of):
                f = ff[k]
                for t in range(NT):
                    pe.wait_ge(x_new[FFNS[k]["layer"] + 1], NT * n + NT + t - 1)
                    for c in range(chunks):
                        ins = mm(PS[0:P, 4 + (5 * u + t) % 2, 0:D], act_of(c)[:, t * P:(t + 1) * P], w_of(c), start=(c == 0), stop=(c == chunks - 1))
                    ins.then_inc(f["ymm"].sem, 1)

            def ffn(k):
                f, hc = ff[k], FFNS[k]["hidden"]
                pe.wait_ge(ln_xnT, NT * (FFNS[k]["layer"] + 1))
                pe.wait_ge(ld_small, 16 * N_SMALL)
                gate_logits(k, DC, lambda c: xnT[:, c], lambda c: wg[k][:, c, :])
                gate_biases(k)
                pe.sem_inc(f["h"].sem, 2)
                with pe.Fori(0, FFNS[k]["experts"] // 2) as i:
                    for u in range(2):
                        pe.wait_ge(*f["w1a" if u == 0 else "w1b"](16 * i + 16))
                        for m in range(hc):
                            pe.wait_ge(*f["h"](hc * (2 * i + u) + m + 1))
                            for b in range(2):
                                for c in range(DC):
                                    ins = mm(PS[:, 2 * (m % 2) + b, 0:NH], w1s[:, u, c * H0 + m * 128:c * H0 + (m + 1) * 128],
                                             xnT[:, c, b * NH:(b + 1) * NH], start=(c == 0), stop=(c == DC - 1))
                            ins.then_inc(f["hmm"].sem, 1)
                    for u in range(2):
                        pe.wait_ge(*f["w2a" if u == 0 else "w2b"](16 * i + 16))
                        pe.wait_ge(*f["h"](hc * (2 * i + u + 1) + 2))
                        outputs(k, 2 * i + u, u, lambda c: hT[:, u, c], hc, lambda c: w2s[:, u, c * D:(c + 1) * D])

            layernorm_transposes(1)
            ffn("f0")

            layernorm_transposes(2)
            c1 = gc["c1"]
            pe.wait_ge(ln_xnT, NT * 3)
            pe.wait_ge(ld_wg, 16 * 8)
            for t in range(NT):
                if t >= 2:
                    pe.wait_ge(c1["hs"], t - 1)
                for c in range(DC):
                    ins = mm(PS[0:P, t % 2, 0:GH], xnT[:, c, t * P:(t + 1) * P], C1W1[:, c, :], start=(c == 0), stop=(c == DC - 1))
                ins.then_inc(c1["hmm"], 1)
            pe.wait_ge(c1["hs"], NT)
            for t in range(NT):
                if t >= 2:
                    pe.wait_ge(c1["h1"], t - 1)
                for k in range(NT):
                    ins = mm(PS[0:P, 2 + t % 2, 0:GH], AT[:, k, t * P:(t + 1) * P], hs[:, k, 0:GH], start=(k == 0), stop=(k == NT - 1))
                ins.then_inc(c1["ymm"], 1)
            pe.wait_ge(c1["h1"], NT)
            for b in range(2):
                for k in range(NT):
                    ins = mm(PS[0:GH, 4 + b, 0:NH], h1c[:, k, 0:GH], AT[:, k, b * NH:(b + 1) * NH], start=(k == 0), stop=(k == NT - 1))
            ins.then_inc(c1["a2mm"], 1)
            pe.wait_ge(c1["a2T"], 1)
            for t in range(NT):
                if t >= 2:
                    pe.wait_ge(x_new[3], t - 1)
                mm(PS[0:P, t % 2, 0:D], cT[0:GH, 0, t * P:(t + 1) * P], C1W2, start=True, stop=True).then_inc(c1["omm"], 1)

            layernorm_transposes(3)
            ffn("f1")

            layernorm_transposes(4)

            def gat(l):
                q = ga[l]
                pe.wait_ge(*((ln_xnT, NT * 5) if l == 0 else ga[0]["hT"](NT)))
                for r in range(2):
                    for t in range(NT):
                        n = NT * r + t
                        if n >= 2:
                            pe.wait_ge(*q["xev"](n - 1))
                        for c in range(DC):
                            ins = mm(PS[0:P, n % 2, 0:D], xnT[:, c, t * P:(t + 1) * P], GW[l][r][:, c, :], start=(c == 0), stop=(c == DC - 1))
                        ins.then_inc(q["xmm"].sem, 1)
                for t in range(NT):
                    pe.wait_ge(*q["exp"](HEADS * (t + 1)))
                    for k in range(NT):
                        n = NT * t + k
                        if n >= 2:
                            pe.wait_ge(*q["pt"](n - 1))
                        for h in range(HEADS):
                            ins = m_.transpose(PS[0:P, k % 2, h * P:(h + 1) * P] if True else None, ex[:, h, k * P:(k + 1) * P], ident[0:P, 0:P])
                        ins.then_inc(q["tr"].sem, 1)
                    pe.wait_ge(*q["pt"](NT * (t + 1)))
                    for h in range(HEADS):
                        for k in range(NT):
                            ins = mm(PS[0:P, 2 + t % 2, h * (HD + 1):(h + 1) * (HD + 1)], PT[:, k, h, :], xl1[:, k, h, :],
                                     start=(k == 0), stop=(k == NT - 1))
                    ins.then_inc(q["omm"].sem, 1)
                if l == 0:
                    for t in range(NT):
                        pe.wait_ge(*q["h"](t + 1))
                        if t >= 2:
                            pe.wait_ge(*q["hT"](t - 1))
                        for c in range(DC):
                            ins = m_.transpose(PS[:, 6 + t % 2, c * P:(c + 1) * P], xn[:, t, c * 128:(c + 1) * 128], ident[0:P, 0:P])
                        ins.then_inc(q["htr"].sem, 1)

            gat(0)
            gat(1)

            layernorm_transposes(5)
            f = ff["f2"]
            pe.wait_ge(ln_xnT, NT * 6)
            pe.wait_ge(*f["w1a"](16))
            for m in range(8):
                if m >= 2:
                    pe.wait_ge(*f["h"](m - 1))
                for b in range(2):
                    for c in range(DC):
                        ins = mm(PS[:, 2 * (m % 2) + b, 0:NH], w1s[:, 0, c * 1024 + m * 128:c * 1024 + (m + 1) * 128],
                                 xnT[:, c, b * NH:(b + 1) * NH], start=(c == 0), stop=(c == DC - 1))
                ins.then_inc(f["hmm"].sem, 1)
            pe.wait_ge(*f["h"](8))
            gate_logits("f2", 8, lambda c: HT8[:, c], lambda c: wg["f2"][:, c, :])
            gate_biases("f2")
            with pe.Fori(0, 4) as i:
                for u in range(2):
                    pe.wait_ge(*f["w2a" if u == 0 else "w2b"](16 * i + 16))
                    outputs("f2", 2 * i + u, u, lambda c: HT8[:, c], 8, lambda c: w2s[:, u, c * D:(c + 1) * D])

            layernorm_transposes(6)
            c3 = gc["c3"]
            for r, (src_t, ready, mm_s, ev) in enumerate(((hs, "hs", "amm", "aT"), (h1c, "h1", "a2mm", "a2T"))):
                pe.wait_ge(c3[ready], NT)
                for m in range(DC):
                    for b in range(2):
                        for k in range(NT):
                            ins = mm(PS[:, 2 * m + b, 0:NH], src_t[:, k, m * 128:(m + 1) * 128], AT[:, k, b * NH:(b + 1) * NH],
                                     start=(k == 0), stop=(k == NT - 1))
                    ins.then_inc(c3[mm_s], 1)
                pe.wait_ge(c3[ev], DC)
                for t in range(NT):
                    if t >= 2:
                        pe.wait_ge(c3["h1"] if r == 0 else x_new[7], t - 1)
                    for c in range(DC):
                        ins = mm(PS[0:P, 4 + t % 2, 0:D], cT[:, c, t * P:(t + 1) * P], C3W[r][:, c, :], start=(c == 0), stop=(c == DC - 1))
                    ins.then_inc(c3["ymm"] if r == 0 else c3["omm"], 1)

            layernorm_transposes(7)
            f = ff["f3"]
            pe.wait_ge(ln_xnT, NT * 8)
            for b in range(2):
                for c in range(DC):
                    ins = mm(PS[:, 4 + b, 0:NH], rw1[:, c, :], xnT[:, c, b * NH:(b + 1) * NH], start=(c == 0), stop=(c == DC - 1))
            ins.then_inc(f["rmm"].sem, 1)
            pe.wait_ge(*f["rh"](1))
            gate_logits("f3", 1, lambda c: rhT, lambda c: wg["f3"][:, :])
            gate_biases("f3")
            pe.sem_inc(f["h2"].sem, 2)
            with pe.Fori(0, 3) as i:
                for u in range(2):
                    n = 2 * i + u
                    pe.wait_ge(*f["w1a" if u == 0 else "w1b"](32 * i + 32))
                    for m in range(DC):
                        pe.wait_ge(*f["h2"](DC * n + m + 1))
                        for b in range(2):
                            for c in range(DC):
                                ins = mm(PS[:, 2 * m + b, 0:NH], w1s[:, u, c * D + m * 128:c * D + (m + 1) * 128],
                                         xnT[:, c, b * NH:(b + 1) * NH], start=(c == 0), stop=(c == DC - 1))
                        ins.then_inc(f["hmm"].sem, 1)
                    pe.wait_ge(*f["h"](DC * (n + 1)))
                    for m in range(DC):
                        for b in range(2):
                            for c in range(DC):
                                ins = mm(PS[:, 2 * m + b, 0:NH], w1s[:, u, 512 + c * D + m * 128:512 + c * D + (m + 1) * 128],
                                         hT[:, u, c, b * NH:(b + 1) * NH], start=(c == 0), stop=(c == DC - 1))
                        ins.then_inc(f["h2mm"].sem, 1)
                for u in range(2):
                    n = 2 * i + u
                    pe.wait_ge(*f["w2a" if u == 0 else "w2b"](16 * i + 16))
                    pe.wait_ge(*f["h2"](DC * (n + 1) + 2))
                    outputs("f3", n, u, lambda c: h2T[:, u, c], DC, lambda c: w2s[:, u, c * D:(c + 1) * D])


N_SMALL = 27


def kernel(**inputs):
    import concourse.bacc as _bacc
    from concourse import mybir as _mybir
    from concourse.bass_utils import run_bass_kernel_spmd as _run

    r = {k: np.asarray(val) for k, val in inputs.items()}

    def cols(b):
        return b.reshape(-1, 128).T

    def chunks(w_):
        e, k, m = w_.shape
        return w_.reshape(e, k // 128, 128, m).transpose(0, 2, 1, 3).reshape(e, 128, -1)

    for k in ("src", "dst"):
        r[k] = r[k].astype(np.int32).reshape(ET, P).T
    r["edge_attr_64"] = r["edge_attr_64"].reshape(ET // 2, 2 * P, ED).transpose(0, 2, 1)
    for k in ("L0_gnn_b1", "L0_gnn_b2", "L0_gnn_b4", "L0_ffn_bg", "L0_ffn_bias", "L1_gnn_b1", "L1_gnn_b2", "L1_ffn_bg",
              "L2_gnn_att0", "L2_gnn_b0", "L2_gnn_att1", "L2_gnn_b1", "L2_ffn_bg", "L3_ffn_router_b2"):
        r[k] = r[k].reshape(1, -1)
    for k in ("L0_gnn_b3", "L0_ffn_b1", "L1_ffn_b1", "L2_ffn_b1", "L3_ffn_router_b1"):
        r[k] = cols(r[k])
    for k in ("L0_ffn_W1", "L0_ffn_W2", "L1_ffn_W1", "L1_ffn_W2", "L2_ffn_Wd", "L3_ffn_expert_w1", "L3_ffn_expert_w2",
              "L3_ffn_expert_w3"):
        r[k] = chunks(r[k])
    r["L2_ffn_W1"] = chunks(r["L2_ffn_W1"][None])[0]
    r["L3_b12"] = cols(np.concatenate([r.pop("L3_ffn_expert_b1"), r.pop("L3_ffn_expert_b2")], axis=1))

    nc = _bacc.Bacc("TRN2", target_bir_lowering=False, num_devices=1)
    arrays, aps = {}, {}
    for name, arr in r.items():
        arr = np.ascontiguousarray(arr)
        arrays[f"in_{name}"] = arr
        aps[name] = nc.dram_tensor(f"in_{name}", arr.shape, _mybir.dt.from_np(arr.dtype), kind="ExternalInput").ap()
    out = nc.dram_tensor("out", (N, D), _mybir.dt.float32, kind="ExternalOutput").ap()
    build(nc, aps, out)
    res = _run(nc, [arrays], core_ids=[0])
    return res.results[0]["out"]
```

```python
from contextlib import ExitStack

import numpy as np

import concourse.bass as bass
from concourse import mybir

F32 = mybir.dt.float32
F32R = mybir.dt.float32r
BF16 = mybir.dt.bfloat16
I32 = mybir.dt.int32
U32 = mybir.dt.uint32
ALU = mybir.AluOpType
ACT = mybir.ActivationFunctionType
AX = mybir.AxisListType

N, E, D, ED, H0 = 625, 10000, 256, 64, 512
P = 125
NT, ET = N // P, E // P
NP = N + 3
NH = NP // 2
DC, HC = D // 128, H0 // 128
HEADS, HD = 4, 64
TR_BANK = (0, 1, 4, 5)
OUT_BANK = (2, 3, 6, 7, 2)
GH = 64
U = 4
EI = ET // U
LN_EPS = 1e-5
NEG = -1.0e30

FFNS = {
    "f0": dict(experts=8, hidden=4, act=ACT.Relu, layer=1),
    "f1": dict(experts=8, hidden=4, act=ACT.Gelu, layer=3),
    "f2": dict(experts=8, hidden=8, act=ACT.Gelu, layer=5),
    "f3": dict(experts=6, hidden=2, act=ACT.Relu, layer=7),
}


class Signal:

    def __init__(self, sem, base):
        self.sem, self.base = sem, base

    def __call__(self, n):
        return self.sem, self.base + n


def build(nc, a, out):
    with ExitStack() as ctx:
        def sb(name, shape, dt=F32):
            return ctx.enter_context(nc.sbuf_tensor(name, shape, dt))

        def sem(name):
            return ctx.enter_context(nc.semaphore(name))

        def dram(name, shape):
            return nc.dram_tensor(name, shape, F32).ap()

        P_tab = dram("P_tab", [N, H0])
        Q_tab = dram("Q_tab", [N, H0])
        XL_tab = [dram(f"XL_tab{l}", [N, D]) for l in range(2)]
        S_tab = dram("S_tab", [2 * N * (N + 1), HEADS])

        x = sb("x", [P, NT, D])
        xn = sb("xn", [P, NT, D])
        xnT = sb("xnT", [128, DC, NP])
        AT = sb("AT", [P, NT, NP])
        ident = sb("ident", [128, 128])
        iota = sb("iota", [128, NP])
        iota8 = iota[0:P, 0:8]
        ones = sb("ones", [128, 8])
        zrow = sb("zrow", [1, 512], BF16)
        neghalf = sb("neghalf", [P, 8])
        negfill = sb("negfill", [P, N])
        sd_i = sb("sd_i", [P, ET, 2], I32)
        pair_i = sb("pair_i", [P, ET], I32)
        srcf = sb("srcf", [P, ET])
        dstf = sb("dstf", [P, ET])
        deg = sb("deg", [P, 8])
        dinv = sb("dinv", [P, 8])
        dinv2 = sb("dinv2", [P, 8])
        indeg_row = sb("indeg_row", [1, NP])
        nw = sb("nw", [P, 4, 8])
        stats = sb("stats", [P, NT, 6])
        mv = sb("mv", [P, NT, 2])
        rstd = sb("rstd", [P, 8])
        bias_rows = sb("bias_rows", [P, 4, D])
        b1row = sb("b1row", [P, H0])
        gcnb = sb("gcnb", [P, GH])
        att = sb("att", [P, 2, D])
        b3T = sb("b3T", [128, HC])
        ffb = {"f0": sb("f0_b", [128, 8 * 4]), "f1": sb("f1_b", [128, 8 * 4]), "f2": sb("f2_b", [128, 8]),
               "f3": sb("f3_b", [128, 6 * 4]), "rt": sb("rt_b", [128, 1])}
        ffb2 = {k: sb(k + "_b2", [8, D]) for k in FFNS}
        wg = {"f0": sb("f0_wg", [128, DC, 8]), "f1": sb("f1_wg", [128, DC, 8]), "f2": sb("f2_wg", [128, 8, 8]),
              "f3": sb("f3_wg", [128, 6])}
        rw1 = sb("rw1", [128, DC, 128])
        rhT = sb("rhT", [128, NP])
        bg = sb("bg", [P, 5, 8])
        lg = sb("lg", [P, NT, 8])
        top = sb("top", [P, NT, 8])
        topi = sb("topi", [P, NT, 8], U32)
        topf = sb("topf", [P, NT, 8])
        gt = sb("gt", [P, 4, NT, 8])
        gate = sb("gate", [P, NT, 8])
        gateT = sb("gateT", [8, NP])
        with nc.sbuf_tensor("exR", [P, 2500], F32) as exR:
            pass
        ZR = sb("ZR", [P, 5060], F32R)
        hi = ZR[:, 0:U * H0].rearrange("p (s n) -> p s n", s=U)
        lo = ZR[:, U * H0:2 * U * H0].rearrange("p (s n) -> p s n", s=U)
        OHT = ZR[:, 0:2 * NT * 2 * P].rearrange("p (s k e) -> p s k e", s=2, k=NT)
        xrS = ZR[:, 2500:5060].rearrange("p (s k d) -> p s k d", s=2, k=NT)
        nodeid = sb("nodeid", [P, 8])
        eaT = sb("eaT", [ED, 2, 2 * P])
        gidx = sb("gidx", [P, 4, 4], I32)
        sidx = sb("sidx", [P, 4, 2], I32)
        s4 = sb("s4", [P, 4, 2, HEADS])
        s4self = sb("s4self", [P, NT, HEADS])
        nmax = sb("nmax", [P, NT, HEADS])
        rden = sb("rden", [P, NT, HEADS])
        xl1 = sb("xl1", [P, NT, HEADS, HD + 1])
        w1s = sb("w1s", [128, 2, 2048])
        w2s = sb("w2s", [128, 2, 2048])
        WA = sb("WA", [128, 9216])
        W1a = WA[:, 0:1024].rearrange("p (c m) -> p c m", c=DC)
        W1b = WA[:, 1024:2048].rearrange("p (c m) -> p c m", c=DC)
        W1c = WA[0:ED, 2048:2560]
        W2 = WA[:, 2560:4608].rearrange("p (c m) -> p c m", c=HC)
        W3 = WA[:, 4608:7680].rearrange("p (c m) -> p c m", c=DC + HC)
        W4 = WA[:, 7680:8704].rearrange("p (c m) -> p c m", c=HC)
        b2row = WA[0:1, 8704:9216]
        C1W1 = WA[:, 0:128].rearrange("p (c m) -> p c m", c=DC)
        C1W2 = WA[0:GH, 128:384]
        GW = [[WA[:, 512 * (1 + 2 * l + r):512 * (2 + 2 * l + r)].rearrange("p (c m) -> p c m", c=DC)
               for r in range(2)] for l in range(2)]
        C3W = [WA[:, 2560 + 512 * l:3072 + 512 * l].rearrange("p (c m) -> p c m", c=DC) for l in range(2)]
        with nc.sbuf_tensor("ZF", [128, 2512], F32R) as ZF:
            pass
        Z = sb("Z", [128, 13312])

        def z(at, dims, parts=128):
            n = int(np.prod(dims))
            v = Z[0:parts, at:at + n]
            names = "abcd"[:len(dims)]
            if len(dims) == 1:
                return v
            return v.rearrange(f"p ({' '.join(names)}) -> p {' '.join(names)}", **dict(zip(names, dims)))

        PQ = z(0, [2, NT, H0], P)
        gP = z(5120, [4, H0], P)
        gQ = z(7168, [4, H0], P)
        tsum = z(9216, [U, H0], P)
        OH = ZF[0:P, :].rearrange("p (s n) -> p s n", s=U)
        agg = z(HC * NP, [NT, H0], P)
        aggT = z(0, [HC, NP])
        msgT = z(HC * NP, [HC, NP])
        gT = z(8192, [HC, NP])
        ohS = Z[0:P, 11264:11264 + 2 * NP].bitcast(BF16).rearrange("p (s n) -> p s n", s=4)
        hT = z(0, [2, HC, NP])
        HT8 = z(0, [2 * HC, NP])
        h2T = z(2 * HC * NP, [2, DC, NP])
        hs = z(0, [NT, D], P)
        cT = z(1280, [DC, NP])
        h1c = z(2600, [NT, D], P)
        ctmp = z(3900, [NT, D], P)
        XLR = z(0, [2, NT, D], P)
        ag = z(2560, [4, 2, D], P)
        bt = z(4608, [2, 2, D], P)
        sf = z(5632, [NT, D], P)
        sf2 = z(6912, [NT, D], P)
        dstrow = z(8192, [4, 2 * P], P).bitcast(I32)
        Sd = z(0, [2, N, 2, HEADS], P)
        ex = [z(10000, [HEADS, N], P), exR.rearrange("p (h n) -> p h n", h=HEADS)]
        PT = WA[0:P, 3584:6084].rearrange("p (k h n) -> p k h n", k=NT, h=HEADS)
        v = WA[0:P, 6084:7364].rearrange("p (t d) -> p t d", t=NT)
        v2 = WA[0:P, 7364:8644].rearrange("p (t d) -> p t d", t=NT)

        PS = ctx.enter_context(nc.psum_tensor("PS", [128, 8, 512], F32))

        ld_first = [sem(f"ld_first{i}") for i in range(3)]
        ld_small = sem("ld_small")
        ld_w0 = sem("ld_w0")
        ld_wg = sem("ld_wg")
        c_iota, c_ident, c_ones, c_zero, c_half, c_neg = (sem(s) for s in ("c_iota", "c_ident", "c_ones", "c_zero", "c_half", "c_neg"))
        c_xnT = sem("c_xnT")
        s_init = sem("s_init")
        idx_f = sem("idx_f")
        pairs_ready = sem("pairs_ready")
        ln_var = sem("ln_var")
        ln_pow = sem("ln_pow")
        ln_xn = sem("ln_xn")
        ln_tr = sem("ln_tr")
        ln_xnT = sem("ln_xnT")
        x_new = [sem(f"x_new{i}") for i in range(9)]
        dch = sem("dch")
        pq_mm, p_ev, q_ev, pq_st = sem("pq_mm"), sem("p_ev"), sem("q_ev"), sem("pq_st")
        a_oh, a_mm, a_done, at_ready = sem("a_oh"), sem("a_mm"), sem("a_done"), sem("at_ready")
        deg_mm, deg_v, deg_pow, dinv_ready = sem("deg_mm"), sem("deg_v"), sem("deg_pow"), sem("dinv_ready")
        ea_ld = [sem(f"ea_ld{i}") for i in range(2)]
        g_idx = sem("g_idx")
        pool_go = sem("pool_go")
        gp_ld = [sem(f"gp_ld{i}") for i in range(4)]
        l0_free = sem("l0_free")
        l0_oh = sem("l0_oh")
        l0_e = sem("l0_e")
        l0_sum = sem("l0_sum")
        l0_pre = sem("l0_pre")
        l0_hi = sem("l0_hi")
        l0_lo = sem("l0_lo")
        l0_seg = sem("l0_seg")
        l0_acc = sem("l0_acc")
        l0_agg_act, l0_agg_dve, l0_tr = sem("l0_agg_act"), sem("l0_agg_dve"), sem("l0_tr")
        l0_aggT, l0_m, l0_msgT, l0_g, l0_gT, l0_o = (sem(s) for s in ("l0_aggT", "l0_m", "l0_msgT", "l0_g", "l0_gT", "l0_o"))
        ff, raised = {k: {} for k in FFNS}, {}
        for k, f in FFNS.items():
            n_e, hc = f["experts"], f["hidden"]
            totals = dict(w1a=8 * n_e, w1b=8 * n_e, w2a=8 * n_e, w2b=8 * n_e, lgmm=1, lgv=1, gexp=1, gate=1, gT=NT, gTs=NT, b2mm=NT,
                          hmm=hc * n_e, h=hc * n_e + 2, ymm=NT * n_e)
            if k == "f2":
                totals.update(w1a=16, w1b=0, hmm=hc, h=hc)
            if k == "f3":
                totals.update(w1a=16 * n_e, w1b=16 * n_e, lgv=2, gexp=2, h=hc * n_e, h2mm=hc * n_e, h2=hc * n_e + 2, rmm=1, rh=1)
            if k == "f1":
                totals.update(lgv=0, gexp=0)
            for n, total in totals.items():
                if n not in raised:
                    raised[n] = [sem(f"ff_{n}"), 0]
                ff[k][n] = Signal(*raised[n])
                raised[n][1] += total
        gc = {k: {s: sem(f"{k}_{s}") for s in ("hmm", "hs", "amm", "aT", "ymm", "h1", "a2mm", "a2T", "omm")}
              for k in ("c1", "c3")}
        totals = dict(xmm=2 * NT, xev=2 * NT, st=16, self=1, diag=16 * NT, gi=ET // 2, gl0=4 * ET, gl1=4 * ET, gl2=4 * ET, gl3=4 * ET,
                      dr0=2 * ET, dr1=2 * ET, dr2=2 * ET, dr3=2 * ET, xrs=1, oht=ET // 2, xg=ET // 2, lr=3 * ET // 2,
                      s4=ET // 2, si=ET // 2, scat0=8 * ET, scat1=8 * ET, sd0=32 * 3, sd1=32 * 2, mrg=NT, max=NT, exp=NT * HEADS, tr=NT * NT,
                      pt=NT * NT, omm=NT, min=1, emin=1, h=NT, htr=NT, hT=NT)
        ga_sems = {n: sem(f"ga_{n}") for n in totals}
        ga = [{n: Signal(ga_sems[n], l * total) for n, total in totals.items()} for l in range(2)]
        out_done = sem("out_done")

        block = ctx.enter_context(nc.Block())
        bg_of = {"f0": 0, "f1": 2, "f2": 3, "f3": 4}

        @block.sync
        def _(sp):
            sp.dma_start(x[:, :, :], a["x"].rearrange("(t p) d -> p t d", p=P)).then_inc(ld_first[2], 16)
            sp.dma_start(sd_i[:, :, :], a["src_dst"]).then_inc(ld_first[0], 16)
            sp.dma_start(W1a, a["L0_gnn_W1"][0:D, :].rearrange("(c p) m -> p c m", p=128)).then_inc(ld_w0, 16)
            sp.dma_start(W1b, a["L0_gnn_W1"][D:2 * D, :].rearrange("(c p) m -> p c m", p=128)).then_inc(ld_w0, 16)
            sp.dma_start(W1c, a["L0_gnn_W1"][2 * D:2 * D + ED, :]).then_inc(ld_w0, 16)
            sp.dma_start(W2, a["L0_gnn_W2"].rearrange("(c p) m -> p c m", p=128)).then_inc(ld_w0, 16)
            sp.dma_start(W3, a["L0_gnn_W3"].rearrange("(c p) m -> p c m", p=128)).then_inc(ld_w0, 16)
            sp.dma_start(W4, a["L0_gnn_W4"].rearrange("(c p) m -> p c m", p=128)).then_inc(ld_w0, 16)
            sp.dma_start(b2row, a["L0_gnn_b2"]).then_inc(ld_w0, 16)
            sp.dma_start(b1row[:, :], a["L0_gnn_b1"].to_broadcast([P, H0])).then_inc(ld_w0, 16)
            n = 0
            for dst_ap, src_ap in (
                    [(bias_rows[:, j, :], a[k].to_broadcast([P, D])) for j, k in
                     enumerate(("L0_gnn_b4", "L1_gnn_b2", "L2_gnn_b0", "L2_gnn_b1"))]
                    + [(gcnb[:, :], a["L1_gnn_b1"].to_broadcast([P, GH])), (b3T[:, :], a["L0_gnn_b3"])]
                    + [(att[:, l, :], a[f"L2_gnn_att{l}"].to_broadcast([P, D])) for l in range(2)]
                    + [(ffb[k][:, :], a[s]) for k, s in
                       (("f0", "L0_ffn_b1"), ("f1", "L1_ffn_b1"), ("f2", "L2_ffn_b1"), ("f3", "L3_b12"), ("rt", "L3_ffn_router_b1"))]
                    + [(ffb2[k][0:FFNS[k]["experts"], :], a[s]) for k, s in
                       (("f0", "L0_ffn_b2"), ("f1", "L1_ffn_b2"), ("f2", "L2_ffn_bd"), ("f3", "L3_ffn_expert_b3"))]
                    + [(wg[k][:, :, :], a[s].rearrange("(c p) e -> p c e", p=128)) for k, s in
                       (("f0", "L0_ffn_Wg"), ("f1", "L1_ffn_Wg"), ("f2", "L2_ffn_Wg"))]
                    + [(wg["f3"][:, :], a["L3_ffn_router_w2"]),
                       (rw1[:, :, :], a["L3_ffn_router_w1"].rearrange("(c p) m -> p c m", p=128))]
                    + [(bg[:, j, 0:m], a[k].to_broadcast([P, m])) for j, (k, m) in
                       enumerate((("L0_ffn_bg", 8), ("L0_ffn_bias", 8), ("L1_ffn_bg", 8), ("L2_ffn_bg", 8), ("L3_ffn_router_b2", 6)))]):
                sp.dma_start(dst_ap, src_ap).then_inc(ld_small, 16)
                n += 1
            assert n == N_SMALL
            sp.wait_ge(c_neg, 1)
            rows = S_tab[0:2 * N * N, :].rearrange("(t p s) h -> t p (s h)", t=NT, p=P)
            for t in range(NT):
                for q in range(2 * HEADS):
                    sp.dma_start(rows[t, :, q * N:(q + 1) * N], negfill[:, :]).then_inc(s_init, 16)
            for j, tab in enumerate((P_tab, Q_tab)):
                sp.wait_ge((p_ev, q_ev)[j], NT)
                sp.dma_start(tab.rearrange("(t p) m -> p t m", p=P), PQ[:, j, :, :]).then_inc(pq_st, 16)
            for h in range(2):
                sp.dma_start(eaT[:, h, :], a["edge_attr_64"][h]).then_inc(ea_ld[h], 16)
            with sp.Fori(0, EI - 1) as i:
                for h in range(2):
                    sp.wait_ge(l0_e, U * i + 2 * h + 2)
                    sp.dma_start(eaT[:, h, :], a["edge_attr_64"][bass.ds((i + 1) * 2 + h, 1)].rearrange("a p m -> (a p) m"))\
                        .then_inc(ea_ld[h], 16)

            def experts(k, w1, w2, before):
                f, n_e = ff[k], FFNS[k]["experts"]
                before()
                for u, (s1, s2) in enumerate(((f["w1a"].sem, f["w2a"].sem), (f["w1b"].sem, f["w2b"].sem))):
                    w1(0, u, s1)
                    w2(0, u, s2)
                with sp.Fori(1, n_e // 2) as i:
                    for u, (s1, s2) in enumerate(((f["w1a"].sem, f["w2a"].sem), (f["w1b"].sem, f["w2b"].sem))):
                        if w1 is not nothing:
                            sp.wait_ge(*f["hmm" if k != "f3" else "h2mm"](FFNS[k]["hidden"] * (2 * i - 2 + u + 1)))
                            w1(i, u, s1)
                        sp.wait_ge(*f["ymm"](NT * (2 * i - 2 + u + 1)))
                        w2(i, u, s2)

            def nothing(i, u, s):
                pass

            def wload(slots, cols, name):
                def load(i, u, s):
                    dst_ap = slots[:, u, 0:cols]
                    src_ap = a[name][bass.ds(2 * i + u, 1)].rearrange("e p m -> (e p) m") if not isinstance(i, int) \
                        else a[name][2 * i + u]
                    sp.dma_start(dst_ap, src_ap).then_inc(s, 16)
                return load

            experts("f0", wload(w1s, 1024, "L0_ffn_W1"), wload(w2s, 1024, "L0_ffn_W2"), lambda: None)
            sp.wait_ge(l0_o, NT)
            sp.dma_start(C1W1, a["L1_gnn_W1"].rearrange("(c p) m -> p c m", p=128)).then_inc(ld_wg, 16)
            sp.dma_start(C1W2, a["L1_gnn_W2"]).then_inc(ld_wg, 16)
            for l in range(2):
                for r, k in enumerate(("l", "r")):
                    sp.dma_start(GW[l][r], a[f"L2_gnn_W{k}{l}"].rearrange("(c p) m -> p c m", p=128)).then_inc(ld_wg, 16)
                sp.dma_start(C3W[l], a[f"L3_gnn_W{l + 1}"].rearrange("(c p) m -> p c m", p=128)).then_inc(ld_wg, 16)
            experts("f1", wload(w1s, 1024, "L1_ffn_W1"), wload(w2s, 1024, "L1_ffn_W2"),
                    lambda: sp.wait_ge(*ff["f0"]["ymm"](8 * NT)))

            def gat_tables(l):
                g = ga[l]
                sp.wait_ge(*g["xev"](NT))
                sp.dma_start(XL_tab[l].rearrange("(t p) m -> p t m", p=P), XLR[:, 0, :, :]).then_inc(g["st"].sem, 16)

                def target_rows(i):
                    for q in range(4):
                        if not isinstance(i, int):
                            sp.wait_ge(*g["oht"](4 * i + q - 3))
                        row = a["dst_row"][4 * i + q] if isinstance(i, int) else a["dst_row"][bass.ds(4 * i + q, 1)].rearrange("a o e -> (a o) e")
                        sp.dma_start(dstrow[:, q, :], row.to_broadcast([P, 2 * P])).then_inc(g[f"dr{q}"].sem, 16)

                target_rows(0)
                sp.wait_ge(*g["self"](1))
                sp.wait_ge(s_init, 16 * 2 * NT * HEADS)
                for t in range(NT):
                    diag = S_tab.rearrange("(t p r) h -> t p r h", t=NT, p=P)[t, :, 0, :]
                    sp.dma_start(diag, s4self[:, t, :]).then_inc(g["diag"].sem, 16)
                with sp.Fori(1, ET // 8) as i:
                    target_rows(i)
                for h in range(2):
                    sp.wait_ge(*g[f"scat{h}"](8 * ET))
                rows = S_tab[0:2 * N * N, :].rearrange("(t p s j) h -> t p s j h", t=NT, p=P, j=2)
                for t in range(NT):
                    if t >= 2:
                        sp.wait_ge(*g["mrg"](t - 1))
                    for h in range(2):
                        half = slice(h * (N // 2), N if h else N // 2)
                        sp.dma_start(Sd[:, t % 2, half, :, :], rows[t][:, half]).then_inc(g[f"sd{t % 2}"].sem, 16)

            gat_tables(0)
            gat_tables(1)

            def before_f2():
                sp.wait_ge(*ff["f1"]["ymm"](8 * NT))
                sp.dma_start(w1s[:, 0, :], a["L2_ffn_W1"]).then_inc(ff["f2"]["w1a"].sem, 16)

            experts("f2", nothing, wload(w2s, 2048, "L2_ffn_Wd"), before_f2)

            def before_f3():
                sp.wait_ge(*ff["f2"]["ymm"](8 * NT))

            def w12(i, u, s):
                for j in range(2):
                    name = f"L3_ffn_expert_w{j + 1}"
                    src_ap = a[name][2 * i + u] if isinstance(i, int) else \
                        a[name][bass.ds(2 * i + u, 1)].rearrange("e p m -> (e p) m")
                    sp.dma_start(w1s[:, u, 512 * j:512 * j + 512], src_ap).then_inc(s, 16)

            experts("f3", w12, wload(w2s, 512, "L3_ffn_expert_w3"), before_f3)
            sp.wait_ge(x_new[8], NT * 7)
            sp.dma_start(out.rearrange("(t p) d -> p t d", p=P), x[:, :, :]).then_inc(out_done, 16)
            sp.wait_ge(out_done, 16)
            sp.wait_ge(pq_st, 32)
            for l in range(2):
                sp.wait_ge(*ga[l]["st"](16))
                sp.wait_ge(*ga[l]["diag"](16 * NT))
                for h in range(2):
                    sp.wait_ge(*ga[l][f"scat{h}"](8 * ET))

        @block.gpsimd
        def _(pool):
            g = nc.gpsimd
            g.iota(iota[:, :], [[1, NP]], base=0, channel_multiplier=0, allow_small_or_imprecise_dtypes=True).then_inc(c_iota, 1)
            g.iota(nodeid[:, 0:NT], [[P, NT]], base=0, channel_multiplier=1, allow_small_or_imprecise_dtypes=True).then_inc(c_iota, 1)
            g.memset(ident[:, :], 0.0).then_inc(c_ident, 1)
            g.memset(ones[:, :], 1.0).then_inc(c_ones, 1)
            g.memset(xnT[:, :, N:NP], 0.0).then_inc(c_xnT, 1)
            g.memset(zrow[:, :], 0.0).then_inc(c_zero, 1)
            g.memset(neghalf[:, :], -0.5).then_inc(c_half, 1)
            g.memset(negfill[:, :], NEG).then_inc(c_neg, 1)
            g.memset(xl1[:, :, :, HD:HD + 1], 1.0).then_inc(c_ones, 1)
            pool.wait_ge(c_ident, 1)
            g.affine_select(out=ident[:, :], in_=ident[:, :], compare_op=ALU.not_equal, fill=1.0, base=0,
                            pattern=[[-1, 128]], channel_multiplier=1).then_inc(c_ident, 1)

            def layernorm_pow(i):
                pool.wait_ge(ln_var, i + 1)
                g.tensor_tensor(nw[:, 1, 0:NT], nw[:, 0, 0:NT], neghalf[:, 0:NT], ALU.pow).then_inc(ln_pow, 1)

            pool.wait_ge(c_half, 1)
            layernorm_pow(0)
            pool.wait_ge(deg_v, 1)
            g.tensor_tensor(nw[:, 1, 0:NT], deg[:, 0:NT], neghalf[:, 0:NT], ALU.pow).then_inc(deg_pow, 1)

            pool.wait_ge(ld_first[0], 16)
            pool.wait_ge(pq_st, 32)

            def gather_step(i):
                for h in range(2):
                    if not isinstance(i, int):
                        for u in (2 * h, 2 * h + 1):
                            pool.wait_ge(gp_ld[u], 32 * i)
                    g.tensor_copy(gidx[:, h, :], sd_i[:, bass.ds(U * i + 2 * h, 2), :].rearrange("p t j -> p (t j)")).then_inc(g_idx, 1)
                    pool.wait_ge(g_idx, 2 * i + h + 1)
                    for j in range(2):
                        u = 2 * h + j
                        pool.wait_ge(l0_free, U * i + u + 1)
                        pool.sem_inc(pool_go)
                        for gath, tab, c in ((gP, P_tab, 2 * j), (gQ, Q_tab, 2 * j + 1)):
                            g.indirect_dma_start(gath[:, u, :], None, tab, bass.IndirectOffsetOnAxis(ap=gidx[:, h, c:c + 1], axis=0))\
                                .then_inc(gp_ld[u], 16)

            gather_step(0)
            with pool.Fori(1, EI) as i:
                gather_step(i)
            for i in range(1, 5):
                layernorm_pow(i)

            def gat(l):
                q = ga[l]
                pool.wait_ge(*q["st"](16))

                def gather(p, k):
                    if not isinstance(p, int):
                        pool.wait_ge(*q["s4"](p - 3))
                    pool.wait_ge(*q["gi"](p + 1))
                    pool.sem_inc(pool_go)
                    for j in range(2):
                        g.indirect_dma_start(ag[:, k, j, :], None, XL_tab[l], bass.IndirectOffsetOnAxis(ap=gidx[:, k, 2 * j:2 * j + 1], axis=0))\
                            .then_inc(q[f"gl{k}"].sem, 16)

                def scatter(p, k):
                    for j in range(2):
                        if not isinstance(p, int) or p:
                            pool.wait_ge(*q[f"scat{j}"](16 * p))
                        if j == 0:
                            pool.wait_ge(*q["si"](p + 1))
                            pool.wait_ge(*q["s4"](p + 1))
                        pool.sem_inc(pool_go)
                        g.indirect_dma_start(S_tab, bass.IndirectOffsetOnAxis(ap=sidx[:, k, j:j + 1], axis=0), s4[:, k, j, :], None)\
                            .then_inc(q[f"scat{j}"].sem, 16)

                for p in range(4):
                    gather(p, p)
                    if p == 2:
                        pool.wait_ge(*q["diag"](16 * NT))
                    if p >= 2:
                        scatter(p - 2, p - 2)
                with pool.Fori(1, ET // 8) as i:
                    for k in range(4):
                        gather(4 * i + k, k)
                        scatter(4 * i + k - 2, (k - 2) % 4)
                for p in (ET // 2 - 2, ET // 2 - 1):
                    scatter(p, p % 4)

            gat(0)
            gat(1)
            for i in range(5, 8):
                layernorm_pow(i)

        @block.scalar
        def _(act):
            s = nc.scalar

            def layernorm_evac(i):
                for t in range(NT):
                    act.wait_ge(ln_tr, NT * i + t + 1)
                    s.activation(xnT[:, :, t * P:(t + 1) * P], PS[:, 6 + t % 2, 0:DC * P].rearrange("p (c n) -> p c n", c=DC),
                                 ACT.Copy).then_inc(ln_xnT, 1)

            act.wait_ge(c_xnT, 1)
            layernorm_evac(0)
            for t in range(NT):
                act.wait_ge(pq_mm, t + 1)
                s.activation(PQ[:, 0, t, :], PS[0:P, t % 4, :], ACT.Copy).then_inc(p_ev, 1)
            with act.Fori(0, EI) as i:
                for u in range(U):
                    act.wait_ge(l0_pre, U * i + u + 3)
                    act.wait_ge(l0_seg, U * i + u + 1)
                    s.activation(hi[:, u, :], tsum[:, u, :], ACT.Relu).then_inc(l0_hi, 1)
            act.wait_ge(l0_acc, 1)
            for t in range(0, NT, 2):
                s.activation(agg[:, t, :], PS[0:P, t, :], ACT.Copy).then_inc(l0_agg_act, 1)
            for t in range(NT):
                act.wait_ge(l0_tr, t + 1)
                s.activation(aggT[:, :, t * P:(t + 1) * P], PS[:, 5 + t % 2, 0:HC * P].rearrange("p (c n) -> p c n", c=HC),
                             ACT.Copy).then_inc(l0_aggT, 1)
            for dst_t, mm, ev, bias in ((msgT, l0_m, l0_msgT, None), (gT, l0_g, l0_gT, b3T)):
                if bias is not None:
                    act.wait_ge(ld_small, 16 * N_SMALL)
                for m in range(HC):
                    act.wait_ge(mm, m + 1)
                    src_ap = PS[:, 2 * (m % 2):2 * (m % 2) + 2, 0:NH]
                    dst_ap = dst_t[:, m, :].rearrange("p (b n) -> p b n", b=2)
                    if bias is None:
                        s.activation(dst_ap, src_ap, ACT.Copy).then_inc(ev, 1)
                    else:
                        s.activation(dst_ap, src_ap, ACT.Relu, bias=bias[:, m:m + 1]).then_inc(ev, 1)

            def hidden(k, dst_of, mm, ev, per, col, stride, func):
                f, n_e = ff[k], FFNS[k]["experts"]
                with act.Fori(0, n_e // 2) as i:
                    for u in range(2):
                        for m in range(per):
                            act.wait_ge(*f[mm](per * (2 * i + u) + m + 1))
                            s.activation(dst_of(u)[:, m, :].rearrange("p (b n) -> p b n", b=2),
                                         PS[:, 2 * (m % 2):2 * (m % 2) + 2, 0:NH], func,
                                         bias=ffb[k][:, bass.ds(stride * (2 * i + u) + col + m, 1)]).then_inc(f[ev].sem, 1)

            def gate_exp(k, out_ap, in_ap):
                act.wait_ge(*ff[k]["lgv"](1))
                s.activation(out_ap, in_ap, ACT.Exp).then_inc(ff[k]["gexp"].sem, 1)

            layernorm_evac(1)
            gate_exp("f0", gt[:, 0, :, 0], gt[:, 1, :, 0])
            hidden("f0", lambda u: hT[:, u], "hmm", "h", HC, 0, HC, ACT.Relu)
            layernorm_evac(2)
            c = gc["c1"]
            for t in range(NT):
                act.wait_ge(c["hmm"], t + 1)
                s.activation(hs[:, t, 0:GH], PS[0:P, t % 2, 0:GH], ACT.Copy, scale=dinv[:, t:t + 1]).then_inc(c["hs"], 1)
            act.wait_ge(c["a2mm"], 1)
            s.activation(cT[0:GH, 0, :].rearrange("p (b n) -> p b n", b=2), PS[0:GH, 4:6, 0:NH], ACT.Copy).then_inc(c["a2T"], 1)
            layernorm_evac(3)
            hidden("f1", lambda u: hT[:, u], "hmm", "h", HC, 0, HC, ACT.Gelu)

            layernorm_evac(4)

            def gat(l):
                q = ga[l]
                for t in range(NT):
                    act.wait_ge(*q["xmm"](t + 1))
                    s.activation(XLR[:, 0, t, :], PS[0:P, t % 2, 0:D], ACT.Copy).then_inc(q["xev"].sem, 1)
                for t in range(NT):
                    act.wait_ge(*q["xmm"](NT + t + 1))
                    s.activation(XLR[:, 1, t, :], PS[0:P, (NT + t) % 2, 0:D], ACT.Copy).then_inc(q["xev"].sem, 1)
                act.wait_ge(pairs_ready, 2)

                def indices(i):
                    for k in range(4):
                        p = 4 * i + k
                        if not isinstance(i, int):
                            act.wait_ge(*q[f"gl{k}"](32 * i))
                        s.activation(gidx[:, k, :], sd_i[:, bass.ds(2 * p, 2), :].rearrange("p t j -> p (t j)"), ACT.Copy)\
                            .then_inc(q["gi"].sem, 1)
                        if not isinstance(i, int):
                            for j in range(2):
                                act.wait_ge(*q[f"scat{j}"](16 * (p - 3)))
                        s.activation(sidx[:, k, :], pair_i[:, bass.ds(2 * p, 2)], ACT.Copy).then_inc(q["si"].sem, 1)

                indices(0)
                with act.Fori(1, ET // 8) as i:
                    indices(i)
                for t in range(NT):
                    act.wait_ge(*q["max"](t + 1))
                    for h in range(HEADS):
                        s.activation(ex[t % 2][:, h, :], ex[t % 2][:, h, :], ACT.Exp, bias=nmax[:, t, h:h + 1]).then_inc(q["exp"].sem, 1)
                act.wait_ge(*q["min"](1))
                s.activation(v2[:, :, :], v2[:, :, :], ACT.Exp).then_inc(q["emin"].sem, 1)
                if l == 0:
                    for t in range(NT):
                        act.wait_ge(*q["htr"](t + 1))
                        s.activation(xnT[:, :, t * P:(t + 1) * P], PS[:, 6 + t % 2, 0:DC * P].rearrange("p (c n) -> p c n", c=DC),
                                     ACT.Copy).then_inc(q["hT"].sem, 1)

            gat(0)
            gat(1)
            layernorm_evac(5)
            f = ff["f2"]
            for m in range(8):
                act.wait_ge(*f["hmm"](m + 1))
                s.activation(HT8[:, m, :].rearrange("p (b n) -> p b n", b=2), PS[:, 2 * (m % 2):2 * (m % 2) + 2, 0:NH], ACT.Gelu,
                             bias=ffb["f2"][:, m:m + 1]).then_inc(f["h"].sem, 1)
            gate_exp("f2", gt[:, 1, :, :], gt[:, 0, :, :])
            layernorm_evac(6)
            c = gc["c3"]
            for mm, ev in (("amm", "aT"), ("a2mm", "a2T")):
                for m in range(DC):
                    act.wait_ge(c[mm], m + 1)
                    s.activation(cT[:, m, :].rearrange("p (b n) -> p b n", b=2), PS[:, 2 * m:2 * m + 2, 0:NH], ACT.Copy).then_inc(c[ev], 1)
                if mm == "amm":
                    for t in range(NT):
                        act.wait_ge(c["ymm"], t + 1)
                        s.activation(h1c[:, t, :], PS[0:P, 4 + t % 2, 0:D], ACT.Relu, scale=dinv2[:, t:t + 1]).then_inc(c["h1"], 1)
            layernorm_evac(7)
            f = ff["f3"]
            act.wait_ge(*f["rmm"](1))
            s.activation(rhT[:, :].rearrange("p (b n) -> p b n", b=2), PS[:, 4:6, 0:NH], ACT.Relu, bias=ffb["rt"][:, 0:1]).then_inc(f["rh"].sem, 1)
            gate_exp("f3", gt[:, 1, :, :], gt[:, 0, :, :])
            act.wait_ge(*f["lgv"](2))
            s.activation(gt[:, 0, :, 0], gt[:, 2, :, 0], ACT.Exp).then_inc(f["gexp"].sem, 1)
            with act.Fori(0, 3) as i:
                for u in range(2):
                    for step, (mm, ev, dst_t, bank) in enumerate((("hmm", "h", hT, 0), ("h2mm", "h2", h2T, 2))):
                        for m in range(DC):
                            act.wait_ge(*f[mm](DC * (2 * i + u) + m + 1))
                            s.activation(dst_t[:, u, m, :].rearrange("p (b n) -> p b n", b=2),
                                         PS[:, 2 * (m % 2):2 * (m % 2) + 2, 0:NH], ACT.Relu,
                                         bias=ffb["f3"][:, bass.ds(4 * (2 * i + u) + 2 * step + m, 1)]).then_inc(f[ev].sem, 1)

        @block.vector
        def _(dve):
            w = nc.vector
            chain = [0]

            def link(ins):
                chain[0] += 1
                ins.then_inc(dch, 1)
                dve.wait_ge(dch, chain[0])

            def newton(ve, r0, dst):
                link(w.scalar_tensor_tensor(nw[:, 2, 0:NT], r0, -0.5, r0, ALU.mult, ALU.mult))
                link(w.tensor_tensor(nw[:, 3, 0:NT], nw[:, 2, 0:NT], ve, ALU.mult))
                return w.scalar_tensor_tensor(dst, nw[:, 3, 0:NT], 1.5, r0, ALU.add, ALU.mult)

            def layernorm(i, before):
                for t in range(NT):
                    before(t)
                    ins = w.bn_stats(stats[:, t, :], x[:, t, :])
                link(ins)
                for t in range(NT):
                    ins = w.bn_aggr(mv[:, t, :], stats[:, t, :])
                link(ins)
                w.tensor_scalar(nw[:, 0, 0:NT], mv[:, :, 1], LN_EPS, None, ALU.add).then_inc(ln_var, 1)
                dve.wait_ge(ln_pow, i + 1)
                link(newton(nw[:, 0, 0:NT], nw[:, 1, 0:NT], rstd[:, 0:NT]))
                for t in range(NT):
                    w.tensor_scalar(xn[:, t, :], x[:, t, :], mv[:, t, 0:1], rstd[:, t:t + 1], ALU.subtract, ALU.mult)\
                        .then_inc(ln_xn, 1)

            dve.wait_ge(ld_first[0], 16)
            w.tensor_copy(srcf[:, :], sd_i[:, :, 0]).then_inc(idx_f, 1)
            w.tensor_copy(dstf[:, :], sd_i[:, :, 1]).then_inc(idx_f, 1)
            dve.wait_ge(idx_f, 2)
            pairf = z(0, [2, ET // 2, 2], P)
            link(w.scalar_tensor_tensor(pairf[:, 0].rearrange("p a b -> p (a b)"), dstf[:, :], float(N), srcf[:, :], ALU.mult, ALU.add))
            for j in range(2):
                w.tensor_scalar(pair_i[:, :].rearrange("p (a b) -> p a b", b=2)[:, :, j], pairf[:, 0, :, j], 2.0, float(j), ALU.mult, ALU.add)\
                    .then_inc(pairs_ready, 1)
            dve.wait_ge(ld_first[2], 16)
            layernorm(0, lambda t: None)
            dve.wait_ge(ld_w0, 16 * 8)
            for t in range(NT):
                dve.wait_ge(pq_mm, NT + t + 1)
                w.tensor_tensor(PQ[:, 1, t, :], PS[0:P, (NT + t) % 4, :], b1row[:, :], ALU.add).then_inc(q_ev, 1)
            dve.wait_ge(c_iota, 2)
            dve.sem_inc(a_mm, 2)
            with dve.Fori(0, ET // 2) as i:
                for u in range(2):
                    dve.wait_ge(a_mm, 2 * i + u + 1)
                    w.tensor_scalar(ohS[:, 2 * u, :], iota[0:P, :], srcf[:, bass.ds(2 * i + u, 1)], None, ALU.is_equal)
                    w.tensor_scalar(ohS[:, 2 * u + 1, :], iota[0:P, :], dstf[:, bass.ds(2 * i + u, 1)], None, ALU.is_equal).then_inc(a_oh, 1)
            dve.wait_ge(a_done, 1)
            for k in range(NT):
                w.tensor_copy(AT[:, k, 0:500], PS[0:P, k, 0:500])
                ins = w.tensor_copy(AT[:, k, 500:NP], PS[0:P, 5 + k // 4, 128 * (k % 4):128 * (k % 4) + 128])
            link(ins)
            dve.wait_ge(c_ident, 2)
            for k in range(NT):
                w.tensor_tensor(AT[:, k, k * P:(k + 1) * P], AT[:, k, k * P:(k + 1) * P], ident[0:P, 0:P], ALU.add).then_inc(at_ready, 1)
            dve.wait_ge(deg_mm, 1)
            w.tensor_scalar(indeg_row[:, :].rearrange("p (b n) -> p b n", b=2), PS[0:1, 6:8, 0:NH], 1.0, None, ALU.subtract)
            w.tensor_copy(deg[:, 0:NT], PS[0:P, 5, 0:NT]).then_inc(deg_v, 1)
            dve.wait_ge(deg_pow, 1)
            link(newton(deg[:, 0:NT], nw[:, 1, 0:NT], dinv[:, 0:NT]))
            w.tensor_tensor(dinv2[:, 0:NT], dinv[:, 0:NT], dinv[:, 0:NT], ALU.mult).then_inc(dinv_ready, 1)
            dve.wait_ge(ld_small, 16 * N_SMALL)

            dve.sem_inc(l0_free, 4)
            dve.sem_inc(l0_pre, 2)
            dve.sem_inc(l0_seg, U)

            def pre(i, u):
                n = U * i + u
                dve.wait_ge(l0_seg, n + 1)
                w.tensor_scalar(OH[:, u, :], iota[0:P, :], dstf[:, bass.ds(n, 1)], None, ALU.is_equal)
                dve.wait_ge(gp_ld[u], 32 * i + 32)
                w.tensor_tensor(tsum[:, u, :], gP[:, u, :], gQ[:, u, :], ALU.add).then_inc(l0_free, 1)
                dve.wait_ge(l0_e, n + 1)
                dve.wait_ge(l0_free, n + U + 1)
                w.tensor_tensor(tsum[:, u, :], tsum[:, u, :], PS[0:P, 5 + u % 2, :], ALU.add).then_inc(l0_pre, 1)

            def low(i, u):
                dve.wait_ge(l0_hi, U * i + u + 1)
                w.scalar_tensor_tensor(lo[:, u, :], tsum[:, u, :], 0.0, hi[:, u, :].bitcast(F32), ALU.max, ALU.subtract)\
                    .then_inc(l0_lo, 1)

            dve.wait_ge(pq_st, 32)
            pre(0, 0)
            pre(0, 1)
            with dve.Fori(0, EI - 1) as i:
                for u in range(U):
                    low(i, u)
                    pre(i + (u + 2) // U, (u + 2) % U)
            for u in range(U):
                low(EI - 1, u)
                if u < 2:
                    pre(EI - 1, u + 2)
            dve.wait_ge(l0_acc, 1)
            w.memset(aggT[:, :, N:NP], 0.0).then_inc(l0_agg_dve, 1)
            for t in range(1, NT, 2):
                w.tensor_copy(agg[:, t, :], PS[0:P, t, :]).then_inc(l0_agg_dve, 1)
            for t in range(NT):
                ins = w.tensor_tensor(x[:, t, :], x[:, t, :], xn[:, t, :], ALU.add)
            link(ins)
            for t in range(NT):
                ins = w.tensor_tensor(x[:, t, :], x[:, t, :], bias_rows[:, 0, :], ALU.add)
            link(ins)
            for t in range(NT):
                dve.wait_ge(l0_o, t + 1)
                w.tensor_tensor(x[:, t, :], x[:, t, :], PS[0:P, 4 + t % 2, 0:D], ALU.add).then_inc(x_new[1], 1)

            def top2(k):
                for t in range(NT):
                    ins = w.max(top[:, t, :], lg[:, t, :])
                link(ins)
                for t in range(NT):
                    ins = w.max_index(topi[:, t, :], top[:, t, :], lg[:, t, :])
                link(ins)
                link(w.tensor_copy(topf[:, :, :], topi[:, :, :]))

            def onehot(j, dst_ap):
                for t in range(NT):
                    ins = w.tensor_scalar(dst_ap[:, t, :], iota8, topf[:, t, j:j + 1], None, ALU.is_equal)
                link(ins)

            def logits(k, biases):
                dve.wait_ge(*ff[k]["lgmm"](1))
                n_e = FFNS[k]["experts"]
                src_ap = PS[0:P, 6, 0:NT * 8].rearrange("p (t e) -> p t e", t=NT)[:, :, 0:n_e]
                for j in biases:
                    b = bg[:, j, 0:n_e].unsqueeze(1).to_broadcast([P, NT, n_e])
                    link(w.tensor_tensor(lg[:, :, 0:n_e], src_ap, b, ALU.add))
                    src_ap = lg[:, :, 0:n_e]

            def bc8(ap, n=8):
                return ap.unsqueeze(2).to_broadcast([P, NT, n])

            def residual(k):
                f = ff[k]
                for t in range(NT):
                    dve.wait_ge(*f["gT"](t + 1))
                    w.tensor_copy(gateT[0:8, t * P:(t + 1) * P], PS[0:8, 6 + t % 2, 0:P]).then_inc(f["gTs"].sem, 1)
                for t in range(NT):
                    dve.wait_ge(*f["b2mm"](t + 1))
                    w.tensor_tensor(x[:, t, :], x[:, t, :], PS[0:P, 6 + t % 2, 0:D], ALU.add)\
                        .then_inc(x_new[FFNS[k]["layer"] + 1], 1)

            def combine(k):
                f, n_e, xs = ff[k], FFNS[k]["experts"], x_new[FFNS[k]["layer"] + 1]
                with dve.Fori(0, n_e // 2) as i:
                    for u in range(2):
                        for t in range(NT):
                            n = NT * (2 * i + u) + t
                            dve.wait_ge(*f["ymm"](n + 1))
                            dve.wait_ge(xs, n + 1)
                            w.scalar_tensor_tensor(x[:, t, :], PS[0:P, 4 + (5 * u + t) % 2, 0:D], gate[:, t, bass.ds(2 * i + u, 1)],
                                                   x[:, t, :], ALU.mult, ALU.add).then_inc(xs, 1)

            def ffn_x(layer):
                n_e = {2: 8, 4: 8, 6: 8, 8: 6}[layer]
                return lambda t: dve.wait_ge(x_new[layer], NT * n_e + t + 1)

            layernorm(1, lambda t: dve.wait_ge(x_new[1], t + 1))
            logits("f0", (0, 1))
            top2("f0")
            w.tensor_tensor(gt[:, 1, :, 0], top[:, :, 1], top[:, :, 0], ALU.subtract).then_inc(ff["f0"]["lgv"].sem, 1)
            onehot(0, gt[:, 2])
            onehot(1, gt[:, 3])
            dve.wait_ge(*ff["f0"]["gexp"](1))
            link(w.tensor_scalar(gt[:, 0, :, 1], gt[:, 0, :, 0], 1.0, None, ALU.add))
            link(w.reciprocal(gt[:, 0, :, 2], gt[:, 0, :, 1]))
            link(w.tensor_tensor(gt[:, 0, :, 3], gt[:, 0, :, 0], gt[:, 0, :, 2], ALU.mult))
            link(w.tensor_tensor(gt[:, 1, :, :], gt[:, 2, :, :], bc8(gt[:, 0, :, 2]), ALU.mult))
            link(w.tensor_tensor(gt[:, 2, :, :], gt[:, 3, :, :], bc8(gt[:, 0, :, 3]), ALU.mult))
            w.tensor_tensor(gate[:, :, :], gt[:, 1, :, :], gt[:, 2, :, :], ALU.add).then_inc(ff["f0"]["gate"].sem, 1)
            residual("f0")
            combine("f0")

            layernorm(2, ffn_x(2))
            c = gc["c1"]
            for t in range(NT):
                dve.wait_ge(c["ymm"], t + 1)
                link(w.scalar_tensor_tensor(ctmp[:, t, 0:GH], PS[0:P, 2 + t % 2, 0:GH], dinv[:, t:t + 1], gcnb[:, :], ALU.mult, ALU.add))
                w.tensor_scalar(h1c[:, t, 0:GH], ctmp[:, t, 0:GH], 0.0, dinv[:, t:t + 1], ALU.max, ALU.mult).then_inc(c["h1"], 1)
            for t in range(NT):
                dve.wait_ge(c["omm"], t + 1)
                link(w.scalar_tensor_tensor(ctmp[:, t, :], PS[0:P, t % 2, 0:D], dinv[:, t:t + 1], bias_rows[:, 1, :], ALU.mult, ALU.add))
                w.scalar_tensor_tensor(x[:, t, :], ctmp[:, t, :], 0.0, x[:, t, :], ALU.max, ALU.add).then_inc(x_new[3], 1)

            layernorm(3, lambda t: dve.wait_ge(x_new[3], t + 1))
            logits("f1", (2,))
            top2("f1")
            onehot(0, gt[:, 2])
            onehot(1, gt[:, 3])
            w.tensor_tensor(gate[:, :, :], gt[:, 2, :, :], gt[:, 3, :, :], ALU.add).then_inc(ff["f1"]["gate"].sem, 1)
            residual("f1")
            combine("f1")

            layernorm(4, ffn_x(4))

            def gat(l):
                q = ga[l]
                for t in range(NT):
                    dve.wait_ge(*q["xev"](t + 1))
                    w.tensor_copy(xl1[:, t, :, 0:HD], XLR[:, 0, t, :].rearrange("p (h c) -> p h c", h=HEADS))
                dve.wait_ge(*q["xev"](2 * NT))
                link(w.tensor_tensor(sf[:, :, :], XLR[:, 0, :, :], XLR[:, 1, :, :], ALU.add))
                link(w.scalar_tensor_tensor(sf2[:, :, :], sf[:, :, :], 0.2, sf[:, :, :], ALU.mult, ALU.max))
                link(w.tensor_tensor(sf[:, :, :], sf2[:, :, :], att[:, l, :].unsqueeze(1).to_broadcast([P, NT, D]), ALU.mult))
                w.tensor_reduce(s4self[:, :, :], sf[:, :, :].rearrange("p t (h c) -> p t h c", h=HEADS), AX.X, ALU.add).then_inc(q["self"].sem, 1)
                link(w.tensor_copy(xrS[:, 0], XLR[:, 1, :, :]))
                w.tensor_tensor(xrS[:, 1], XLR[:, 1, :, :], xrS[:, 0].bitcast(F32), ALU.subtract).then_inc(q["xrs"].sem, 1)
                att_b = att[:, l, :].unsqueeze(1).to_broadcast([P, 2, D])

                def targets(i, k, tiles):
                    p = 4 * i + k
                    if 0 in tiles:
                        dve.wait_ge(*q[f"dr{k}"](16 * i + 16))
                        if not isinstance(i, int) or p >= 2:
                            dve.wait_ge(*q["xg"](p - 1))
                    for t in tiles:
                        ins = w.tensor_scalar(OHT[:, k % 2, t, :], dstrow[:, k, :], nodeid[:, t:t + 1], None, ALU.is_equal)
                    if NT - 1 in tiles:
                        ins.then_inc(q["oht"].sem, 1)

                def edges(i, k, last=False):
                    p = 4 * i + k
                    ahead = (i + (k + 2) // 4, (k + 2) % 4)
                    a_, b_ = ag[:, k, :, :], bt[:, k % 2, :, :]
                    dve.wait_ge(*q[f"gl{k}"](32 * i + 32))
                    dve.wait_ge(*q["xg"](p + 1))
                    w.tensor_tensor(a_, a_, PS[0:P, 2 + k, :].rearrange("p (j d) -> p j d", j=2), ALU.add).then_inc(q["lr"].sem, 1)
                    if not last:
                        targets(*ahead, (0, 1))
                    dve.wait_ge(*q["lr"](3 * p + 1))
                    w.scalar_tensor_tensor(b_, a_, 0.2, a_, ALU.mult, ALU.max).then_inc(q["lr"].sem, 1)
                    if not last:
                        targets(*ahead, (2,))
                    dve.wait_ge(*q["lr"](3 * p + 2))
                    w.tensor_tensor(a_, b_, att_b, ALU.mult).then_inc(q["lr"].sem, 1)
                    if not last:
                        targets(*ahead, (3, 4))
                    dve.wait_ge(*q["lr"](3 * p + 3))
                    if not isinstance(i, int) or i:
                        for j in range(2):
                            dve.wait_ge(*q[f"scat{j}"](16 * (p - 3)))
                    w.tensor_reduce(s4[:, k, :, :], a_.rearrange("p j (h c) -> p j h c", h=HEADS), AX.X, ALU.add)\
                        .then_inc(q["s4"].sem, 1)

                targets(0, 0, range(NT))
                targets(0, 1, range(NT))
                for k in range(4):
                    edges(0, k)
                with dve.Fori(1, ET // 8 - 1) as i:
                    for k in range(4):
                        edges(i, k)
                for k in range(4):
                    edges(ET // 8 - 1, k, last=k >= 2)
                def tmax(t):
                    dve.wait_ge(*q[f"sd{t % 2}"](32 * (t // 2 + 1)))
                    if t >= 2:
                        dve.wait_ge(*q["tr"](NT * (t - 1)))
                    w.tensor_tensor(ex[t % 2].rearrange("p h s -> p s h"), Sd[:, t % 2, :, 0, :], Sd[:, t % 2, :, 1, :], ALU.max)\
                        .then_inc(q["mrg"].sem, 1)
                    dve.wait_ge(*q["mrg"](t + 1))
                    w.tensor_reduce(nmax[:, t, :], ex[t % 2], AX.X, ALU.max, negate=True).then_inc(q["max"].sem, 1)

                def finish(t):
                    dve.wait_ge(*q["omm"](t + 1))
                    po = PS[0:P, OUT_BANK[t], 0:HEADS * (HD + 1)].rearrange("p (h c) -> p h c", h=HEADS)
                    link(w.tensor_scalar(rden[:, t, :], po[:, :, HD], 1e-16, None, ALU.add))
                    link(w.reciprocal(rden[:, t, :], rden[:, t, :]))
                    link(w.tensor_tensor(v[:, t, :].rearrange("p (h c) -> p h c", h=HEADS), po[:, :, 0:HD],
                                         rden[:, t, :].unsqueeze(2).to_broadcast([P, HEADS, HD]), ALU.mult))

                tmax(0)
                tmax(1)
                for t in range(NT):
                    for k in range(NT):
                        dve.wait_ge(*q["tr"](NT * t + k + 1))
                        if k == 0 and t:
                            dve.wait_ge(*q["omm"](t))
                        w.tensor_tensor(PT[:, k, :, :], PS[0:P, TR_BANK[(NT * t + k) % 4], 0:HEADS * P].rearrange("p (h n) -> p h n", h=HEADS),
                                        AT[:, k, t * P:(t + 1) * P].unsqueeze(1).to_broadcast([P, HEADS, P]), ALU.mult)\
                            .then_inc(q["pt"].sem, 1)
                    if t + 2 < NT:
                        tmax(t + 2)
                    if t:
                        finish(t - 1)
                finish(NT - 1)
                link(w.tensor_tensor(v[:, :, :], v[:, :, :], bias_rows[:, 2 + l, :].unsqueeze(1).to_broadcast([P, NT, D]), ALU.add))
                w.tensor_scalar(v2[:, :, :], v[:, :, :], 0.0, None, ALU.min).then_inc(q["min"].sem, 1)
                dve.wait_ge(*q["emin"](1))
                link(w.scalar_tensor_tensor(v[:, :, :], v[:, :, :], 0.0, v2[:, :, :], ALU.max, ALU.add))
                for t in range(NT):
                    if l == 0:
                        w.tensor_scalar(xn[:, t, :], v[:, t, :], -1.0, None, ALU.add).then_inc(q["h"].sem, 1)
                    else:
                        w.scalar_tensor_tensor(x[:, t, :], v[:, t, :], -1.0, x[:, t, :], ALU.add, ALU.add).then_inc(x_new[5], 1)

            gat(0)
            gat(1)

            def softmax8(k, n_e):
                for t in range(NT):
                    ins = w.tensor_reduce(gt[:, 2, t, 0:1], lg[:, t, 0:n_e], AX.X, ALU.max)
                link(ins)
                w.tensor_tensor(gt[:, 0, :, 0:n_e], lg[:, :, 0:n_e], bc8(gt[:, 2, :, 0], n_e), ALU.subtract).then_inc(ff[k]["lgv"].sem, 1)
                dve.wait_ge(*ff[k]["gexp"](1))
                link(w.tensor_reduce(gt[:, 2, :, 1], gt[:, 1, :, 0:n_e], AX.X, ALU.add))
                link(w.reciprocal(gt[:, 2, :, 2], gt[:, 2, :, 1]))
                link(w.tensor_tensor(lg[:, :, 0:n_e], gt[:, 1, :, 0:n_e], bc8(gt[:, 2, :, 2], n_e), ALU.mult))

            layernorm(5, lambda t: dve.wait_ge(x_new[5], t + 1))
            logits("f2", (3,))
            softmax8("f2", 8)
            top2("f2")
            onehot(0, gt[:, 2])
            w.tensor_tensor(gate[:, :, :], gt[:, 2, :, :], bc8(top[:, :, 0]), ALU.mult).then_inc(ff["f2"]["gate"].sem, 1)
            residual("f2")
            combine("f2")

            layernorm(6, ffn_x(6))
            c = gc["c3"]
            for t in range(NT):
                dve.wait_ge(ln_xn, NT * 6 + t + 1)
                w.tensor_scalar(hs[:, t, :], xn[:, t, :], dinv[:, t:t + 1], None, ALU.mult).then_inc(c["hs"], 1)
            for t in range(NT):
                dve.wait_ge(c["omm"], t + 1)
                w.scalar_tensor_tensor(x[:, t, :], PS[0:P, 4 + t % 2, 0:D], dinv[:, t:t + 1], x[:, t, :], ALU.mult, ALU.add)\
                    .then_inc(x_new[7], 1)

            layernorm(7, lambda t: dve.wait_ge(x_new[7], t + 1))
            link(w.memset(lg[:, :, 6:8], -1.0))
            logits("f3", (4,))
            softmax8("f3", 6)
            top2("f3")
            w.tensor_tensor(gt[:, 2, :, 0], top[:, :, 1], top[:, :, 0], ALU.subtract).then_inc(ff["f3"]["lgv"].sem, 1)
            dve.wait_ge(*ff["f3"]["gexp"](2))
            link(w.tensor_scalar(gt[:, 0, :, 1], gt[:, 0, :, 0], 1.0, None, ALU.add))
            link(w.reciprocal(gt[:, 0, :, 2], gt[:, 0, :, 1]))
            link(w.tensor_tensor(gt[:, 0, :, 3], gt[:, 0, :, 0], gt[:, 0, :, 2], ALU.mult))
            onehot(0, gt[:, 2])
            onehot(1, gt[:, 3])
            link(w.tensor_tensor(gt[:, 1, :, :], gt[:, 2, :, :], bc8(gt[:, 0, :, 2]), ALU.mult))
            link(w.tensor_tensor(gt[:, 2, :, :], gt[:, 3, :, :], bc8(gt[:, 0, :, 3]), ALU.mult))
            w.tensor_tensor(gate[:, :, :], gt[:, 1, :, :], gt[:, 2, :, :], ALU.add).then_inc(ff["f3"]["gate"].sem, 1)
            residual("f3")
            combine("f3")

        @block.tensor
        def _(pe):
            m_ = nc.tensor

            def mm(*args, **kw):
                return m_.matmul(*args, skip_group_check=True, **kw)

            def layernorm_transposes(i):
                for t in range(NT):
                    pe.wait_ge(ln_xn, NT * i + t + 1)
                    if t >= 2:
                        pe.wait_ge(ln_xnT, NT * i + t - 1)
                    for c in range(DC):
                        ins = m_.transpose(PS[:, 6 + t % 2, c * P:(c + 1) * P], xn[:, t, c * 128:(c + 1) * 128], ident[0:P, 0:P])
                    ins.then_inc(ln_tr, 1)

            pe.wait_ge(c_ident, 2)
            layernorm_transposes(0)
            pe.wait_ge(ld_w0, 16 * 8)
            pe.wait_ge(ln_xnT, NT)
            for j, wt in enumerate((W1a, W1b)):
                for t in range(NT):
                    n = NT * j + t
                    if n >= 4:
                        pe.wait_ge(p_ev if n - 3 <= NT else q_ev, n - 3 if n - 3 <= NT else n - 3 - NT)
                    for c in range(DC):
                        ins = mm(PS[0:P, n % 4, :], xnT[:, c, t * P:(t + 1) * P], wt[:, c, :], start=(c == 0), stop=(c == DC - 1))
                    ins.then_inc(pq_mm, 1)
            pe.wait_ge(c_zero, 1)
            pe.wait_ge(q_ev, NT)
            for b in range(7):
                mm(PS[0:P, b, :], zrow[:, 0:P], zrow[:, :], start=True, stop=False)
            with pe.Fori(0, ET // 2) as i:
                for u in range(2):
                    pe.wait_ge(a_oh, 2 * i + u + 1)
                    for k in range(NT):
                        wt = ohS[:, 2 * u, k * P:(k + 1) * P]
                        mm(PS[0:P, k, 0:500], wt, ohS[:, 2 * u + 1, 0:500], start=False, stop=False)
                        ins = mm(PS[0:P, 5 + k // 4, 128 * (k % 4):128 * (k % 4) + 128], wt, ohS[:, 2 * u + 1, 500:NP],
                                 start=False, stop=False)
                    ins.then_inc(a_mm, 1)
            for b in range(7):
                ins = mm(PS[0:P, b, :], zrow[:, 0:P], zrow[:, :], start=False, stop=True)
            ins.then_inc(a_done, 1)
            pe.wait_ge(at_ready, NT)
            for t in range(NT):
                for k in range(NT):
                    mm(PS[0:P, 5, t:t + 1], AT[:, k, t * P:(t + 1) * P], ones[0:P, 0:1], start=(k == 0), stop=(k == NT - 1))
            for b in range(2):
                for k in range(NT):
                    ins = mm(PS[0:1, 6 + b, 0:NH], ones[0:P, 0:1], AT[:, k, b * NH:(b + 1) * NH], start=(k == 0), stop=(k == NT - 1))
            ins.then_inc(deg_mm, 1)

            for b in range(NT):
                mm(PS[0:P, b, :], zrow[:, 0:P], zrow[:, :], start=True, stop=False)

            def edge(i, u):
                if u % 2 == 0:
                    pe.wait_ge(ea_ld[u // 2], 16 * i + 16)
                pe.wait_ge(l0_pre, U * i + u + 1)
                mm(PS[0:P, 5 + u % 2, :], eaT[:, u // 2, (u % 2) * P:(u % 2 + 1) * P], W1c, start=True, stop=True).then_inc(l0_e, 1)

            def segments(i, u):
                pe.wait_ge(l0_lo, U * i + u + 1)
                for t in range(NT):
                    for part in (hi, lo):
                        ins = mm(PS[0:P, t, :], OH[:, u, t * P:(t + 1) * P], part[:, u, :], start=False, stop=False)
                ins.then_inc(l0_seg, 1)

            edge(0, 0)
            edge(0, 1)
            with pe.Fori(0, EI - 1) as i:
                for u in range(U):
                    edge(i + (u + 2) // U, (u + 2) % U)
                    segments(i, u)
            for u in range(U):
                if u < 2:
                    edge(EI - 1, u + 2)
                segments(EI - 1, u)
            for b in range(NT):
                ins = mm(PS[0:P, b, :], zrow[:, 0:P], zrow[:, :], start=False, stop=True)
            ins.then_inc(l0_acc, 1)
            pe.wait_ge(l0_agg_dve, NT // 2 + 1)
            for t in range(NT):
                pe.wait_ge(l0_agg_act, t // 2 + 1)
                if t >= 2:
                    pe.wait_ge(l0_aggT, t - 1)
                for c in range(HC):
                    ins = m_.transpose(PS[:, 5 + t % 2, c * P:(c + 1) * P], agg[:, t, c * 128:(c + 1) * 128], ident[0:P, 0:P])
                ins.then_inc(l0_tr, 1)
            pe.wait_ge(l0_aggT, NT)
            for m in range(HC):
                if m >= 2:
                    pe.wait_ge(l0_msgT, m - 1)
                for b in range(2):
                    for c in range(HC):
                        mm(PS[:, 2 * (m % 2) + b, 0:NH], W2[:, c, m * 128:(m + 1) * 128], aggT[:, c, b * NH:(b + 1) * NH],
                           start=(c == 0), stop=False)
                    ins = mm(PS[:, 2 * (m % 2) + b, 0:NH], b2row[:, m * 128:(m + 1) * 128], indeg_row[:, b * NH:(b + 1) * NH],
                             start=False, stop=True)
                ins.then_inc(l0_m, 1)
            for m in range(HC):
                pe.wait_ge(l0_msgT, HC)
                if m >= 2:
                    pe.wait_ge(l0_gT, m - 1)
                for b in range(2):
                    for c in range(DC + HC):
                        rhs = xnT[:, c, b * NH:(b + 1) * NH] if c < DC else msgT[:, c - DC, b * NH:(b + 1) * NH]
                        ins = mm(PS[:, 2 * (m % 2) + b, 0:NH], W3[:, c, m * 128:(m + 1) * 128], rhs, start=(c == 0), stop=(c == DC + HC - 1))
                ins.then_inc(l0_g, 1)
            pe.wait_ge(l0_gT, HC)
            for t in range(NT):
                if t >= 2:
                    pe.wait_ge(x_new[1], t - 1)
                for c in range(HC):
                    ins = mm(PS[0:P, 4 + t % 2, 0:D], gT[:, c, t * P:(t + 1) * P], W4[:, c, :], start=(c == 0), stop=(c == HC - 1))
                ins.then_inc(l0_o, 1)

            def gate_logits(k, chunks, act_of, w_of):
                n_e = FFNS[k]["experts"]
                for t in range(NT):
                    for c in range(chunks):
                        ins = mm(PS[0:P, 6, 8 * t:8 * t + n_e], act_of(c)[:, t * P:(t + 1) * P], w_of(c), start=(c == 0), stop=(c == chunks - 1))
                ins.then_inc(ff[k]["lgmm"].sem, 1)

            def gate_biases(k):
                f, n_e = ff[k], FFNS[k]["experts"]
                pe.wait_ge(*f["gate"](1))
                for t in range(NT):
                    if t >= 2:
                        pe.wait_ge(*f["gTs"](t - 1))
                    m_.transpose(PS[0:8, 6 + t % 2, 0:P], gate[:, t, :], ident[0:P, 0:P]).then_inc(f["gT"].sem, 1)
                for t in range(NT):
                    pe.wait_ge(*f["gTs"](NT))
                    if t >= 2:
                        pe.wait_ge(x_new[FFNS[k]["layer"] + 1], t - 1)
                    mm(PS[0:P, 6 + t % 2, 0:D], gateT[0:n_e, t * P:(t + 1) * P], ffb2[k][0:n_e, :], start=True, stop=True)\
                        .then_inc(f["b2mm"].sem, 1)

            def outputs(k, n, u, act_of, chunks, w_of):
                f = ff[k]
                for t in range(NT):
                    pe.wait_ge(x_new[FFNS[k]["layer"] + 1], NT * n + NT + t - 1)
                    for c in range(chunks):
                        ins = mm(PS[0:P, 4 + (5 * u + t) % 2, 0:D], act_of(c)[:, t * P:(t + 1) * P], w_of(c), start=(c == 0), stop=(c == chunks - 1))
                    ins.then_inc(f["ymm"].sem, 1)

            def ffn(k):
                f, hc = ff[k], FFNS[k]["hidden"]
                pe.wait_ge(ln_xnT, NT * (FFNS[k]["layer"] + 1))
                pe.wait_ge(ld_small, 16 * N_SMALL)
                gate_logits(k, DC, lambda c: xnT[:, c], lambda c: wg[k][:, c, :])
                gate_biases(k)
                pe.sem_inc(f["h"].sem, 2)
                with pe.Fori(0, FFNS[k]["experts"] // 2) as i:
                    for u in range(2):
                        pe.wait_ge(*f["w1a" if u == 0 else "w1b"](16 * i + 16))
                        for m in range(hc):
                            pe.wait_ge(*f["h"](hc * (2 * i + u) + m + 1))
                            for b in range(2):
                                for c in range(DC):
                                    ins = mm(PS[:, 2 * (m % 2) + b, 0:NH], w1s[:, u, c * H0 + m * 128:c * H0 + (m + 1) * 128],
                                             xnT[:, c, b * NH:(b + 1) * NH], start=(c == 0), stop=(c == DC - 1))
                            ins.then_inc(f["hmm"].sem, 1)
                    for u in range(2):
                        pe.wait_ge(*f["w2a" if u == 0 else "w2b"](16 * i + 16))
                        pe.wait_ge(*f["h"](hc * (2 * i + u + 1) + 2))
                        outputs(k, 2 * i + u, u, lambda c: hT[:, u, c], hc, lambda c: w2s[:, u, c * D:(c + 1) * D])

            layernorm_transposes(1)
            ffn("f0")

            layernorm_transposes(2)
            c1 = gc["c1"]
            pe.wait_ge(ln_xnT, NT * 3)
            pe.wait_ge(ld_wg, 16 * 8)
            for t in range(NT):
                if t >= 2:
                    pe.wait_ge(c1["hs"], t - 1)
                for c in range(DC):
                    ins = mm(PS[0:P, t % 2, 0:GH], xnT[:, c, t * P:(t + 1) * P], C1W1[:, c, :], start=(c == 0), stop=(c == DC - 1))
                ins.then_inc(c1["hmm"], 1)
            pe.wait_ge(c1["hs"], NT)
            for t in range(NT):
                if t >= 2:
                    pe.wait_ge(c1["h1"], t - 1)
                for k in range(NT):
                    ins = mm(PS[0:P, 2 + t % 2, 0:GH], AT[:, k, t * P:(t + 1) * P], hs[:, k, 0:GH], start=(k == 0), stop=(k == NT - 1))
                ins.then_inc(c1["ymm"], 1)
            pe.wait_ge(c1["h1"], NT)
            for b in range(2):
                for k in range(NT):
                    ins = mm(PS[0:GH, 4 + b, 0:NH], h1c[:, k, 0:GH], AT[:, k, b * NH:(b + 1) * NH], start=(k == 0), stop=(k == NT - 1))
            ins.then_inc(c1["a2mm"], 1)
            pe.wait_ge(c1["a2T"], 1)
            for t in range(NT):
                if t >= 2:
                    pe.wait_ge(x_new[3], t - 1)
                mm(PS[0:P, t % 2, 0:D], cT[0:GH, 0, t * P:(t + 1) * P], C1W2, start=True, stop=True).then_inc(c1["omm"], 1)

            layernorm_transposes(3)
            ffn("f1")

            layernorm_transposes(4)

            def gat(l):
                q = ga[l]
                pe.wait_ge(*((ln_xnT, NT * 5) if l == 0 else ga[0]["hT"](NT)))
                for r in range(2):
                    for t in range(NT):
                        n = NT * r + t
                        if n >= 2:
                            pe.wait_ge(*q["xev"](n - 1))
                        for c in range(DC):
                            ins = mm(PS[0:P, n % 2, 0:D], xnT[:, c, t * P:(t + 1) * P], GW[l][r][:, c, :], start=(c == 0), stop=(c == DC - 1))
                        ins.then_inc(q["xmm"].sem, 1)
                pe.wait_ge(*q["xrs"](1))

                def xr_step(i):
                    for u in range(4):
                        pe.wait_ge(*q["oht"](4 * i + u + 1))
                        if not isinstance(i, int):
                            pe.wait_ge(*q["s4"](4 * i + u - 3))
                        for j in range(2):
                            for k in range(NT):
                                for part in range(2):
                                    ins = mm(PS[0:P, 2 + u, j * D:(j + 1) * D], OHT[:, u % 2, k, j * P:(j + 1) * P], xrS[:, part, k, :],
                                             start=(k + part == 0), stop=(k + part == NT))
                        ins.then_inc(q["xg"].sem, 1)

                xr_step(0)
                with pe.Fori(1, ET // 8) as i:
                    xr_step(i)
                for t in range(NT):
                    pe.wait_ge(*q["exp"](HEADS * (t + 1)))
                    for k in range(NT):
                        n = NT * t + k
                        if n >= 4:
                            pe.wait_ge(*q["pt"](n - 3))
                        for h in range(HEADS):
                            ins = m_.transpose(PS[0:P, TR_BANK[n % 4], h * P:(h + 1) * P], ex[t % 2][:, h, k * P:(k + 1) * P], ident[0:P, 0:P])
                        ins.then_inc(q["tr"].sem, 1)
                    pe.wait_ge(*q["pt"](NT * (t + 1)))
                    for h in range(HEADS):
                        for k in range(NT):
                            ins = mm(PS[0:P, OUT_BANK[t], h * (HD + 1):(h + 1) * (HD + 1)], PT[:, k, h, :], xl1[:, k, h, :],
                                     start=(k == 0), stop=(k == NT - 1))
                    ins.then_inc(q["omm"].sem, 1)
                if l == 0:
                    for t in range(NT):
                        pe.wait_ge(*q["h"](t + 1))
                        if t >= 2:
                            pe.wait_ge(*q["hT"](t - 1))
                        for c in range(DC):
                            ins = m_.transpose(PS[:, 6 + t % 2, c * P:(c + 1) * P], xn[:, t, c * 128:(c + 1) * 128], ident[0:P, 0:P])
                        ins.then_inc(q["htr"].sem, 1)

            gat(0)
            gat(1)

            layernorm_transposes(5)
            f = ff["f2"]
            pe.wait_ge(ln_xnT, NT * 6)
            pe.wait_ge(*f["w1a"](16))
            for m in range(8):
                if m >= 2:
                    pe.wait_ge(*f["h"](m - 1))
                for b in range(2):
                    for c in range(DC):
                        ins = mm(PS[:, 2 * (m % 2) + b, 0:NH], w1s[:, 0, c * 1024 + m * 128:c * 1024 + (m + 1) * 128],
                                 xnT[:, c, b * NH:(b + 1) * NH], start=(c == 0), stop=(c == DC - 1))
                ins.then_inc(f["hmm"].sem, 1)
            pe.wait_ge(*f["h"](8))
            gate_logits("f2", 8, lambda c: HT8[:, c], lambda c: wg["f2"][:, c, :])
            gate_biases("f2")
            with pe.Fori(0, 4) as i:
                for u in range(2):
                    pe.wait_ge(*f["w2a" if u == 0 else "w2b"](16 * i + 16))
                    outputs("f2", 2 * i + u, u, lambda c: HT8[:, c], 8, lambda c: w2s[:, u, c * D:(c + 1) * D])

            layernorm_transposes(6)
            c3 = gc["c3"]
            for r, (src_t, ready, mm_s, ev) in enumerate(((hs, "hs", "amm", "aT"), (h1c, "h1", "a2mm", "a2T"))):
                pe.wait_ge(c3[ready], NT)
                for m in range(DC):
                    for b in range(2):
                        for k in range(NT):
                            ins = mm(PS[:, 2 * m + b, 0:NH], src_t[:, k, m * 128:(m + 1) * 128], AT[:, k, b * NH:(b + 1) * NH],
                                     start=(k == 0), stop=(k == NT - 1))
                    ins.then_inc(c3[mm_s], 1)
                pe.wait_ge(c3[ev], DC)
                for t in range(NT):
                    if t >= 2:
                        pe.wait_ge(c3["h1"] if r == 0 else x_new[7], t - 1)
                    for c in range(DC):
                        ins = mm(PS[0:P, 4 + t % 2, 0:D], cT[:, c, t * P:(t + 1) * P], C3W[r][:, c, :], start=(c == 0), stop=(c == DC - 1))
                    ins.then_inc(c3["ymm"] if r == 0 else c3["omm"], 1)

            layernorm_transposes(7)
            f = ff["f3"]
            pe.wait_ge(ln_xnT, NT * 8)
            for b in range(2):
                for c in range(DC):
                    ins = mm(PS[:, 4 + b, 0:NH], rw1[:, c, :], xnT[:, c, b * NH:(b + 1) * NH], start=(c == 0), stop=(c == DC - 1))
            ins.then_inc(f["rmm"].sem, 1)
            pe.wait_ge(*f["rh"](1))
            gate_logits("f3", 1, lambda c: rhT, lambda c: wg["f3"][:, :])
            gate_biases("f3")
            pe.sem_inc(f["h2"].sem, 2)
            with pe.Fori(0, 3) as i:
                for u in range(2):
                    n = 2 * i + u
                    pe.wait_ge(*f["w1a" if u == 0 else "w1b"](32 * i + 32))
                    for m in range(DC):
                        pe.wait_ge(*f["h2"](DC * n + m + 1))
                        for b in range(2):
                            for c in range(DC):
                                ins = mm(PS[:, 2 * m + b, 0:NH], w1s[:, u, c * D + m * 128:c * D + (m + 1) * 128],
                                         xnT[:, c, b * NH:(b + 1) * NH], start=(c == 0), stop=(c == DC - 1))
                        ins.then_inc(f["hmm"].sem, 1)
                    pe.wait_ge(*f["h"](DC * (n + 1)))
                    for m in range(DC):
                        for b in range(2):
                            for c in range(DC):
                                ins = mm(PS[:, 2 * m + b, 0:NH], w1s[:, u, 512 + c * D + m * 128:512 + c * D + (m + 1) * 128],
                                         hT[:, u, c, b * NH:(b + 1) * NH], start=(c == 0), stop=(c == DC - 1))
                        ins.then_inc(f["h2mm"].sem, 1)
                for u in range(2):
                    n = 2 * i + u
                    pe.wait_ge(*f["w2a" if u == 0 else "w2b"](16 * i + 16))
                    pe.wait_ge(*f["h2"](DC * (n + 1) + 2))
                    outputs("f3", n, u, lambda c: h2T[:, u, c], DC, lambda c: w2s[:, u, c * D:(c + 1) * D])


N_SMALL = 27


def kernel(**inputs):
    import concourse.bacc as _bacc
    from concourse import mybir as _mybir
    from concourse.bass_utils import run_bass_kernel_spmd as _run

    r = {k: np.asarray(val) for k, val in inputs.items()}

    def cols(b):
        return b.reshape(-1, 128).T

    def chunks(w_):
        e, k, m = w_.shape
        return w_.reshape(e, k // 128, 128, m).transpose(0, 2, 1, 3).reshape(e, 128, -1)

    src, dst = r.pop("src"), r.pop("dst")
    r["src_dst"] = np.stack([src, dst], axis=1).reshape(ET, P, 2).transpose(1, 0, 2)
    r["dst_row"] = dst.reshape(ET // 2, 1, 2 * P)
    r["edge_attr_64"] = r["edge_attr_64"].reshape(ET // 2, 2 * P, ED).transpose(0, 2, 1)
    for k in ("L0_gnn_b1", "L0_gnn_b2", "L0_gnn_b4", "L0_ffn_bg", "L0_ffn_bias", "L1_gnn_b1", "L1_gnn_b2", "L1_ffn_bg",
              "L2_gnn_att0", "L2_gnn_b0", "L2_gnn_att1", "L2_gnn_b1", "L2_ffn_bg", "L3_ffn_router_b2"):
        r[k] = r[k].reshape(1, -1)
    for k in ("L0_gnn_b3", "L0_ffn_b1", "L1_ffn_b1", "L2_ffn_b1", "L3_ffn_router_b1"):
        r[k] = cols(r[k])
    for k in ("L0_ffn_W1", "L0_ffn_W2", "L1_ffn_W1", "L1_ffn_W2", "L2_ffn_Wd", "L3_ffn_expert_w1", "L3_ffn_expert_w2",
              "L3_ffn_expert_w3"):
        r[k] = chunks(r[k])
    r["L2_ffn_W1"] = chunks(r["L2_ffn_W1"][None])[0]
    r["L3_b12"] = cols(np.concatenate([r.pop("L3_ffn_expert_b1"), r.pop("L3_ffn_expert_b2")], axis=1))

    nc = _bacc.Bacc("TRN2", target_bir_lowering=False, num_devices=1)
    arrays, aps = {}, {}
    for name, arr in r.items():
        arr = np.ascontiguousarray(arr)
        arrays[f"in_{name}"] = arr
        aps[name] = nc.dram_tensor(f"in_{name}", arr.shape, _mybir.dt.from_np(arr.dtype), kind="ExternalInput").ap()
    out = nc.dram_tensor("out", (N, D), _mybir.dt.float32, kind="ExternalOutput").ap()
    build(nc, aps, out)
    res = _run(nc, [arrays], core_ids=[0])
    return res.results[0]["out"]
```

```python
from contextlib import ExitStack

import numpy as np

import concourse.bass as bass
from concourse import mybir

F32 = mybir.dt.float32
F32R = mybir.dt.float32r
BF16 = mybir.dt.bfloat16
I32 = mybir.dt.int32
U32 = mybir.dt.uint32
ALU = mybir.AluOpType
ACT = mybir.ActivationFunctionType
AX = mybir.AxisListType

N, E, D, ED, H0 = 625, 10000, 256, 64, 512
P = 125
NT, ET = N // P, E // P
NP = N + 3
NH = NP // 2
DC, HC = D // 128, H0 // 128
HEADS, HD = 4, 64
TR_BANK = (0, 1, 4, 5)
OUT_BANK = (2, 3, 6, 7, 2)
GH = 64
U = 4
GATHERED = (0, 1, 2)
EI = ET // U
PQ_FROM = 6
LN_EPS = 1e-5
NEG = -1.0e30

FIRST = {"f0": ("L0_ffn_W1",), "f1": ("L1_ffn_W1",), "f3": ("L3_ffn_expert_w1", "L3_ffn_expert_w2")}
LAST = {"f0": "L0_ffn_W2", "f1": "L1_ffn_W2", "f2": "L2_ffn_Wd", "f3": "L3_ffn_expert_w3"}
FFNS = {
    "f0": dict(experts=8, hidden=4, act=ACT.Relu, layer=1),
    "f1": dict(experts=8, hidden=4, act=ACT.Gelu, layer=3),
    "f2": dict(experts=8, hidden=8, act=ACT.Gelu, layer=5),
    "f3": dict(experts=6, hidden=2, act=ACT.Relu, layer=7),
}


FQ = 8


def hidden_chunk(k, c):
    if k == "f3":
        return (c // 2) % 2, c // 4, c % 2
    return c // HC, 0, c % HC


def output_chunks(k, u):
    if k == "f2":
        return range(FQ)
    if k == "f3":
        return range(4 + 2 * u, 6 + 2 * u)
    return range(HC * u, HC * (u + 1))


def slot(k, u):
    return 1 - u if k == "f2" else u


def y_bank(k, u, t):
    return t if k == "f2" else 4 + (NT * u + t) % 2


class Signal:

    def __init__(self, sem, base):
        self.sem, self.base = sem, base

    def __call__(self, n):
        return self.sem, self.base + n


def build(nc, a, out):
    with ExitStack() as ctx:
        def sb(name, shape, dt=F32):
            return ctx.enter_context(nc.sbuf_tensor(name, shape, dt))

        def sem(name):
            return ctx.enter_context(nc.semaphore(name))

        def dram(name, shape):
            return nc.dram_tensor(name, shape, F32).ap()

        P_tab = dram("P_tab", [N, H0])
        Q_tab = dram("Q_tab", [N, H0])
        XL_tab = [dram(f"XL_tab{l}", [N, D]) for l in range(2)]
        S_tab = dram("S_tab", [2 * N * (N + 1), HEADS])

        x = sb("x", [P, NT, D])
        xn = sb("xn", [P, NT, D])
        xnT = sb("xnT", [128, DC, NP])
        AT = sb("AT", [P, NT, NP])
        ident = sb("ident", [128, 128])
        iota = sb("iota", [128, NP])
        iota8 = iota[0:P, 0:8]
        ones = sb("ones", [128, 8])
        zrow = sb("zrow", [1, 512], BF16)
        neghalf = sb("neghalf", [P, 8])
        negfill = sb("negfill", [P, N])
        sd_i = sb("sd_i", [P, ET, 2], I32)
        pair_i = sb("pair_i", [P, ET], I32)
        srcf = sb("srcf", [P, ET])
        dstf = sb("dstf", [P, ET])
        deg = sb("deg", [P, 8])
        dinv = sb("dinv", [P, 8])
        dinv2 = sb("dinv2", [P, 8])
        indeg_row = sb("indeg_row", [1, NP])
        nw = sb("nw", [P, 4, 8])
        stats = sb("stats", [P, NT, 6])
        mv = sb("mv", [P, NT, 2])
        rstd = sb("rstd", [P, 8])
        bias_rows = sb("bias_rows", [P, 4, D])
        b1row = sb("b1row", [P, H0])
        gcnb = sb("gcnb", [P, GH])
        att = sb("att", [P, 2, D])
        b3T = sb("b3T", [128, HC])
        ffb = {"f0": sb("f0_b", [128, 8 * 4]), "f1": sb("f1_b", [128, 8 * 4]), "f2": sb("f2_b", [128, 8]),
               "f3": sb("f3_b", [128, 6 * 4]), "rt": sb("rt_b", [128, 1])}
        ffb2 = {k: sb(k + "_b2", [8, D]) for k in FFNS}
        wg = {"f0": sb("f0_wg", [128, DC, 8]), "f1": sb("f1_wg", [128, DC, 8]), "f2": sb("f2_wg", [128, 8, 8]),
              "f3": sb("f3_wg", [128, 6])}
        rw1 = sb("rw1", [128, DC, 128])
        rhT = sb("rhT", [128, NP])
        bg = sb("bg", [P, 5, 8])
        lg = sb("lg", [P, NT, 8])
        top = sb("top", [P, NT, 8])
        topi = sb("topi", [P, NT, 8], U32)
        topf = sb("topf", [P, NT, 8])
        gt = sb("gt", [P, 4, NT, 8])
        gate = sb("gate", [P, NT, 8])
        gateT = sb("gateT", [8, NP])
        onehots, parts = 2 * NT * P, 2 * NT * D
        with nc.sbuf_tensor("exR", [P, HEADS * N], F32) as exR:
            pass
        ZR = sb("ZR", [128, 2 * onehots + parts], F32R)
        xH, xL = (ZR[:, j * DC * NP:(j + 1) * DC * NP].rearrange("p (c n) -> p c n", c=DC) for j in range(2))
        hi = ZR[0:P, 0:U * H0].rearrange("p (s n) -> p s n", s=U)
        lo = ZR[0:P, U * H0:2 * U * H0].rearrange("p (s n) -> p s n", s=U)
        OHT = ZR[0:P, 0:2 * onehots].rearrange("p (s k e) -> p s k e", s=2, k=NT)
        xrS = ZR[0:P, 2 * onehots:].rearrange("p (s k d) -> p s k d", s=2, k=NT)
        nodeid = sb("nodeid", [P, 8])
        negid = sb("negid", [P, 8])
        eaT = sb("eaT", [2 * ED, 2, 2 * P])
        gidx = sb("gidx", [P, 4, 4], I32)
        sidx = sb("sidx", [P, 4, 2], I32)
        s4 = sb("s4", [P, 4, 2, HEADS])
        s4self = sb("s4self", [P, NT, HEADS])
        nmax = sb("nmax", [P, NT, HEADS])
        rden = sb("rden", [P, NT, HEADS])
        xl1 = sb("xl1", [P, NT, HEADS, HD + 1])
        ws = sb("ws", [128, 2, 2048])
        WH = sb("WH", [128, 2, 2048], F32R)
        wg2 = sb("wg2", [128, 2, 8 * 8], F32R)
        with nc.sbuf_tensor("WA_graph", [128, 3584], F32):
            with nc.sbuf_tensor("WL", [128, 2, 2048], F32R) as WL:
                pass
        WA = sb("WA", [128, 9216])
        W1a = WA[:, 0:1024].rearrange("p (c m) -> p c m", c=DC)
        W1b = WA[:, 1024:2048].rearrange("p (c m) -> p c m", c=DC)
        W1c = WA[:, 2048:2560]
        W2 = WA[:, 2560:4608].rearrange("p (c m) -> p c m", c=HC)
        W3 = WA[:, 4608:7680].rearrange("p (c m) -> p c m", c=DC + HC)
        W4 = WA[:, 7680:8704].rearrange("p (c m) -> p c m", c=HC)
        b2row = WA[0:1, 8704:9216]
        C1W1 = WA[:, 0:128].rearrange("p (c m) -> p c m", c=DC)
        C1W2 = WA[0:GH, 128:384]
        GW = [[WA[:, 512 * (1 + 2 * l + r):512 * (2 + 2 * l + r)].rearrange("p (c m) -> p c m", c=DC)
               for r in range(2)] for l in range(2)]
        C3W = [WA[:, 2560 + 512 * l:3072 + 512 * l].rearrange("p (c m) -> p c m", c=DC) for l in range(2)]
        GAT_AT = 9216
        with nc.sbuf_tensor("ZF", [128, 2 * FQ * NP], F32R) as ZF:
            pass
        with nc.sbuf_tensor("Z_before", [128, GAT_AT], F32):
            with nc.sbuf_tensor("ZE", [P, parts + onehots], F32R) as ZE:
                pass
        Z = sb("Z", [128, GAT_AT + 4096])

        def z(at, dims, rows=128):
            n = int(np.prod(dims))
            view = Z[0:rows, at:at + n]
            names = "abcd"[:len(dims)]
            if len(dims) == 1:
                return view
            return view.rearrange(f"p ({' '.join(names)}) -> p {' '.join(names)}", **dict(zip(names, dims)))

        PQ = z(0, [2, NT, H0], P)
        gP = z(5120, [4, H0], P)
        gQ = z(7168, [4, H0], P)
        tsum = z(9216, [U, H0], P)
        OH = ZF[0:P, 0:U * NP].rearrange("p (s n) -> p s n", s=U)
        W1cH = ZF[:, U * NP:U * NP + H0]
        W1cL = ZF[0:ED, U * NP + H0:U * NP + 2 * H0]
        eaS = ZF[:, U * NP + 2 * H0:U * NP + 2 * H0 + 4 * P].rearrange("p (s e) -> p s e", s=2)
        agg = z(HC * NP, [NT, H0], P)
        aggT = z(0, [HC, NP])
        msgT = z(HC * NP, [HC, NP])
        gT = z(8192, [HC, NP])
        ohS = Z[0:P, 11264:11264 + 2 * NP].bitcast(BF16).rearrange("p (s n) -> p s n", s=4)
        hH, hL = (ZF[:, j * FQ * NP:(j + 1) * FQ * NP].rearrange("p (c n) -> p c n", c=FQ) for j in range(2))
        hfull = z(2 * FQ * NP, [2, NP])
        hs = z(0, [NT, D], P)
        cT = z(1280, [DC, NP])
        h1c = z(2600, [NT, D], P)
        ctmp = z(3900, [NT, D], P)
        XLR = z(0, [2, NT, D], P)
        ag = z(2560, [4, 2, D], P)
        xlS = ZE[:, 0:parts].rearrange("p (s k d) -> p s k d", s=2, k=NT)
        OHS = ZE[:, parts:].rearrange("p (k e) -> p k e", k=NT)
        srcrow = z(GAT_AT + parts + onehots, [2 * P], P).bitcast(I32)
        apart = z(5632, [NT, 2 * P], P)
        bt = z(4608, [2, 2, D], P)
        sf = z(5632, [NT, D], P)
        sf2 = z(6912, [NT, D], P)
        dstrow = z(8192, [4, 2 * P], P).bitcast(I32)
        Sd = z(0, [2, N, 2, HEADS], P)
        ex = [z(10000, [HEADS, N], P), exR.rearrange("p (h n) -> p h n", h=HEADS)]
        PT = WA[0:P, 3584:6084].rearrange("p (k h n) -> p k h n", k=NT, h=HEADS)
        v = WA[0:P, 6084:7364].rearrange("p (t d) -> p t d", t=NT)
        v2 = WA[0:P, 7364:8644].rearrange("p (t d) -> p t d", t=NT)

        PS = ctx.enter_context(nc.psum_tensor("PS", [128, 8, 512], F32))

        ld_first = [sem(f"ld_first{i}") for i in range(3)]
        ld_small = sem("ld_small")
        ld_w0 = sem("ld_w0")
        ld_wg = sem("ld_wg")
        c_iota, c_ident, c_ones, c_zero, c_half, c_neg = (sem(s) for s in ("c_iota", "c_ident", "c_ones", "c_zero", "c_half", "c_neg"))
        c_xnT = sem("c_xnT")
        s_init = sem("s_init")
        idx_f = sem("idx_f")
        pairs_ready = sem("pairs_ready")
        ln_var = sem("ln_var")
        ln_pow = sem("ln_pow")
        ln_xn = sem("ln_xn")
        ln_tr = sem("ln_tr")
        ln_xnT = sem("ln_xnT")
        x_new = {i: sem(f"x_new{i}") for i in range(1, 9)}
        dch = sem("dch")
        pq_mm, p_ev, q_ev, pq_st = sem("pq_mm"), sem("p_ev"), sem("q_ev"), sem("pq_st")
        a_oh, a_mm, a_done, at_act, at_dve, at_ready = (sem(n) for n in ("a_oh", "a_mm", "a_done", "at_act", "at_dve", "at_ready"))
        deg_mm, deg_v, deg_pow, dinv_ready = sem("deg_mm"), sem("deg_v"), sem("deg_pow"), sem("dinv_ready")
        ea_ld = [sem(f"ea_ld{i}") for i in range(2)]
        g_idx = sem("g_idx")
        pool_go = sem("pool_go")
        gp_ld = [sem(f"gp_ld{i}") for i in range(4)]
        ea_hi, ea_lo, w1c_hi, w1c_lo = (sem(n) for n in ("ea_hi", "ea_lo", "w1c_hi", "w1c_lo"))
        l0_free = sem("l0_free")
        l0_e = sem("l0_e")
        l0_pre = sem("l0_pre")
        l0_hi = sem("l0_hi")
        l0_lo = sem("l0_lo")
        l0_seg = sem("l0_seg")
        l0_acc = sem("l0_acc")
        l0_agg_act, l0_agg_dve, l0_tr = sem("l0_agg_act"), sem("l0_agg_dve"), sem("l0_tr")
        l0_aggT, l0_m, l0_msgT, l0_g, l0_gT, l0_o = (sem(s) for s in ("l0_aggT", "l0_m", "l0_msgT", "l0_g", "l0_gT", "l0_o"))
        ff, raised = {k: {} for k in FFNS}, {}
        for k, f in FFNS.items():
            n_e, hc = f["experts"], f["hidden"]
            pairs = n_e // 2
            totals = dict(w1a=16 * pairs, w1b=16 * pairs, w2a=16 * pairs, w2b=16 * pairs, whi=4 * pairs, wlp=4 * pairs - 2, wld=2,
                          xh=NT, xl=NT, lgmm=1, lgv=1, gexp=1, gate=1, gT=NT, gTs=NT, b2mm=NT,
                          hmm=FQ * pairs, h=FQ * pairs, hlp=FQ, hld=FQ * (pairs - 1), ymm=NT * n_e)
            if k == "f2":
                totals.update(w1a=16, w1b=0, whi=1 + 2 * pairs, wlp=1 + 2 * (pairs - 1), hmm=FQ, h=FQ, hld=0, wgh=1, wgl=1, lgT=1, lgTs=1)
            if k == "f3":
                totals.update(w1a=32 * pairs, w1b=32 * pairs, lgv=2, gexp=2, rmm=1, rh=1)
            if k == "f1":
                totals.update(lgv=0, gexp=0)
            for n, total in totals.items():
                if n not in raised:
                    raised[n] = [sem(f"ff_{n}"), 0]
                ff[k][n] = Signal(*raised[n])
                raised[n][1] += total
        PAIRS = {k: f["experts"] // 2 for k, f in FFNS.items()}
        W_COLS = {"f0": (1024, 1024), "f1": (1024, 1024), "f2": (0, 2048), "f3": (1024, 512)}
        W_AT = {k: 0 if k == "f2" else 1024 for k in FFNS}

        def whi_n(k, i, g, u):
            return 2 * i + u + 2 if k == "f2" else 4 * i + 2 * g + u + 1

        def wlp_n(k, i, g, u):
            if k == "f2":
                return 2 * i + u
            return 4 * i + 2 * g + u - 1 if not isinstance(i, int) or i else u + 1

        gc = {k: {s: sem(f"{k}_{s}") for s in names + ("hs", "ymm", "h1", "a2mm", "a2T", "omm")}
              for k, names in (("c1", ("hmm",)), ("c3", ("amm", "aT")))}
        totals = dict(xmm=2 * NT, xev=2 * NT, st=16, self=1, diag=16 * NT, gi=3 * ET // 8, gl0=4 * ET, gl1=4 * ET, gl2=4 * ET, sr=2 * ET, ohs=ET // 8, xls=NT, apart=ET // 8, cp=ET // 8,
                      dr0=2 * ET, dr1=2 * ET, dr2=2 * ET, dr3=2 * ET, xrs=NT, oht=ET // 2, xg=ET // 2, lr=11 * ET // 8,
                      s4=ET // 2, si=ET // 2, scat0=8 * ET, scat1=8 * ET, sd0=32 * 3, sd1=32 * 2, mrg=NT, max=NT, exp=NT * HEADS, tr=NT * NT,
                      pt=NT * NT, omm=NT, min=NT, emin=NT, h=NT, htr=NT, hT=NT)
        ga_sems = {n: sem(f"ga_{n}") for n in totals}
        ga = [{n: Signal(ga_sems[n], l * total) for n, total in totals.items()} for l in range(2)]
        out_done = sem("out_done")

        block = ctx.enter_context(nc.Block())
        bg_of = {"f0": 0, "f1": 2, "f2": 3, "f3": 4}

        @block.sync
        def _(sp):
            sp.dma_start(x[:, :, :], a["x"].rearrange("(t p) d -> p t d", p=P)).then_inc(ld_first[2], 16)
            sp.dma_start(sd_i[:, :, :], a["src_dst"]).then_inc(ld_first[0], 16)
            sp.dma_start(W1a, a["L0_gnn_W1"][0:D, :].rearrange("(c p) m -> p c m", p=128)).then_inc(ld_w0, 16)
            sp.dma_start(W1b, a["L0_gnn_W1"][D:2 * D, :].rearrange("(c p) m -> p c m", p=128)).then_inc(ld_w0, 16)
            for r in range(2):
                sp.dma_start(W1c[r * ED:(r + 1) * ED, :], a["L0_gnn_W1"][2 * D:2 * D + ED, :]).then_inc(ld_w0, 16)
            sp.dma_start(W2, a["L0_gnn_W2"].rearrange("(c p) m -> p c m", p=128)).then_inc(ld_w0, 16)
            sp.dma_start(W3, a["L0_gnn_W3"].rearrange("(c p) m -> p c m", p=128)).then_inc(ld_w0, 16)
            sp.dma_start(W4, a["L0_gnn_W4"].rearrange("(c p) m -> p c m", p=128)).then_inc(ld_w0, 16)
            sp.dma_start(b2row, a["L0_gnn_b2"]).then_inc(ld_w0, 16)
            sp.dma_start(b1row[:, :], a["L0_gnn_b1"].to_broadcast([P, H0])).then_inc(ld_w0, 16)
            n = 0
            for dst_ap, src_ap in (
                    [(bias_rows[:, j, :], a[k].to_broadcast([P, D])) for j, k in
                     enumerate(("L0_gnn_b4", "L1_gnn_b2", "L2_gnn_b0", "L2_gnn_b1"))]
                    + [(gcnb[:, :], a["L1_gnn_b1"].to_broadcast([P, GH])), (b3T[:, :], a["L0_gnn_b3"])]
                    + [(att[:, l, :], a[f"L2_gnn_att{l}"].to_broadcast([P, D])) for l in range(2)]
                    + [(ffb[k][:, :], a[s]) for k, s in
                       (("f0", "L0_ffn_b1"), ("f1", "L1_ffn_b1"), ("f2", "L2_ffn_b1"), ("f3", "L3_b12"), ("rt", "L3_ffn_router_b1"))]
                    + [(ffb2[k][0:FFNS[k]["experts"], :], a[s]) for k, s in
                       (("f0", "L0_ffn_b2"), ("f1", "L1_ffn_b2"), ("f2", "L2_ffn_bd"), ("f3", "L3_ffn_expert_b3"))]
                    + [(wg[k][:, :, :], a[s].rearrange("(c p) e -> p c e", p=128)) for k, s in
                       (("f0", "L0_ffn_Wg"), ("f1", "L1_ffn_Wg"), ("f2", "L2_ffn_Wg"))]
                    + [(wg["f3"][:, :], a["L3_ffn_router_w2"]),
                       (rw1[:, :, :], a["L3_ffn_router_w1"].rearrange("(c p) m -> p c m", p=128))]
                    + [(bg[:, j, 0:m], a[k].to_broadcast([P, m])) for j, (k, m) in
                       enumerate((("L0_ffn_bg", 8), ("L0_ffn_bias", 8), ("L1_ffn_bg", 8), ("L2_ffn_bg", 8), ("L3_ffn_router_b2", 6)))]):
                sp.dma_start(dst_ap, src_ap).then_inc(ld_small, 16)
                n += 1
            assert n == N_SMALL
            sp.wait_ge(c_neg, 1)
            rows = S_tab[0:2 * N * N, :].rearrange("(t p s) h -> t p (s h)", t=NT, p=P)
            for t in range(NT):
                for q in range(2 * HEADS):
                    sp.dma_start(rows[t, :, q * N:(q + 1) * N], negfill[:, :]).then_inc(s_init, 16)
            for j, tab in enumerate((P_tab, Q_tab)):
                sp.wait_ge((p_ev, q_ev)[j], NT)
                sp.dma_start(tab.rearrange("(t p) m -> p t m", p=P), PQ[:, j, :, :]).then_inc(pq_st, 16)
            for h in range(2):
                for r in range(2):
                    sp.dma_start(eaT[r * ED:(r + 1) * ED, h, :], a["edge_attr_64"][h]).then_inc(ea_ld[h], 16)
            with sp.Fori(0, EI - 1) as i:
                for h in range(2):
                    sp.wait_ge(ea_lo, 2 * i + h + 1)
                    for r in range(2):
                        sp.dma_start(eaT[r * ED:(r + 1) * ED, h, :], a["edge_attr_64"][bass.ds((i + 1) * 2 + h, 1)].rearrange("a p m -> (a p) m"))\
                            .then_inc(ea_ld[h], 16)

            def pair_of(name, i, u):
                return a[name][2 * i + u] if isinstance(i, int) else a[name][bass.ds(2 * i + u, 1)].rearrange("e p m -> (e p) m")

            def load_first(k, i, u):
                for j, name in enumerate(FIRST[k]):
                    m = W_COLS[k][0] // len(FIRST[k])
                    sp.dma_start(ws[:, u, j * m:(j + 1) * m], pair_of(name, i, u)).then_inc(ff[k]["w1" + "ab"[u]].sem, 16)

            def load_last(k, i, u):
                sp.dma_start(ws[:, slot(k, u), W_AT[k]:W_AT[k] + W_COLS[k][1]], pair_of(LAST[k], i, u))\
                    .then_inc(ff[k]["w2" + "ab"[u]].sem, 16)

            def first_pair(k):
                for u in range(2):
                    load_first(k, 0, u)
                    load_last(k, 0, u)

            def later_pairs(k):
                f = ff[k]
                for u in range(2):
                    if W_COLS[k][0]:
                        sp.wait_ge(*f["wlp"](wlp_n(k, 0, 0, u)))
                        load_first(k, 1, u)
                for u in range(2):
                    sp.wait_ge(*f["wld"](u + 1))
                    load_last(k, 1, u)
                with sp.Fori(2, PAIRS[k]) as i:
                    for u in range(2):
                        if W_COLS[k][0]:
                            sp.wait_ge(*f["wlp"](wlp_n(k, i - 1, 0, u)))
                            load_first(k, i, u)
                    for u in range(2):
                        sp.wait_ge(*f["wlp"](wlp_n(k, i - 1, 1, u)))
                        load_last(k, i, u)

            first_pair("f0")
            later_pairs("f0")
            sp.wait_ge(l0_o, NT)
            sp.dma_start(C1W1, a["L1_gnn_W1"].rearrange("(c p) m -> p c m", p=128)).then_inc(ld_wg, 16)
            sp.dma_start(C1W2, a["L1_gnn_W2"]).then_inc(ld_wg, 16)
            for l in range(2):
                for r, k in enumerate(("l", "r")):
                    sp.dma_start(GW[l][r], a[f"L2_gnn_W{k}{l}"].rearrange("(c p) m -> p c m", p=128)).then_inc(ld_wg, 16)
                sp.dma_start(C3W[l], a[f"L3_gnn_W{l + 1}"].rearrange("(c p) m -> p c m", p=128)).then_inc(ld_wg, 16)
            sp.wait_ge(*ff["f1"]["wlp"](0))
            first_pair("f1")
            later_pairs("f1")
            sp.wait_ge(*ff["f2"]["wlp"](0))
            sp.dma_start(ws[:, 0, :], a["L2_ffn_W1"]).then_inc(ff["f2"]["w1a"].sem, 16)
            load_last("f2", 0, 0)

            def gat_tables(l):
                g = ga[l]

                def target_rows(i):
                    for q in range(4):
                        if not isinstance(i, int):
                            sp.wait_ge(*g["oht"](4 * i + q - 3))
                        row = a["dst_row"][4 * i + q] if isinstance(i, int) else a["dst_row"][bass.ds(4 * i + q, 1)].rearrange("a o e -> (a o) e")
                        sp.dma_start(dstrow[:, q, :], row.to_broadcast([P, 2 * P])).then_inc(g[f"dr{q}"].sem, 16)
                    if not isinstance(i, int):
                        sp.wait_ge(*g["apart"](i))
                    row = a["src_row"][i] if isinstance(i, int) else a["src_row"][bass.ds(i, 1)].rearrange("a o e -> (a o) e")
                    sp.dma_start(srcrow, row.to_broadcast([P, 2 * P])).then_inc(g["sr"].sem, 16)

                sp.wait_ge(*g["xmm"](1))
                target_rows(0)
                sp.wait_ge(*g["xev"](NT))
                sp.dma_start(XL_tab[l].rearrange("(t p) m -> p t m", p=P), XLR[:, 0, :, :]).then_inc(g["st"].sem, 16)
                sp.wait_ge(*g["self"](1))
                sp.wait_ge(s_init, 16 * 2 * NT * HEADS)
                for t in range(NT):
                    diag = S_tab.rearrange("(t p r) h -> t p r h", t=NT, p=P)[t, :, 0, :]
                    sp.dma_start(diag, s4self[:, t, :]).then_inc(g["diag"].sem, 16)
                with sp.Fori(1, ET // 8) as i:
                    target_rows(i)
                for h in range(2):
                    sp.wait_ge(*g[f"scat{h}"](8 * ET))
                rows = S_tab[0:2 * N * N, :].rearrange("(t p s j) h -> t p s j h", t=NT, p=P, j=2)
                for t in range(NT):
                    if t >= 2:
                        sp.wait_ge(*g["mrg"](t - 1))
                    elif t:
                        sp.wait_ge(*g["sd0"](32))
                    for h in range(2):
                        half = slice(h * (N // 2), N if h else N // 2)
                        sp.dma_start(Sd[:, t % 2, half, :, :], rows[t][:, half]).then_inc(g[f"sd{t % 2}"].sem, 16)

            gat_tables(0)
            gat_tables(1)

            sp.wait_ge(*ff["f2"]["wlp"](1))
            load_last("f2", 0, 1)
            later_pairs("f2")
            sp.wait_ge(*ff["f3"]["wlp"](0))
            first_pair("f3")
            later_pairs("f3")
            sp.wait_ge(x_new[8], NT * 7)
            sp.dma_start(out.rearrange("(t p) d -> p t d", p=P), x[:, :, :]).then_inc(out_done, 16)
            sp.wait_ge(out_done, 16)
            sp.wait_ge(pq_st, 32)
            for l in range(2):
                sp.wait_ge(*ga[l]["st"](16))
                sp.wait_ge(*ga[l]["diag"](16 * NT))
                for h in range(2):
                    sp.wait_ge(*ga[l][f"scat{h}"](8 * ET))

        @block.gpsimd
        def _(pool):
            g = nc.gpsimd
            g.iota(iota[:, :], [[1, NP]], base=0, channel_multiplier=0, allow_small_or_imprecise_dtypes=True).then_inc(c_iota, 1)
            g.iota(nodeid[:, 0:NT], [[P, NT]], base=0, channel_multiplier=1, allow_small_or_imprecise_dtypes=True).then_inc(c_iota, 1)
            g.iota(negid[:, 0:NT], [[-P, NT]], base=0, channel_multiplier=-1, allow_small_or_imprecise_dtypes=True).then_inc(c_iota, 1)
            g.memset(ident[:, :], 0.0).then_inc(c_ident, 1)
            g.memset(ones[:, :], 1.0).then_inc(c_ones, 1)
            g.memset(xnT[:, :, N:NP], 0.0).then_inc(c_xnT, 1)
            g.memset(zrow[:, :], 0.0).then_inc(c_zero, 1)
            g.memset(neghalf[:, :], -0.5).then_inc(c_half, 1)
            g.memset(negfill[:, :], NEG).then_inc(c_neg, 1)
            g.memset(xl1[:, :, :, HD:HD + 1], 1.0).then_inc(c_ones, 1)
            pool.wait_ge(c_ident, 1)
            g.affine_select(out=ident[:, :], in_=ident[:, :], compare_op=ALU.not_equal, fill=1.0, base=0,
                            pattern=[[-1, 128]], channel_multiplier=1).then_inc(c_ident, 1)

            def layernorm_pow(i):
                pool.wait_ge(ln_var, i + 1)
                g.tensor_tensor(nw[:, 1, 0:NT], nw[:, 0, 0:NT], neghalf[:, 0:NT], ALU.pow).then_inc(ln_pow, 1)

            pool.wait_ge(c_half, 1)
            layernorm_pow(0)
            pool.wait_ge(ld_first[0], 16)
            pool.wait_ge(pq_st, 32)

            def gather_step(i):
                for h in range(2):
                    if not isinstance(i, int):
                        for u in (2 * h, 2 * h + 1):
                            pool.wait_ge(gp_ld[u], 32 * i)
                    g.tensor_copy(gidx[:, h, :], sd_i[:, bass.ds(U * i + 2 * h, 2), :].rearrange("p t j -> p (t j)")).then_inc(g_idx, 1)
                    pool.wait_ge(g_idx, 2 * i + h + 1)
                    for j in range(2):
                        u = 2 * h + j
                        pool.wait_ge(l0_free, U * i + u + 1)
                        pool.sem_inc(pool_go)
                        for gath, tab, c in ((gP, P_tab, 2 * j), (gQ, Q_tab, 2 * j + 1)):
                            g.indirect_dma_start(gath[:, u, :], None, tab, bass.IndirectOffsetOnAxis(ap=gidx[:, h, c:c + 1], axis=0))\
                                .then_inc(gp_ld[u], 16)

            gather_step(0)
            with pool.Fori(1, EI) as i:
                gather_step(i)

            pool.wait_ge(deg_v, 1)
            g.tensor_tensor(nw[:, 1, 0:NT], deg[:, 0:NT], neghalf[:, 0:NT], ALU.pow).then_inc(deg_pow, 1)

            def low(out_, full, high, sem_):
                g.tensor_tensor(out_, full, high.bitcast(F32), ALU.subtract).then_inc(sem_, 1)

            def weights_low(k, i, g_, u):
                at, cols = (W_AT[k], W_COLS[k][1]) if g_ else (0, W_COLS[k][0])
                pool.wait_ge(*ff[k]["whi"](whi_n(k, i, g_, u)))
                w_ = slot(k, u)
                low(WL[:, w_, at:at + cols], ws[:, w_, at:at + cols], WH[:, w_, at:at + cols], ff[k]["wlp"].sem)

            def hidden_low(k):
                for c in range(FQ):
                    pool.wait_ge(*ff[k]["h"](c + 1))
                    low(hL[:, c, :], hfull[:, c % 2, :], hH[:, c, :], ff[k]["hlp"].sem)

            def ffn(k):
                hidden_low(k)
                with pool.Fori(1, PAIRS[k]) as i:
                    for g_ in range(2):
                        for u in range(2):
                            if W_COLS[k][g_]:
                                weights_low(k, i, g_, u)

            pool.wait_ge(l0_o, NT)
            weights_low("f0", 0, 0, 0)
            layernorm_pow(1)
            weights_low("f0", 0, 0, 1)
            ffn("f0")
            layernorm_pow(2)
            weights_low("f1", 0, 0, 0)
            weights_low("f1", 0, 0, 1)
            layernorm_pow(3)
            ffn("f1")
            layernorm_pow(4)

            def gat(l):
                q = ga[l]
                pool.wait_ge(*q["st"](16))

                def gather(i, k):
                    if not isinstance(i, int):
                        pool.wait_ge(*q["s4"](4 * i + k - 3))
                    pool.wait_ge(*q["gi"](len(GATHERED) * i + k + 1))
                    pool.sem_inc(pool_go)
                    for j in range(2):
                        g.indirect_dma_start(ag[:, k, j, :], None, XL_tab[l], bass.IndirectOffsetOnAxis(ap=gidx[:, k, 2 * j:2 * j + 1], axis=0))\
                            .then_inc(q[f"gl{k}"].sem, 16)

                def scatter(p, k):
                    for j in range(2):
                        if not isinstance(p, int) or p:
                            pool.wait_ge(*q[f"scat{j}"](16 * p))
                        if j == 0:
                            pool.wait_ge(*q["si"](p + 1))
                            pool.wait_ge(*q["s4"](p + 1))
                        pool.sem_inc(pool_go)
                        g.indirect_dma_start(S_tab, bass.IndirectOffsetOnAxis(ap=sidx[:, k, j:j + 1], axis=0), s4[:, k, j, :], None)\
                            .then_inc(q[f"scat{j}"].sem, 16)

                for p in range(4):
                    if p in GATHERED:
                        gather(0, p)
                    if p == 2:
                        pool.wait_ge(*q["diag"](16 * NT))
                    if p >= 2:
                        scatter(p - 2, p - 2)
                with pool.Fori(1, ET // 8) as i:
                    for k in range(4):
                        if k in GATHERED:
                            gather(i, k)
                        scatter(4 * i + k - 2, (k - 2) % 4)
                for p in (ET // 2 - 2, ET // 2 - 1):
                    scatter(p, p % 4)

            gat(0)
            gat(1)
            pool.wait_ge(*ga[1]["omm"](NT))
            pool.wait_ge(*ff["f2"]["whi"](1))
            low(WL[:, 0, :], ws[:, 0, :], WH[:, 0, :], ff["f2"]["wlp"].sem)
            layernorm_pow(5)
            ffn("f2")
            layernorm_pow(6)
            weights_low("f3", 0, 0, 0)
            weights_low("f3", 0, 0, 1)
            layernorm_pow(7)
            ffn("f3")

        @block.scalar
        def _(act):
            s = nc.scalar

            def layernorm_evac(i, k=None):
                for t in range(NT):
                    act.wait_ge(ln_tr, NT * i + t + 1)
                    s.activation(xnT[:, :, t * P:(t + 1) * P], PS[:, 6 + t % 2, 0:DC * P].rearrange("p (c n) -> p c n", c=DC),
                                 ACT.Copy).then_inc(ln_xnT, 1)
                    if k:
                        act.wait_ge(ln_xnT, NT * i + t + 1)
                        cols = slice(t * P, (t + 1) * P if t < NT - 1 else NP)
                        s.activation(xH[:, :, cols], xnT[:, :, cols], ACT.Copy).then_inc(ff[k]["xh"].sem, 1)

            act.wait_ge(c_xnT, 1)
            layernorm_evac(0)
            for t in range(NT):
                act.wait_ge(pq_mm, t + 1)
                s.activation(PQ[:, 0, t, :], PS[0:P, 7, :], ACT.Copy).then_inc(p_ev, 1)
            act.wait_ge(a_done, 1)
            s.activation(AT[:, NT - 1, 0:500], PS[0:P, NT - 1, 0:500], ACT.Copy)
            for k in range(NT):
                s.activation(AT[:, k, 500:NP], PS[0:P, 5 + k // 4, 128 * (k % 4):128 * (k % 4) + 128], ACT.Copy).then_inc(at_act, 1)
            act.wait_ge(ld_w0, 16 * 9)
            act.wait_ge(pq_st, 32)
            s.activation(W1cH, W1c, ACT.Copy).then_inc(w1c_hi, 1)

            def attr_high(i, h):
                act.wait_ge(ea_ld[h], 32 * i + 32)
                if not isinstance(i, int):
                    act.wait_ge(l0_e, U * i + 2 * h - 2)
                s.activation(eaS[:, h, :], eaT[:, h, :], ACT.Copy).then_inc(ea_hi, 1)

            def high(i, u):
                act.wait_ge(l0_pre, U * i + u + 3)
                act.wait_ge(l0_seg, U * i + u + 1)
                s.activation(hi[:, u, :], tsum[:, u, :], ACT.Relu).then_inc(l0_hi, 1)

            attr_high(0, 0)
            attr_high(0, 1)
            with act.Fori(0, EI - 1) as i:
                for u in range(U):
                    high(i, u)
                    if u % 2 == 0:
                        attr_high(i + 1, u // 2)
            for u in range(U):
                high(EI - 1, u)
            act.wait_ge(l0_acc, 1)
            for t in range(0, NT, 2):
                s.activation(agg[:, t, :], PS[0:P, t, :], ACT.Copy).then_inc(l0_agg_act, 1)
            for t in range(NT):
                act.wait_ge(l0_tr, t + 1)
                s.activation(aggT[:, :, t * P:(t + 1) * P], PS[:, 5 + t % 2, 0:HC * P].rearrange("p (c n) -> p c n", c=HC),
                             ACT.Copy).then_inc(l0_aggT, 1)
            for dst_t, mm, ev, bias in ((msgT, l0_m, l0_msgT, None), (gT, l0_g, l0_gT, b3T)):
                if bias is not None:
                    act.wait_ge(ld_small, 16 * N_SMALL)
                for m in range(HC):
                    act.wait_ge(mm, m + 1)
                    src_ap = PS[:, 2 * (m % 2):2 * (m % 2) + 2, 0:NH]
                    dst_ap = dst_t[:, m, :].rearrange("p (b n) -> p b n", b=2)
                    if bias is None:
                        s.activation(dst_ap, src_ap, ACT.Copy).then_inc(ev, 1)
                    else:
                        s.activation(dst_ap, src_ap, ACT.Relu, bias=bias[:, m:m + 1]).then_inc(ev, 1)

            def weights_high(k, i, g_, u):
                at, cols = (W_AT[k], W_COLS[k][1]) if g_ else (0, W_COLS[k][0])
                per = 32 if k == "f3" and not g_ else 16
                act.wait_ge(*ff[k][("w1", "w2")[g_] + "ab"[u]](per * i + per))
                if g_ and (not isinstance(i, int) or i):
                    act.wait_ge(*ff[k]["ymm"](NT * (2 * i - 1 + u)))
                w_ = slot(k, u)
                s.activation(WH[:, w_, at:at + cols], ws[:, w_, at:at + cols], ACT.Copy).then_inc(ff[k]["whi"].sem, 1)

            def hidden(k, i, chunks):
                f = ff[k]
                for c in chunks:
                    u, layer, m = hidden_chunk(k, c)
                    col = FQ * i + (c if k != "f3" else 4 * u + 2 * layer + m)
                    bias = ffb[k][:, col:col + 1] if isinstance(i, int) else ffb[k][:, bass.ds(col, 1)]
                    src_ap = PS[:, 2 * (c % 2):2 * (c % 2) + 2, 0:NH]
                    if c >= 2:
                        act.wait_ge(*(f["hlp"](c - 1) if isinstance(i, int) else f["hld"](FQ * i - FQ + c - 1)))
                    act.wait_ge(*f["hmm"](FQ * i + c + 1))
                    s.activation(hH[:, c, :].rearrange("p (b n) -> p b n", b=2), src_ap, FFNS[k]["act"], bias=bias)
                    s.activation(hfull[:, c % 2, :].rearrange("p (b n) -> p b n", b=2), src_ap, FFNS[k]["act"], bias=bias)\
                        .then_inc(f["h"].sem, 1)

            def first_high(k):
                for g_ in range(2):
                    for u in range(2):
                        weights_high(k, 0, g_, u)

            def later_hidden(k):
                with act.Fori(1, PAIRS[k]) as i:
                    for u in range(2):
                        if W_COLS[k][0]:
                            weights_high(k, i, 0, u)
                    for u in range(2):
                        weights_high(k, i, 1, u)
                        if k != "f2":
                            hidden(k, i, range(4 * u, 4 * u + 4))

            def gate_exp(k, out_ap, in_ap):
                act.wait_ge(*ff[k]["lgv"](1))
                s.activation(out_ap, in_ap, ACT.Exp).then_inc(ff[k]["gexp"].sem, 1)

            first_high("f0")
            layernorm_evac(1, "f0")
            gate_exp("f0", gt[:, 0, :, 0], gt[:, 1, :, 0])
            hidden("f0", 0, range(FQ))
            later_hidden("f0")
            layernorm_evac(2)
            c = gc["c1"]
            for t in range(NT):
                act.wait_ge(c["hmm"], t + 1)
                s.activation(hs[:, t, 0:GH], PS[0:P, t % 2, 0:GH], ACT.Copy, scale=dinv[:, t:t + 1]).then_inc(c["hs"], 1)
            act.wait_ge(*ff["f0"]["ymm"](NT * FFNS["f0"]["experts"]))
            first_high("f1")
            act.wait_ge(c["a2mm"], 1)
            s.activation(cT[0:GH, 0, :].rearrange("p (b n) -> p b n", b=2), PS[0:GH, 4:6, 0:NH], ACT.Copy).then_inc(c["a2T"], 1)
            layernorm_evac(3, "f1")
            hidden("f1", 0, range(FQ))
            later_hidden("f1")
            act.wait_ge(*ff["f1"]["ymm"](NT * FFNS["f1"]["experts"]))
            act.wait_ge(*ff["f2"]["w1a"](16))
            s.activation(WH[:, 0, :], ws[:, 0, :], ACT.Copy).then_inc(ff["f2"]["whi"].sem, 1)
            weights_high("f2", 0, 1, 0)
            s.activation(wg2[:, 0, :], wg["f2"][:, :, :].rearrange("p c e -> p (c e)"), ACT.Copy).then_inc(ff["f2"]["wgh"].sem, 1)

            layernorm_evac(4)

            def gat(l):
                q = ga[l]
                for t in range(NT):
                    act.wait_ge(*q["xmm"](t + 1))
                    s.activation(XLR[:, 0, t, :], PS[0:P, t % 2, 0:D], ACT.Copy)
                    s.activation(xlS[:, 0, t, :], PS[0:P, t % 2, 0:D], ACT.Copy).then_inc(q["xev"].sem, 1)
                for t in range(NT):
                    act.wait_ge(*q["xmm"](NT + t + 1))
                    s.activation(XLR[:, 1, t, :], PS[0:P, (NT + t) % 2, 0:D], ACT.Copy)
                    s.activation(xrS[:, 0, t, :], PS[0:P, (NT + t) % 2, 0:D], ACT.Copy).then_inc(q["xev"].sem, 1)

                def elu_exp(t):
                    act.wait_ge(*q["min"](t + 1))
                    s.activation(v2[:, t, :], v2[:, t, :], ACT.Exp).then_inc(q["emin"].sem, 1)

                act.wait_ge(pairs_ready, 2)

                def sources(i):
                    act.wait_ge(*q["sr"](16 * i + 16))
                    if not isinstance(i, int):
                        act.wait_ge(*q["xg"](4 * i))
                    for t in range(NT):
                        ins = s.activation(apart[:, t, :], srcrow, ACT.Abs, bias=negid[:, t:t + 1])
                    ins.then_inc(q["apart"].sem, 1)
                    act.wait_ge(*q["apart"](i + 1))
                    s.activation(OHS, apart[:, :, :], ACT.Relu, bias=ones[0:P, 0:1], scale=-1.0).then_inc(q["ohs"].sem, 1)

                def copy_sum(i):
                    act.wait_ge(*q["xg"](4 * i + 4))
                    s.activation(ag[:, 3, :, :].rearrange("p j d -> p (j d)"), PS[0:P, 5, :], ACT.Copy).then_inc(q["cp"].sem, 1)

                act.wait_ge(*q["self"](1))

                def indices(i):
                    for k in range(4):
                        p = 4 * i + k
                        if k in GATHERED:
                            if not isinstance(i, int):
                                act.wait_ge(*q[f"gl{k}"](32 * i))
                            s.activation(gidx[:, k, :], sd_i[:, bass.ds(2 * p, 2), :].rearrange("p t j -> p (t j)"), ACT.Copy)\
                                .then_inc(q["gi"].sem, 1)
                        if not isinstance(i, int):
                            for j in range(2):
                                act.wait_ge(*q[f"scat{j}"](16 * (p - 3)))
                        s.activation(sidx[:, k, :], pair_i[:, bass.ds(2 * p, 2)], ACT.Copy).then_inc(q["si"].sem, 1)
                        if k == 0 and not isinstance(i, int):
                            copy_sum(i - 1)
                        if k == 1:
                            sources(i)

                indices(0)
                with act.Fori(1, ET // 8) as i:
                    indices(i)
                copy_sum(ET // 8 - 1)
                for t in range(NT):
                    act.wait_ge(*q["max"](t + 1))
                    for h in range(HEADS):
                        s.activation(ex[t % 2][:, h, :], ex[t % 2][:, h, :], ACT.Exp, bias=nmax[:, t, h:h + 1]).then_inc(q["exp"].sem, 1)
                    if t >= 3:
                        elu_exp(t - 3)
                for t in range(NT - 3, NT):
                    elu_exp(t)
                if l == 0:
                    for t in range(NT):
                        act.wait_ge(*q["htr"](t + 1))
                        s.activation(xnT[:, :, t * P:(t + 1) * P], PS[:, 4 + t % 2, 0:DC * P].rearrange("p (c n) -> p c n", c=DC),
                                     ACT.Copy).then_inc(q["hT"].sem, 1)

            gat(0)
            gat(1)
            layernorm_evac(5, "f2")
            hidden("f2", 0, range(FQ))
            act.wait_ge(*ff["f2"]["lgT"](1))
            s.activation(gateT[:, :].rearrange("p (b n) -> p b n", b=2), PS[0:8, 4:6, 0:NH], ACT.Copy).then_inc(ff["f2"]["lgTs"].sem, 1)
            weights_high("f2", 0, 1, 1)
            gate_exp("f2", gt[:, 1, :, :], gt[:, 0, :, :])
            later_hidden("f2")
            layernorm_evac(6)
            first_high("f3")
            c = gc["c3"]
            for mm, ev in (("amm", "aT"), ("a2mm", "a2T")):
                for m in range(DC):
                    act.wait_ge(c[mm], m + 1)
                    s.activation(cT[:, m, :].rearrange("p (b n) -> p b n", b=2), PS[:, 2 * m:2 * m + 2, 0:NH], ACT.Copy).then_inc(c[ev], 1)
                if mm == "amm":
                    for t in range(NT):
                        act.wait_ge(c["ymm"], t + 1)
                        s.activation(h1c[:, t, :], PS[0:P, 4 + t % 2, 0:D], ACT.Relu, scale=dinv2[:, t:t + 1]).then_inc(c["h1"], 1)
            layernorm_evac(7, "f3")
            f = ff["f3"]
            act.wait_ge(*f["rmm"](1))
            s.activation(rhT[:, :].rearrange("p (b n) -> p b n", b=2), PS[:, 4:6, 0:NH], ACT.Relu, bias=ffb["rt"][:, 0:1]).then_inc(f["rh"].sem, 1)
            gate_exp("f3", gt[:, 1, :, :], gt[:, 0, :, :])
            act.wait_ge(*f["lgv"](2))
            s.activation(gt[:, 0, :, 0], gt[:, 2, :, 0], ACT.Exp).then_inc(f["gexp"].sem, 1)
            hidden("f3", 0, range(FQ))
            later_hidden("f3")

        @block.vector
        def _(dve):
            w = nc.vector
            chain = [0]

            def link(ins):
                chain[0] += 1
                ins.then_inc(dch, 1)
                dve.wait_ge(dch, chain[0])

            def newton(ve, r0, dst):
                link(w.scalar_tensor_tensor(nw[:, 2, 0:NT], r0, -0.5, r0, ALU.mult, ALU.mult))
                link(w.tensor_tensor(nw[:, 3, 0:NT], nw[:, 2, 0:NT], ve, ALU.mult))
                return w.scalar_tensor_tensor(dst, nw[:, 3, 0:NT], 1.5, r0, ALU.add, ALU.mult)

            def moments(t):
                return w.bn_stats(stats[:, t, :], x[:, t, :])

            def layernorm(i, before, k=None):
                for t in range(NT):
                    if before:
                        before(t)
                        ins = moments(t)
                if not before:
                    ins = moments(NT - 1)
                link(ins)
                for t in range(NT):
                    ins = w.bn_aggr(mv[:, t, :], stats[:, t, :])
                link(ins)
                w.tensor_scalar(nw[:, 0, 0:NT], mv[:, :, 1], LN_EPS, None, ALU.add).then_inc(ln_var, 1)
                dve.wait_ge(ln_pow, i + 1)
                link(newton(nw[:, 0, 0:NT], nw[:, 1, 0:NT], rstd[:, 0:NT]))
                for t in range(NT):
                    w.tensor_scalar(xn[:, t, :], x[:, t, :], mv[:, t, 0:1], rstd[:, t:t + 1], ALU.subtract, ALU.mult)\
                        .then_inc(ln_xn, 1)
                if k:
                    for t in range(NT):
                        dve.wait_ge(*ff[k]["xh"](t + 1))
                        cols = slice(t * P, (t + 1) * P if t < NT - 1 else NP)
                        w.tensor_tensor(xL[:, :, cols], xnT[:, :, cols], xH[:, :, cols].bitcast(F32), ALU.subtract)\
                            .then_inc(ff[k]["xl"].sem, 1)

            def last_low(k, u):
                dve.wait_ge(*ff[k]["whi"](whi_n(k, 0, 1, u)))
                w_, cols = slot(k, u), slice(W_AT[k], W_AT[k] + W_COLS[k][1])
                w.tensor_tensor(WL[:, w_, cols], ws[:, w_, cols], WH[:, w_, cols].bitcast(F32), ALU.subtract).then_inc(ff[k]["wld"].sem, 1)

            dve.wait_ge(ld_first[0], 16)
            w.tensor_copy(srcf[:, :], sd_i[:, :, 0]).then_inc(idx_f, 1)
            w.tensor_copy(dstf[:, :], sd_i[:, :, 1]).then_inc(idx_f, 1)
            dve.wait_ge(idx_f, 2)
            pairf = z(0, [2, ET // 2, 2], P)
            link(w.scalar_tensor_tensor(pairf[:, 0].rearrange("p a b -> p (a b)"), dstf[:, :], float(N), srcf[:, :], ALU.mult, ALU.add))
            for j in range(2):
                w.tensor_scalar(pair_i[:, :].rearrange("p (a b) -> p a b", b=2)[:, :, j], pairf[:, 0, :, j], 2.0, float(j), ALU.mult, ALU.add)\
                    .then_inc(pairs_ready, 1)
            dve.wait_ge(ld_first[2], 16)
            layernorm(0, lambda t: None)
            dve.wait_ge(c_iota, 3)
            dve.sem_inc(a_mm, 2)

            def count_onehots(i, u):
                dve.wait_ge(a_mm, 2 * i + u + 1)
                w.tensor_scalar(ohS[:, 2 * u, :], iota[0:P, :], srcf[:, bass.ds(2 * i + u, 1)], None, ALU.is_equal)
                w.tensor_scalar(ohS[:, 2 * u + 1, :], iota[0:P, :], dstf[:, bass.ds(2 * i + u, 1)], None, ALU.is_equal).then_inc(a_oh, 1)

            with dve.Fori(0, PQ_FROM) as i:
                for u in range(2):
                    count_onehots(i, u)
            for n in range(2 * NT):
                count_onehots(PQ_FROM + n // 2, n % 2)
                if n == NT:
                    dve.wait_ge(ld_w0, 16 * 9)
                if n >= NT:
                    dve.wait_ge(pq_mm, n + 1)
                    w.tensor_tensor(PQ[:, 1, n - NT, :], PS[0:P, 7, :], b1row[:, :], ALU.add).then_inc(q_ev, 1)
            with dve.Fori(PQ_FROM + NT, ET // 2) as i:
                for u in range(2):
                    count_onehots(i, u)
            dve.wait_ge(a_done, 1)
            for k in range(NT - 1):
                w.tensor_copy(AT[:, k, 0:500], PS[0:P, k, 0:500]).then_inc(at_dve, 1)
            dve.wait_ge(c_ident, 2)
            dve.wait_ge(at_act, NT)
            dve.wait_ge(at_dve, NT - 1)
            for k in range(NT):
                w.tensor_tensor(AT[:, k, k * P:(k + 1) * P], AT[:, k, k * P:(k + 1) * P], ident[0:P, 0:P], ALU.add).then_inc(at_ready, 1)
            dve.wait_ge(ld_small, 16 * N_SMALL)

            dve.sem_inc(l0_free, 4)
            dve.sem_inc(l0_pre, 2)
            dve.sem_inc(l0_seg, U)

            def pre(i, u):
                n = U * i + u
                dve.wait_ge(l0_seg, n + 1)
                w.tensor_scalar(OH[:, u, :], iota[0:P, :], dstf[:, bass.ds(n, 1)], None, ALU.is_equal)
                dve.wait_ge(gp_ld[u], 32 * i + 32)
                w.tensor_tensor(tsum[:, u, :], gP[:, u, :], gQ[:, u, :], ALU.add).then_inc(l0_free, 1)
                dve.wait_ge(l0_e, n + 1)
                dve.wait_ge(l0_free, n + U + 1)
                w.tensor_tensor(tsum[:, u, :], tsum[:, u, :], PS[0:P, 5 + u % 2, :], ALU.add).then_inc(l0_pre, 1)

            def low(i, u):
                dve.wait_ge(l0_hi, U * i + u + 1)
                w.scalar_tensor_tensor(lo[:, u, :], tsum[:, u, :], 0.0, hi[:, u, :].bitcast(F32), ALU.max, ALU.subtract)\
                    .then_inc(l0_lo, 1)

            dve.wait_ge(pq_st, 32)
            dve.wait_ge(w1c_hi, 1)
            w.tensor_tensor(W1cL, W1c[0:ED, :], W1cH[0:ED, :].bitcast(F32), ALU.subtract).then_inc(w1c_lo, 1)

            def attr_low(i, h):
                dve.wait_ge(ea_hi, 2 * i + h + 1)
                low_half = eaS[ED:2 * ED, h, :]
                w.tensor_tensor(low_half, eaT[ED:2 * ED, h, :], low_half.bitcast(F32), ALU.subtract).then_inc(ea_lo, 1)

            attr_low(0, 0)
            attr_low(0, 1)
            pre(0, 0)
            pre(0, 1)
            with dve.Fori(0, EI - 1) as i:
                for u in range(U):
                    low(i, u)
                    pre(i + (u + 2) // U, (u + 2) % U)
                    if u % 2 == 0:
                        attr_low(i + 1, u // 2)
            for u in range(U):
                low(EI - 1, u)
                if u < 2:
                    pre(EI - 1, u + 2)
            dve.wait_ge(l0_acc, 1)
            w.memset(aggT[:, :, N:NP], 0.0).then_inc(l0_agg_dve, 1)
            for t in range(1, NT, 2):
                w.tensor_copy(agg[:, t, :], PS[0:P, t, :]).then_inc(l0_agg_dve, 1)
            dve.wait_ge(deg_mm, 1)
            w.tensor_scalar(indeg_row[:, :].rearrange("p (b n) -> p b n", b=2), PS[0:1, 4:6, 0:NH], 1.0, None, ALU.subtract)
            w.tensor_copy(deg[:, 0:NT], PS[0:P, 6, 0:NT]).then_inc(deg_v, 1)
            dve.wait_ge(deg_pow, 1)
            link(newton(deg[:, 0:NT], nw[:, 1, 0:NT], dinv[:, 0:NT]))
            w.tensor_tensor(dinv2[:, 0:NT], dinv[:, 0:NT], dinv[:, 0:NT], ALU.mult).then_inc(dinv_ready, 1)
            for t in range(NT):
                ins = w.tensor_tensor(x[:, t, :], x[:, t, :], xn[:, t, :], ALU.add)
            link(ins)
            for t in range(NT):
                ins = w.tensor_tensor(x[:, t, :], x[:, t, :], bias_rows[:, 0, :], ALU.add)
            link(ins)
            for t in range(NT):
                dve.wait_ge(l0_o, t + 1)
                w.tensor_tensor(x[:, t, :], x[:, t, :], PS[0:P, 4 + t % 2, 0:D], ALU.add).then_inc(x_new[1], 1)
                if t:
                    dve.wait_ge(x_new[1], t)
                    moments(t - 1)

            def top2(k):
                for t in range(NT):
                    ins = w.max(top[:, t, :], lg[:, t, :])
                link(ins)
                for t in range(NT):
                    ins = w.max_index(topi[:, t, :], top[:, t, :], lg[:, t, :])
                link(ins)
                link(w.tensor_copy(topf[:, :, :], topi[:, :, :]))

            def onehot(j, dst_ap):
                for t in range(NT):
                    ins = w.tensor_scalar(dst_ap[:, t, :], iota8, topf[:, t, j:j + 1], None, ALU.is_equal)
                link(ins)

            def logits(k, biases):
                dve.wait_ge(*ff[k]["lgmm"](1))
                n_e = FFNS[k]["experts"]
                src_ap = PS[0:P, 5, 0:NT * 8].rearrange("p (t e) -> p t e", t=NT)[:, :, 0:n_e]
                for j in biases:
                    b = bg[:, j, 0:n_e].unsqueeze(1).to_broadcast([P, NT, n_e])
                    link(w.tensor_tensor(lg[:, :, 0:n_e], src_ap, b, ALU.add))
                    src_ap = lg[:, :, 0:n_e]

            def bc8(ap, n=8):
                return ap.unsqueeze(2).to_broadcast([P, NT, n])

            def residual(k):
                f = ff[k]
                for t in range(NT):
                    dve.wait_ge(*f["gT"](t + 1))
                    w.tensor_copy(gateT[0:8, t * P:(t + 1) * P], PS[0:8, 6 + t % 2, 0:P]).then_inc(f["gTs"].sem, 1)
                for t in range(NT):
                    dve.wait_ge(*f["b2mm"](t + 1))
                    w.tensor_tensor(x[:, t, :], x[:, t, :], PS[0:P, 6 + t % 2, 0:D], ALU.add)\
                        .then_inc(x_new[FFNS[k]["layer"] + 1], 1)

            def combine(k):
                f, xs = ff[k], x_new[FFNS[k]["layer"] + 1]

                def pair(i):
                    for u in range(2):
                        gate_col = slice(u, u + 1) if isinstance(i, int) else bass.ds(2 * i + u, 1)
                        for t in range(NT):
                            n = NT * (2 * i + u) + t
                            dve.wait_ge(*f["ymm"](n + 1))
                            dve.wait_ge(xs, n + 1)
                            w.scalar_tensor_tensor(x[:, t, :], PS[0:P, y_bank(k, u, t), 0:D], gate[:, t, gate_col],
                                                   x[:, t, :], ALU.mult, ALU.add).then_inc(xs, 1)

                pair(0)
                with dve.Fori(1, PAIRS[k]) as i:
                    if k != "f2":
                        for c in range(FQ):
                            dve.wait_ge(*f["h"](FQ * i + c + 1))
                            w.tensor_tensor(hL[:, c, :], hfull[:, c % 2, :], hH[:, c, :].bitcast(F32), ALU.subtract).then_inc(f["hld"].sem, 1)
                    pair(i)

            def ffn_x(layer):
                n_e = {2: 8, 4: 8, 6: 8, 8: 6}[layer]
                return lambda t: dve.wait_ge(x_new[layer], NT * n_e + t + 1)

            dve.wait_ge(x_new[1], NT)
            layernorm(1, None, "f0")
            logits("f0", (0, 1))
            top2("f0")
            w.tensor_tensor(gt[:, 1, :, 0], top[:, :, 1], top[:, :, 0], ALU.subtract).then_inc(ff["f0"]["lgv"].sem, 1)
            for u in range(2):
                last_low("f0", u)
            onehot(0, gt[:, 2])
            onehot(1, gt[:, 3])
            dve.wait_ge(*ff["f0"]["gexp"](1))
            link(w.tensor_scalar(gt[:, 0, :, 1], gt[:, 0, :, 0], 1.0, None, ALU.add))
            link(w.reciprocal(gt[:, 0, :, 2], gt[:, 0, :, 1]))
            link(w.tensor_tensor(gt[:, 0, :, 3], gt[:, 0, :, 0], gt[:, 0, :, 2], ALU.mult))
            link(w.tensor_tensor(gt[:, 1, :, :], gt[:, 2, :, :], bc8(gt[:, 0, :, 2]), ALU.mult))
            link(w.tensor_tensor(gt[:, 2, :, :], gt[:, 3, :, :], bc8(gt[:, 0, :, 3]), ALU.mult))
            w.tensor_tensor(gate[:, :, :], gt[:, 1, :, :], gt[:, 2, :, :], ALU.add).then_inc(ff["f0"]["gate"].sem, 1)
            residual("f0")
            combine("f0")

            layernorm(2, ffn_x(2))
            c = gc["c1"]
            for t in range(NT):
                dve.wait_ge(c["ymm"], t + 1)
                link(w.scalar_tensor_tensor(ctmp[:, t, 0:GH], PS[0:P, 2 + t % 2, 0:GH], dinv[:, t:t + 1], gcnb[:, :], ALU.mult, ALU.add))
                w.tensor_scalar(h1c[:, t, 0:GH], ctmp[:, t, 0:GH], 0.0, dinv[:, t:t + 1], ALU.max, ALU.mult).then_inc(c["h1"], 1)
            for u in range(2):
                last_low("f1", u)
            for t in range(NT):
                dve.wait_ge(c["omm"], t + 1)
                link(w.scalar_tensor_tensor(ctmp[:, t, :], PS[0:P, t % 2, 0:D], dinv[:, t:t + 1], bias_rows[:, 1, :], ALU.mult, ALU.add))
                w.scalar_tensor_tensor(x[:, t, :], ctmp[:, t, :], 0.0, x[:, t, :], ALU.max, ALU.add).then_inc(x_new[3], 1)
                if t:
                    dve.wait_ge(x_new[3], t)
                    moments(t - 1)

            dve.wait_ge(x_new[3], NT)
            layernorm(3, None, "f1")
            logits("f1", (2,))
            top2("f1")
            onehot(0, gt[:, 2])
            onehot(1, gt[:, 3])
            w.tensor_tensor(gate[:, :, :], gt[:, 2, :, :], gt[:, 3, :, :], ALU.add).then_inc(ff["f1"]["gate"].sem, 1)
            residual("f1")
            combine("f1")

            layernorm(4, ffn_x(4))

            def gat(l):
                q = ga[l]
                def targets(i, k, tiles):
                    p = 4 * i + k
                    if 0 in tiles:
                        dve.wait_ge(*q[f"dr{k}"](16 * i + 16))
                        if not isinstance(i, int) or p >= 2:
                            dve.wait_ge(*q["xg"](p - 1))
                    for t in tiles:
                        ins = w.tensor_scalar(OHT[:, k % 2, t, :], dstrow[:, k, :], nodeid[:, t:t + 1], None, ALU.is_equal)
                    if NT - 1 in tiles:
                        ins.then_inc(q["oht"].sem, 1)

                targets(0, 0, range(NT))
                targets(0, 1, range(NT))
                for t in range(NT):
                    dve.wait_ge(*q["xev"](t + 1))
                    w.tensor_copy(xl1[:, t, :, 0:HD], XLR[:, 0, t, :].rearrange("p (h c) -> p h c", h=HEADS))
                for t in range(NT):
                    dve.wait_ge(*q["xev"](NT + t + 1))
                    w.tensor_tensor(xrS[:, 1, t, :], XLR[:, 1, t, :], xrS[:, 0, t, :].bitcast(F32), ALU.subtract).then_inc(q["xrs"].sem, 1)
                    ins = w.tensor_tensor(sf[:, t, :], XLR[:, 0, t, :], XLR[:, 1, t, :], ALU.add)
                link(ins)
                link(w.scalar_tensor_tensor(sf2[:, :, :], sf[:, :, :], 0.2, sf[:, :, :], ALU.mult, ALU.max))
                link(w.tensor_tensor(sf[:, :, :], sf2[:, :, :], att[:, l, :].unsqueeze(1).to_broadcast([P, NT, D]), ALU.mult))
                w.tensor_reduce(s4self[:, :, :], sf[:, :, :].rearrange("p t (h c) -> p t h c", h=HEADS), AX.X, ALU.add).then_inc(q["self"].sem, 1)
                for t in range(NT):
                    w.tensor_tensor(xlS[:, 1, t, :], XLR[:, 0, t, :], xlS[:, 0, t, :].bitcast(F32), ALU.subtract).then_inc(q["xls"].sem, 1)
                att_b = att[:, l, :].unsqueeze(1).to_broadcast([P, 2, D])

                def edges(i, k, last=False):
                    p = 4 * i + k
                    ahead = (i + (k + 2) // 4, (k + 2) % 4)
                    a_, b_ = ag[:, k, :, :], bt[:, k % 2, :, :]
                    lr = 11 * i + 3 * k
                    if k not in GATHERED:
                        dve.wait_ge(*q["cp"](i + 1))
                    if k in GATHERED:
                        dve.wait_ge(*q["xg"](p + 1))
                        dve.wait_ge(*q[f"gl{k}"](32 * i + 32))
                        w.tensor_tensor(a_, a_, PS[0:P, 2 + k, :].rearrange("p (j d) -> p j d", j=2), ALU.add).then_inc(q["lr"].sem, 1)
                        lr = lr + 1
                    if not last:
                        targets(*ahead, (0, 1))
                    if k in GATHERED:
                        dve.wait_ge(*q["lr"](lr))
                    w.scalar_tensor_tensor(b_, a_, 0.2, a_, ALU.mult, ALU.max).then_inc(q["lr"].sem, 1)
                    if not last:
                        targets(*ahead, (2,))
                    dve.wait_ge(*q["lr"](lr + 1))
                    w.tensor_tensor(a_, b_, att_b, ALU.mult).then_inc(q["lr"].sem, 1)
                    if not last:
                        targets(*ahead, (3, 4))
                    dve.wait_ge(*q["lr"](lr + 2))
                    if not isinstance(i, int) or i:
                        for j in range(2):
                            dve.wait_ge(*q[f"scat{j}"](16 * (p - 3)))
                    w.tensor_reduce(s4[:, k, :, :], a_.rearrange("p j (h c) -> p j h c", h=HEADS), AX.X, ALU.add)\
                        .then_inc(q["s4"].sem, 1)

                for k in range(4):
                    edges(0, k)
                with dve.Fori(1, ET // 8 - 1) as i:
                    for k in range(4):
                        edges(i, k)
                for k in range(4):
                    edges(ET // 8 - 1, k, last=k >= 2)
                def tmax(t):
                    dve.wait_ge(*q[f"sd{t % 2}"](32 * (t // 2 + 1)))
                    if t >= 2:
                        dve.wait_ge(*q["tr"](NT * (t - 1)))
                    w.tensor_tensor(ex[t % 2].rearrange("p h s -> p s h"), Sd[:, t % 2, :, 0, :], Sd[:, t % 2, :, 1, :], ALU.max)\
                        .then_inc(q["mrg"].sem, 1)
                    dve.wait_ge(*q["mrg"](t + 1))
                    w.tensor_reduce(nmax[:, t, :], ex[t % 2], AX.X, ALU.max, negate=True).then_inc(q["max"].sem, 1)

                def finish(t):
                    dve.wait_ge(*q["omm"](t + 1))
                    po = PS[0:P, OUT_BANK[t], 0:HEADS * (HD + 1)].rearrange("p (h c) -> p h c", h=HEADS)
                    link(w.tensor_scalar(rden[:, t, :], po[:, :, HD], 1e-16, None, ALU.add))
                    link(w.reciprocal(rden[:, t, :], rden[:, t, :]))
                    link(w.tensor_tensor(v[:, t, :].rearrange("p (h c) -> p h c", h=HEADS), po[:, :, 0:HD],
                                         rden[:, t, :].unsqueeze(2).to_broadcast([P, HEADS, HD]), ALU.mult))
                    link(w.tensor_tensor(v[:, t, :], v[:, t, :], bias_rows[:, 2 + l, :], ALU.add))
                    w.tensor_scalar(v2[:, t, :], v[:, t, :], 0.0, None, ALU.min).then_inc(q["min"].sem, 1)

                def elu(t):
                    dve.wait_ge(*q["emin"](t + 1))
                    link(w.scalar_tensor_tensor(v[:, t, :], v[:, t, :], 0.0, v2[:, t, :], ALU.max, ALU.add))
                    if l == 0:
                        w.tensor_scalar(xn[:, t, :], v[:, t, :], -1.0, None, ALU.add).then_inc(q["h"].sem, 1)
                    else:
                        w.scalar_tensor_tensor(x[:, t, :], v[:, t, :], -1.0, x[:, t, :], ALU.add, ALU.add).then_inc(x_new[5], 1)
                        if t:
                            dve.wait_ge(x_new[5], t)
                            moments(t - 1)

                tmax(0)
                tmax(1)
                for t in range(NT):
                    for k in range(NT):
                        dve.wait_ge(*q["tr"](NT * t + k + 1))
                        if k == 0 and t:
                            dve.wait_ge(*q["omm"](t))
                        w.tensor_tensor(PT[:, k, :, :], PS[0:P, TR_BANK[(NT * t + k) % 4], 0:HEADS * P].rearrange("p (h n) -> p h n", h=HEADS),
                                        AT[:, k, t * P:(t + 1) * P].unsqueeze(1).to_broadcast([P, HEADS, P]), ALU.mult)\
                            .then_inc(q["pt"].sem, 1)
                    if t + 2 < NT:
                        tmax(t + 2)
                    if t:
                        finish(t - 1)
                    if t >= 2:
                        elu(t - 2)
                finish(NT - 1)
                elu(NT - 2)
                elu(NT - 1)
            gat(0)
            gat(1)

            def softmax8(k, n_e):
                for t in range(NT):
                    ins = w.tensor_reduce(gt[:, 2, t, 0:1], lg[:, t, 0:n_e], AX.X, ALU.max)
                link(ins)
                w.tensor_tensor(gt[:, 0, :, 0:n_e], lg[:, :, 0:n_e], bc8(gt[:, 2, :, 0], n_e), ALU.subtract).then_inc(ff[k]["lgv"].sem, 1)
                dve.wait_ge(*ff[k]["gexp"](1))
                link(w.tensor_reduce(gt[:, 2, :, 1], gt[:, 1, :, 0:n_e], AX.X, ALU.add))
                link(w.reciprocal(gt[:, 2, :, 2], gt[:, 2, :, 1]))
                link(w.tensor_tensor(lg[:, :, 0:n_e], gt[:, 1, :, 0:n_e], bc8(gt[:, 2, :, 2], n_e), ALU.mult))

            dve.wait_ge(x_new[5], NT)
            layernorm(5, None, "f2")
            last_low("f2", 0)
            dve.wait_ge(*ff["f2"]["wgh"](1))
            w.tensor_tensor(wg2[:, 1, :], wg["f2"][:, :, :].rearrange("p c e -> p (c e)"), wg2[:, 0, :].bitcast(F32), ALU.subtract)\
                .then_inc(ff["f2"]["wgl"].sem, 1)
            last_low("f2", 1)
            logits("f2", (3,))
            softmax8("f2", 8)
            top2("f2")
            onehot(0, gt[:, 2])
            w.tensor_tensor(gate[:, :, :], gt[:, 2, :, :], bc8(top[:, :, 0]), ALU.mult).then_inc(ff["f2"]["gate"].sem, 1)
            residual("f2")
            combine("f2")

            layernorm(6, ffn_x(6))
            c = gc["c3"]
            for t in range(NT):
                dve.wait_ge(ln_xn, NT * 6 + t + 1)
                w.tensor_scalar(hs[:, t, :], xn[:, t, :], dinv[:, t:t + 1], None, ALU.mult).then_inc(c["hs"], 1)
            for u in range(2):
                last_low("f3", u)
            for t in range(NT):
                dve.wait_ge(c["omm"], t + 1)
                w.scalar_tensor_tensor(x[:, t, :], PS[0:P, 4 + t % 2, 0:D], dinv[:, t:t + 1], x[:, t, :], ALU.mult, ALU.add)\
                    .then_inc(x_new[7], 1)
                if t:
                    dve.wait_ge(x_new[7], t)
                    moments(t - 1)

            dve.wait_ge(x_new[7], NT)
            layernorm(7, None, "f3")
            link(w.memset(lg[:, :, 6:8], -1.0))
            logits("f3", (4,))
            softmax8("f3", 6)
            top2("f3")
            w.tensor_tensor(gt[:, 2, :, 0], top[:, :, 1], top[:, :, 0], ALU.subtract).then_inc(ff["f3"]["lgv"].sem, 1)
            dve.wait_ge(*ff["f3"]["gexp"](2))
            link(w.tensor_scalar(gt[:, 0, :, 1], gt[:, 0, :, 0], 1.0, None, ALU.add))
            link(w.reciprocal(gt[:, 0, :, 2], gt[:, 0, :, 1]))
            link(w.tensor_tensor(gt[:, 0, :, 3], gt[:, 0, :, 0], gt[:, 0, :, 2], ALU.mult))
            onehot(0, gt[:, 2])
            onehot(1, gt[:, 3])
            link(w.tensor_tensor(gt[:, 1, :, :], gt[:, 2, :, :], bc8(gt[:, 0, :, 2]), ALU.mult))
            link(w.tensor_tensor(gt[:, 2, :, :], gt[:, 3, :, :], bc8(gt[:, 0, :, 3]), ALU.mult))
            w.tensor_tensor(gate[:, :, :], gt[:, 1, :, :], gt[:, 2, :, :], ALU.add).then_inc(ff["f3"]["gate"].sem, 1)
            residual("f3")
            combine("f3")

        @block.tensor
        def _(pe):
            m_ = nc.tensor

            def mm(*args, **kw):
                return m_.matmul(*args, skip_group_check=True, **kw)

            def layernorm_transposes(i, logits=None):
                for t in range(NT):
                    pe.wait_ge(ln_xn, NT * i + t + 1)
                    if t >= 2:
                        pe.wait_ge(ln_xnT, NT * i + t - 1)
                    for c in range(DC):
                        ins = m_.transpose(PS[:, 6 + t % 2, c * P:(c + 1) * P], xn[:, t, c * 128:(c + 1) * 128], ident[0:P, 0:P])
                    ins.then_inc(ln_tr, 1)
                    if logits and t >= 2:
                        pe.wait_ge(ln_xnT, NT * i + t - 1)
                        logits(t - 2)
                if logits:
                    for t in (NT - 2, NT - 1):
                        pe.wait_ge(ln_xnT, NT * i + t + 1)
                        logits(t)

            pe.wait_ge(c_ident, 2)
            layernorm_transposes(0)
            pe.wait_ge(c_zero, 1)
            pe.wait_ge(ln_xnT, NT)
            for b in range(7):
                mm(PS[0:P, b, :], zrow[:, 0:P], zrow[:, :], start=True, stop=False)

            def count(i, u):
                pe.wait_ge(a_oh, 2 * i + u + 1)
                for k in range(NT):
                    wt = ohS[:, 2 * u, k * P:(k + 1) * P]
                    mm(PS[0:P, k, 0:500], wt, ohS[:, 2 * u + 1, 0:500], start=False, stop=False)
                    ins = mm(PS[0:P, 5 + k // 4, 128 * (k % 4):128 * (k % 4) + 128], wt, ohS[:, 2 * u + 1, 500:NP],
                             start=False, stop=False)
                ins.then_inc(a_mm, 1)

            with pe.Fori(0, PQ_FROM) as i:
                for u in range(2):
                    count(i, u)
            pe.wait_ge(ld_w0, 16 * 9)
            for n in range(2 * NT):
                if n:
                    pe.wait_ge(p_ev if n <= NT else q_ev, n if n <= NT else n - NT)
                for c in range(DC):
                    ins = mm(PS[0:P, 7, :], xnT[:, c, (n % NT) * P:(n % NT + 1) * P], (W1a, W1b)[n // NT][:, c, :],
                             start=(c == 0), stop=(c == DC - 1))
                ins.then_inc(pq_mm, 1)
                count(PQ_FROM + n // 2, n % 2)
            with pe.Fori(PQ_FROM + NT, ET // 2) as i:
                for u in range(2):
                    count(i, u)
            for b in range(7):
                ins = mm(PS[0:P, b, :], zrow[:, 0:P], zrow[:, :], start=False, stop=True)
            ins.then_inc(a_done, 1)
            pe.wait_ge(at_act, NT)
            pe.wait_ge(at_dve, NT - 1)
            for b in range(NT):
                mm(PS[0:P, b, :], zrow[:, 0:P], zrow[:, :], start=True, stop=False)

            def edge(i, u):
                if u % 2 == 0:
                    pe.wait_ge(ea_lo, 2 * i + u // 2 + 1)
                pe.wait_ge(l0_pre, U * i + u + 1)
                tile = slice((u % 2) * P, (u % 2 + 1) * P)
                mm(PS[0:P, 5 + u % 2, :], eaS[:, u // 2, tile], W1cH, start=True, stop=False)
                mm(PS[0:P, 5 + u % 2, :], eaS[0:ED, u // 2, tile], W1cL, start=False, stop=True).then_inc(l0_e, 1)

            def segments(i, u):
                pe.wait_ge(l0_lo, U * i + u + 1)
                for t in range(NT):
                    for part in (hi, lo):
                        ins = mm(PS[0:P, t, :], OH[:, u, t * P:(t + 1) * P], part[:, u, :], start=False, stop=False)
                ins.then_inc(l0_seg, 1)

            pe.wait_ge(w1c_lo, 1)
            edge(0, 0)
            edge(0, 1)
            with pe.Fori(0, EI - 1) as i:
                for u in range(U):
                    edge(i + (u + 2) // U, (u + 2) % U)
                    segments(i, u)
            for u in range(U):
                if u < 2:
                    edge(EI - 1, u + 2)
                segments(EI - 1, u)
            for b in range(NT):
                ins = mm(PS[0:P, b, :], zrow[:, 0:P], zrow[:, :], start=False, stop=True)
            ins.then_inc(l0_acc, 1)
            pe.wait_ge(l0_agg_dve, NT // 2 + 1)
            for t in range(NT):
                pe.wait_ge(l0_agg_act, t // 2 + 1)
                if t >= 2:
                    pe.wait_ge(l0_aggT, t - 1)
                for c in range(HC):
                    ins = m_.transpose(PS[:, 5 + t % 2, c * P:(c + 1) * P], agg[:, t, c * 128:(c + 1) * 128], ident[0:P, 0:P])
                ins.then_inc(l0_tr, 1)
            pe.wait_ge(l0_aggT, NT)
            pe.wait_ge(at_ready, NT)
            for t in range(NT):
                for k in range(NT):
                    mm(PS[0:P, 6, t:t + 1], AT[:, k, t * P:(t + 1) * P], ones[0:P, 0:1], start=(k == 0), stop=(k == NT - 1))
            for b in range(2):
                for k in range(NT):
                    ins = mm(PS[0:1, 4 + b, 0:NH], ones[0:P, 0:1], AT[:, k, b * NH:(b + 1) * NH], start=(k == 0), stop=(k == NT - 1))
            ins.then_inc(deg_mm, 1)
            for m in range(HC):
                if m >= 2:
                    pe.wait_ge(l0_msgT, m - 1)
                for b in range(2):
                    for c in range(HC):
                        mm(PS[:, 2 * (m % 2) + b, 0:NH], W2[:, c, m * 128:(m + 1) * 128], aggT[:, c, b * NH:(b + 1) * NH],
                           start=(c == 0), stop=False)
                    pe.wait_ge(deg_v, 1)
                    ins = mm(PS[:, 2 * (m % 2) + b, 0:NH], b2row[:, m * 128:(m + 1) * 128], indeg_row[:, b * NH:(b + 1) * NH],
                             start=False, stop=True)
                ins.then_inc(l0_m, 1)
            for m in range(HC):
                pe.wait_ge(l0_msgT, HC)
                if m >= 2:
                    pe.wait_ge(l0_gT, m - 1)
                for b in range(2):
                    for c in range(DC + HC):
                        rhs = xnT[:, c, b * NH:(b + 1) * NH] if c < DC else msgT[:, c - DC, b * NH:(b + 1) * NH]
                        ins = mm(PS[:, 2 * (m % 2) + b, 0:NH], W3[:, c, m * 128:(m + 1) * 128], rhs, start=(c == 0), stop=(c == DC + HC - 1))
                ins.then_inc(l0_g, 1)
            pe.wait_ge(l0_gT, HC)
            for t in range(NT):
                if t >= 2:
                    pe.wait_ge(x_new[1], t - 1)
                for c in range(HC):
                    ins = mm(PS[0:P, 4 + t % 2, 0:D], gT[:, c, t * P:(t + 1) * P], W4[:, c, :], start=(c == 0), stop=(c == HC - 1))
                ins.then_inc(l0_o, 1)

            def gate_logits(k, chunks, act_of, w_of, t):
                n_e = FFNS[k]["experts"]
                for c in range(chunks):
                    ins = mm(PS[0:P, 5, 8 * t:8 * t + n_e], act_of(c)[:, t * P:(t + 1) * P], w_of(c), start=(c == 0), stop=(c == chunks - 1))
                if t == NT - 1:
                    ins.then_inc(ff[k]["lgmm"].sem, 1)

            def gate_biases(k):
                f, n_e = ff[k], FFNS[k]["experts"]
                pe.wait_ge(*f["gate"](1))
                for t in range(NT):
                    if t >= 2:
                        pe.wait_ge(*f["gTs"](t - 1))
                    m_.transpose(PS[0:8, 6 + t % 2, 0:P], gate[:, t, :], ident[0:P, 0:P]).then_inc(f["gT"].sem, 1)
                for t in range(NT):
                    pe.wait_ge(*f["gTs"](NT))
                    if t >= 2:
                        pe.wait_ge(x_new[FFNS[k]["layer"] + 1], t - 1)
                    mm(PS[0:P, 6 + t % 2, 0:D], gateT[0:n_e, t * P:(t + 1) * P], ffb2[k][0:n_e, :], start=True, stop=True)\
                        .then_inc(f["b2mm"].sem, 1)

            def mm3(out_, left, right, first, last):
                (lh, ll), (rh, rl) = left, right
                mm(out_, lh, rh, start=first, stop=False)
                mm(out_, lh, rl, start=False, stop=False)
                return mm(out_, ll, rh, start=False, stop=last)

            def hidden(k, i):
                f = ff[k]
                for c in range(FQ):
                    u, layer, m = hidden_chunk(k, c)
                    if k != "f2" and layer == 0 and m == 0:
                        pe.wait_ge(*f["wlp"](wlp_n(k, i, 0, u)))
                    if layer:
                        lows = f["hlp"](2 * u + 2) if isinstance(i, int) else f["hld"](FQ * i - FQ + 2 * u + 2)
                        pe.wait_ge(*lows)
                    if not isinstance(i, int) or c >= 2:
                        pe.wait_ge(*f["h"](FQ * i + c - 1))
                    stride = {"f0": H0, "f1": H0, "f2": 1024, "f3": D}[k]
                    for b in range(2):
                        cols = slice(b * NH, (b + 1) * NH)
                        for d in range(DC):
                            at = 512 * layer + d * stride + (c if k == "f2" else m) * 128
                            w_ = 0 if k == "f2" else u
                            right = (hH[:, 2 * u + d, cols], hL[:, 2 * u + d, cols]) if layer else (xH[:, d, cols], xL[:, d, cols])
                            ins = mm3(PS[:, 2 * (c % 2) + b, 0:NH], (WH[:, w_, at:at + 128], WL[:, w_, at:at + 128]), right,
                                      d == 0, d == DC - 1)
                    ins.then_inc(f["hmm"].sem, 1)

            def outputs(k, i, u, tiles=range(NT)):
                f = ff[k]
                if isinstance(i, int):
                    pe.wait_ge(*f["hlp"](FQ))
                    pe.wait_ge(*f["wld"](u + 1))
                else:
                    if k != "f2":
                        pe.wait_ge(*f["hld"](FQ * i - FQ + output_chunks(k, u)[-1] + 1))
                    pe.wait_ge(*f["wlp"](wlp_n(k, i, 1, u)))
                deep = NT if k == "f2" else 2
                for t in tiles:
                    if not (isinstance(i, int) and NT * u + t < deep):
                        pe.wait_ge(x_new[FFNS[k]["layer"] + 1], NT * (2 * i + u) + NT + t + 1 - deep)
                    chunks = output_chunks(k, u)
                    for j, c in enumerate(chunks):
                        at = W_AT[k] + j * D
                        w_ = slot(k, u)
                        cols = slice(t * P, (t + 1) * P)
                        ins = mm3(PS[0:P, y_bank(k, u, t), 0:D], (hH[:, c, cols], hL[:, c, cols]), (WH[:, w_, at:at + D], WL[:, w_, at:at + D]),
                                  j == 0, j == len(chunks) - 1)
                    ins.then_inc(f["ymm"].sem, 1)

            def pairs(k):
                pe.wait_ge(*ff[k]["xl"](NT))
                hidden(k, 0)
                gate_biases(k)
                for u in range(2):
                    outputs(k, 0, u)
                with pe.Fori(1, PAIRS[k]) as i:
                    hidden(k, i)
                    for u in range(2):
                        outputs(k, i, u)

            def ffn(k):
                pe.wait_ge(ld_small, 16 * N_SMALL)
                layernorm_transposes(FFNS[k]["layer"], lambda t: gate_logits(k, DC, lambda c: xnT[:, c], lambda c: wg[k][:, c, :], t))
                pairs(k)

            ffn("f0")

            layernorm_transposes(2)
            c1 = gc["c1"]
            pe.wait_ge(ln_xnT, NT * 3)
            pe.wait_ge(ld_wg, 16 * 8)
            for t in range(NT):
                if t >= 2:
                    pe.wait_ge(c1["hs"], t - 1)
                for c in range(DC):
                    ins = mm(PS[0:P, t % 2, 0:GH], xnT[:, c, t * P:(t + 1) * P], C1W1[:, c, :], start=(c == 0), stop=(c == DC - 1))
                ins.then_inc(c1["hmm"], 1)
            pe.wait_ge(c1["hs"], NT)
            for t in range(NT):
                if t >= 2:
                    pe.wait_ge(c1["h1"], t - 1)
                for k in range(NT):
                    ins = mm(PS[0:P, 2 + t % 2, 0:GH], AT[:, k, t * P:(t + 1) * P], hs[:, k, 0:GH], start=(k == 0), stop=(k == NT - 1))
                ins.then_inc(c1["ymm"], 1)
            pe.wait_ge(c1["h1"], NT)
            for b in range(2):
                for k in range(NT):
                    ins = mm(PS[0:GH, 4 + b, 0:NH], h1c[:, k, 0:GH], AT[:, k, b * NH:(b + 1) * NH], start=(k == 0), stop=(k == NT - 1))
            ins.then_inc(c1["a2mm"], 1)
            pe.wait_ge(c1["a2T"], 1)
            for t in range(NT):
                if t >= 2:
                    pe.wait_ge(x_new[3], t - 1)
                mm(PS[0:P, t % 2, 0:D], cT[0:GH, 0, t * P:(t + 1) * P], C1W2, start=True, stop=True).then_inc(c1["omm"], 1)

            ffn("f1")

            layernorm_transposes(4)

            def gat(l):
                q = ga[l]
                for r in range(2):
                    for t in range(NT):
                        n = NT * r + t
                        pe.wait_ge(*((ln_xnT, NT * 4 + t + 1) if l == 0 else ga[0]["hT"](t + 1)))
                        if n >= 2:
                            pe.wait_ge(*q["xev"](n - 1))
                        for c in range(DC):
                            ins = mm(PS[0:P, n % 2, 0:D], xnT[:, c, t * P:(t + 1) * P], GW[l][r][:, c, :], start=(c == 0), stop=(c == DC - 1))
                        ins.then_inc(q["xmm"].sem, 1)
                pe.wait_ge(*q["xrs"](NT))

                def xr_step(i):
                    def rows(u, onehot, table, first, last):
                        for j in range(2):
                            for k in range(NT):
                                for part in range(2):
                                    ins = mm(PS[0:P, 2 + u, j * D:(j + 1) * D], onehot[:, k, j * P:(j + 1) * P], table[:, part, k, :],
                                             start=(first and j + k + part == 0), stop=(last and k + part == NT))
                        return ins

                    for u in range(4):
                        if not isinstance(i, int):
                            pe.wait_ge(*q["s4"](4 * i + u - 3))
                        if u not in GATHERED:
                            pe.wait_ge(*q["ohs"](i + 1))
                            pe.wait_ge(*q["xls"](NT))
                            rows(u, OHS, xlS, True, False)
                        pe.wait_ge(*q["oht"](4 * i + u + 1))
                        ins = rows(u, OHT[:, u % 2], xrS, u in GATHERED, True)
                        ins.then_inc(q["xg"].sem, 1)

                xr_step(0)
                with pe.Fori(1, ET // 8) as i:
                    xr_step(i)
                for t in range(NT):
                    pe.wait_ge(*q["exp"](HEADS * (t + 1)))
                    for k in range(NT):
                        n = NT * t + k
                        if n >= 4:
                            pe.wait_ge(*q["pt"](n - 3))
                        for h in range(HEADS):
                            ins = m_.transpose(PS[0:P, TR_BANK[n % 4], h * P:(h + 1) * P], ex[t % 2][:, h, k * P:(k + 1) * P], ident[0:P, 0:P])
                        ins.then_inc(q["tr"].sem, 1)
                    pe.wait_ge(*q["pt"](NT * (t + 1)))
                    for h in range(HEADS):
                        for k in range(NT):
                            ins = mm(PS[0:P, OUT_BANK[t], h * (HD + 1):(h + 1) * (HD + 1)], PT[:, k, h, :], xl1[:, k, h, :],
                                     start=(k == 0), stop=(k == NT - 1))
                    ins.then_inc(q["omm"].sem, 1)
                if l == 0:
                    for t in range(NT):
                        pe.wait_ge(*q["h"](t + 1))
                        if t >= 2:
                            pe.wait_ge(*q["hT"](t - 1))
                        for c in range(DC):
                            ins = m_.transpose(PS[:, 4 + t % 2, c * P:(c + 1) * P], xn[:, t, c * 128:(c + 1) * 128], ident[0:P, 0:P])
                        ins.then_inc(q["htr"].sem, 1)

            gat(0)
            gat(1)

            layernorm_transposes(5)
            f = ff["f2"]
            pe.wait_ge(*f["xl"](NT))
            pe.wait_ge(*f["wlp"](1))
            hidden("f2", 0)
            pe.wait_ge(*f["hlp"](FQ))
            pe.wait_ge(*f["wgl"](1))
            for b in range(2):
                cols = slice(b * NH, (b + 1) * NH)
                for c in range(FQ):
                    ins = mm3(PS[0:8, 4 + b, 0:NH], (wg2[:, 0, 8 * c:8 * c + 8], wg2[:, 1, 8 * c:8 * c + 8]), (hH[:, c, cols], hL[:, c, cols]),
                              c == 0, c == FQ - 1)
            ins.then_inc(f["lgT"].sem, 1)
            outputs("f2", 0, 0, range(3))
            pe.wait_ge(*f["lgTs"](1))
            for t in range(NT):
                ins = m_.transpose(PS[0:P, 5, 8 * t:8 * t + 8], gateT[:, t * P:(t + 1) * P], ident[0:8, 0:8])
            ins.then_inc(f["lgmm"].sem, 1)
            outputs("f2", 0, 0, range(3, NT))
            gate_biases("f2")
            outputs("f2", 0, 1)
            with pe.Fori(1, PAIRS["f2"]) as i:
                for u in range(2):
                    outputs("f2", i, u)

            layernorm_transposes(6)
            c3 = gc["c3"]
            for r, (src_t, ready, mm_s, ev) in enumerate(((hs, "hs", "amm", "aT"), (h1c, "h1", "a2mm", "a2T"))):
                pe.wait_ge(c3[ready], NT)
                for m in range(DC):
                    for b in range(2):
                        for k in range(NT):
                            ins = mm(PS[:, 2 * m + b, 0:NH], src_t[:, k, m * 128:(m + 1) * 128], AT[:, k, b * NH:(b + 1) * NH],
                                     start=(k == 0), stop=(k == NT - 1))
                    ins.then_inc(c3[mm_s], 1)
                pe.wait_ge(c3[ev], DC)
                for t in range(NT):
                    if t >= 2:
                        pe.wait_ge(c3["h1"] if r == 0 else x_new[7], t - 1)
                    for c in range(DC):
                        ins = mm(PS[0:P, 4 + t % 2, 0:D], cT[:, c, t * P:(t + 1) * P], C3W[r][:, c, :], start=(c == 0), stop=(c == DC - 1))
                    ins.then_inc(c3["ymm"] if r == 0 else c3["omm"], 1)

            layernorm_transposes(7)
            f = ff["f3"]
            pe.wait_ge(ln_xnT, NT * 8)
            for b in range(2):
                for c in range(DC):
                    ins = mm(PS[:, 4 + b, 0:NH], rw1[:, c, :], xnT[:, c, b * NH:(b + 1) * NH], start=(c == 0), stop=(c == DC - 1))
            ins.then_inc(f["rmm"].sem, 1)
            pe.wait_ge(*f["rh"](1))
            for t in range(NT):
                gate_logits("f3", 1, lambda c: rhT, lambda c: wg["f3"][:, :], t)
            pairs("f3")


N_SMALL = 27


def kernel(**inputs):
    import concourse.bacc as _bacc
    from concourse import mybir as _mybir
    from concourse.bass_utils import run_bass_kernel_spmd as _run

    r = {k: np.asarray(val) for k, val in inputs.items()}

    def cols(b):
        return b.reshape(-1, 128).T

    def chunks(w_):
        e, k, m = w_.shape
        return w_.reshape(e, k // 128, 128, m).transpose(0, 2, 1, 3).reshape(e, 128, -1)

    src, dst = r.pop("src"), r.pop("dst")
    r["src_dst"] = np.stack([src, dst], axis=1).reshape(ET, P, 2).transpose(1, 0, 2)
    r["dst_row"] = dst.reshape(ET // 2, 1, 2 * P)
    r["src_row"] = src.reshape(ET // 8, 4, 1, 2 * P)[:, 3]
    r["edge_attr_64"] = r["edge_attr_64"].reshape(ET // 2, 2 * P, ED).transpose(0, 2, 1)
    for k in ("L0_gnn_b1", "L0_gnn_b2", "L0_gnn_b4", "L0_ffn_bg", "L0_ffn_bias", "L1_gnn_b1", "L1_gnn_b2", "L1_ffn_bg",
              "L2_gnn_att0", "L2_gnn_b0", "L2_gnn_att1", "L2_gnn_b1", "L2_ffn_bg", "L3_ffn_router_b2"):
        r[k] = r[k].reshape(1, -1)
    for k in ("L0_gnn_b3", "L0_ffn_b1", "L1_ffn_b1", "L2_ffn_b1", "L3_ffn_router_b1"):
        r[k] = cols(r[k])
    for k in ("L0_ffn_W1", "L0_ffn_W2", "L1_ffn_W1", "L1_ffn_W2", "L2_ffn_Wd", "L3_ffn_expert_w1", "L3_ffn_expert_w2",
              "L3_ffn_expert_w3"):
        r[k] = chunks(r[k])
    r["L2_ffn_W1"] = chunks(r["L2_ffn_W1"][None])[0]
    r["L3_b12"] = cols(np.concatenate([r.pop("L3_ffn_expert_b1"), r.pop("L3_ffn_expert_b2")], axis=1))

    nc = _bacc.Bacc("TRN2", target_bir_lowering=False, num_devices=1)
    arrays, aps = {}, {}
    for name, arr in r.items():
        arr = np.ascontiguousarray(arr)
        arrays[f"in_{name}"] = arr
        aps[name] = nc.dram_tensor(f"in_{name}", arr.shape, _mybir.dt.from_np(arr.dtype), kind="ExternalInput").ap()
    out = nc.dram_tensor("out", (N, D), _mybir.dt.float32, kind="ExternalOutput").ap()
    build(nc, aps, out)
    res = _run(nc, [arrays], core_ids=[0])
    return res.results[0]["out"]
```
